# Optimizing a Trainium2 kernel written in Bass

```python
import numpy as np
import jax
import jax.numpy as jnp

def _softmax(x, axis=-1):
    return jax.nn.softmax(x, axis=axis)

def _gelu(x):
    return jax.nn.gelu(x, approximate=True)

def _silu(x):
    return jax.nn.silu(x)

def _sigmoid(x):
    return jax.nn.sigmoid(x)

def _layernorm(x, axis=-1, eps=1e-05):
    m = jnp.mean(x, axis=axis, keepdims=True)
    v = jnp.var(x, axis=axis, keepdims=True)
    return (x - m) / jnp.sqrt(v + eps)

def _scatter_add(tgt, idx, src, axis=0):
    return tgt.at[idx].add(src)

def _segment_sum(src, seg, n):
    return jax.ops.segment_sum(src, seg, n)
kernel_name = 'mk_gnn_preln_d2_gnn_r8_99d4df'

def setup_inputs(seed: int=0):
    np.random.seed(seed)
    _w = jnp.asarray

    def _rec_inputs():
        import jax
        import jax.numpy as jnp
        _gk = jax.random.key(seed)
        x = -0.0003713 + 1 * jax.random.normal(jax.random.fold_in(_gk, 1), (6250, 256), jnp.float32)
        _s = jax.random.randint(jax.random.fold_in(_gk, 2), (100000,), 0, 6250, jnp.int32)
        _d = jax.random.randint(jax.random.fold_in(_gk, 3), (100000,), 0, 6250, jnp.int32)
        _loop = jnp.arange(6250, dtype=jnp.int32)
        src = jnp.concatenate([_s, _d, _loop])
        dst = jnp.concatenate([_d, _s, _loop])
        _o = jnp.argsort(dst, stable=True)
        src = src[_o]
        dst = dst[_o]
        edge_type_8 = jax.random.randint(jax.random.fold_in(_gk, 12), (206250,), 0, 8, jnp.int32)
        return (x, src, dst, edge_type_8)
    x, src, dst, edge_type_8 = _rec_inputs()

    def _L0_gnn_setup():
        import jax, jax.numpy as jnp
        import numpy as np
        NUM_NODES = 6250
        NUM_EDGES = 100000
        IN_DIM = 256
        OUT_DIM = 256
        NUM_RELATIONS = 8
        key = jax.random.key(seed)
        k1, k2, k3, k4 = jax.random.split(key, 4)
        node_repr = jax.random.normal(k1, (NUM_NODES, IN_DIM), dtype=jnp.float32)
        edge_index = jax.random.randint(k2, (2, NUM_EDGES), 0, NUM_NODES, dtype=jnp.int64)
        edge_types = jax.random.randint(k3, (NUM_EDGES,), 0, NUM_RELATIONS, dtype=jnp.int64)
        limit = float(np.sqrt(6.0 / (IN_DIM + OUT_DIM)))
        weight = jax.random.uniform(k4, (NUM_RELATIONS, OUT_DIM, IN_DIM), dtype=jnp.float32, minval=-limit, maxval=limit)
        bias = jnp.zeros((OUT_DIM,), dtype=jnp.float32)
        return {'node_repr': node_repr, 'weight': weight, 'bias': bias, 'edge_index': edge_index, 'edge_types': edge_types}
    _L0_gnn_all = _L0_gnn_setup()
    _L0_gnn_in = {k: v for k, v in _L0_gnn_all.items() if k in ('weight', 'bias')}
    del _L0_gnn_all

    def _L1_gnn_setup():
        import jax, jax.numpy as jnp
        import numpy as np
        N_NODES = 12500
        N_EDGES = 400000
        D_IN = 256
        D_OUT = 256
        key = jax.random.key(seed)
        k1, k2, k3, k4 = jax.random.split(key, 4)
        x = jax.random.normal(k1, (N_NODES, D_IN), dtype=jnp.float32)
        edge_index = jax.random.randint(k2, (2, N_EDGES), 0, N_NODES, dtype=jnp.int64)
        limit = np.sqrt(6.0 / (D_IN + D_OUT)).astype(np.float32)
        W = jax.random.uniform(k3, (D_IN, D_OUT), dtype=jnp.float32, minval=-limit, maxval=limit)
        b = jnp.zeros((D_OUT,), dtype=jnp.float32)
        return {'x': x, 'edge_index': edge_index, 'W': W, 'b': b}
    _L1_gnn_all = _L1_gnn_setup()
    _L1_gnn_in = {k: v for k, v in _L1_gnn_all.items() if k in ('W', 'b')}
    del _L1_gnn_all
    return {'x': x, 'src': src, 'dst': dst, 'edge_type_8': edge_type_8, 'L0_gnn_weight': _L0_gnn_in['weight'], 'L0_gnn_bias': _L0_gnn_in['bias'], 'L1_gnn_W': _L1_gnn_in['W'], 'L1_gnn_b': _L1_gnn_in['b']}

def reference(x, src, dst, edge_type_8, L0_gnn_weight, L0_gnn_bias, L1_gnn_W, L1_gnn_b):
    import jax
    import jax.numpy as jnp

    def _L0_gnn_ref(node_repr, weight, bias, edge_index, edge_types):
        import jax, jax.numpy as jnp
        import numpy as np
        NUM_NODES = 6250
        NUM_EDGES = 100000
        IN_DIM = 256
        OUT_DIM = 256
        NUM_RELATIONS = 8
        h_all = jnp.einsum('ni,roi->rno', node_repr, weight)
        src, dst = (edge_index[0], edge_index[1])
        msgs = h_all[edge_types, src]
        messages = jax.ops.segment_sum(msgs, dst, num_segments=node_repr.shape[0])
        return messages + bias

    def _L1_gnn_ref(x, edge_index, W, b):
        import jax, jax.numpy as jnp
        import numpy as np
        N_NODES = 12500
        N_EDGES = 400000
        D_IN = 256
        D_OUT = 256
        N = x.shape[0]
        h = x @ W
        loop = jnp.arange(N, dtype=edge_index.dtype)
        src = jnp.concatenate([edge_index[0], loop])
        dst = jnp.concatenate([edge_index[1], loop])
        deg = jax.ops.segment_sum(jnp.ones(dst.shape, dtype=h.dtype), dst, num_segments=N)
        dinv = jnp.where(deg > 0, jax.lax.rsqrt(deg), 0.0)
        norm = dinv[src] * dinv[dst]
        out = jax.ops.segment_sum(norm[:, None] * h[src], dst, num_segments=N) + b
        return jax.nn.leaky_relu(out, negative_slope=0.2)
    edge_index = jnp.stack([src, dst])
    h = jnp.maximum(_layernorm(x, axis=-1), 0.0)
    x = x + _L0_gnn_ref(h, L0_gnn_weight, L0_gnn_bias, edge_index, edge_type_8)
    h = jnp.maximum(_layernorm(x, axis=-1), 0.0)
    x = x + _L1_gnn_ref(h, edge_index, L1_gnn_W, L1_gnn_b)
    return x

_drawn_inputs = setup_inputs


def setup_inputs(seed=0):
    import zlib

    import numpy as np

    out = dict(_drawn_inputs(seed))
    spreads = {'L0_gnn_bias': (0.0, 0.488), 'L1_gnn_b': (0.0, 0.637)}
    factors = {}
    for name, (base, spread) in spreads.items():
        noise = np.random.default_rng([zlib.crc32(name.encode()), seed]).standard_normal(out[name].shape)
        drawn = base * np.exp(spread * noise) if base else spread * noise
        out[name] = jnp.asarray(drawn.astype(out[name].dtype))
    for name, factor in factors.items():
        out[name] = (out[name] * factor).astype(out[name].dtype)
    return out
```

```python
import concourse.bass as bass
from concourse import mybir
from contextlib import ExitStack

P = 128
WIN = 8
HALF = 64
GRP = 11
NBANK = 6
PAD_DST = 60000.0


class Dims:

    def __init__(self, n, e, d, rel):
        self.n, self.e, self.d, self.rel = n, e, d, rel
        self.nb = d // P
        self.cps = 3 * GRP
        self.chunks = -(-e // P)
        self.segs = -(-self.chunks // self.cps)
        self.tiles = -(-(n + HALF) // P)
        self.kt = -(-(self.segs + 1) * self.cps // P)
        self.ngrp = self.segs * 3
        self.last_rows = n - (P * (self.tiles - 1) - HALF)


def wait(eng, sem, value):
    if isinstance(value, int) and value <= 0:
        return
    eng.wait_ge(sem, value)


def wait_alone(eng, sem, value, mark):
    eng.wait_ge(sem, value)
    eng.sem_inc(mark, 1)


def program(nc, x, src, dst, etype, w0, b0, w1, b1, out):
    f32, bf16, i32 = mybir.dt.float32, mybir.dt.bfloat16, mybir.dt.int32
    ALU, ACT, AX = mybir.AluOpType, mybir.ActivationFunctionType, mybir.AxisListType
    D = Dims(x.shape[0], src.shape[0], x.shape[1], w0.shape[0])
    N, E, DF, R, NB, KT, T = D.n, D.e, D.d, D.rel, D.nb, D.kt, D.tiles
    DF3 = 3 * DF
    LIM = 2 * P
    AW = LIM + WIN

    table0 = nc.dram_tensor("table0", (T * P, DF3), bf16).ap()
    table1 = nc.dram_tensor("table1", (T * P, DF3), bf16).ap()
    offs_d = nc.dram_tensor("offs_d", (KT, P), i32).ap()

    whole = ExitStack()
    with whole:
        def sb(name, shape, dt, ctx=whole):
            return ctx.enter_context(nc.sbuf_tensor(name, shape, dt))

        def sem(name, ctx=whole):
            return ctx.enter_context(nc.semaphore(name))

        ident = sb("ident", [P, P], f32)
        identb = sb("identb", [P, P], bf16)
        ones = sb("ones", [P, P], bf16)
        onef = sb("onef", [1, P], f32)
        iota = sb("iota", [P, R * WIN], bf16)
        eps = sb("eps", [P, 1], f32)
        bias0 = sb("bias0", [1, DF], f32)
        bias1 = sb("bias1", [P, DF], f32)
        xres = sb("xres", [P, T, DF], f32)
        w0t = sb("w0t", [P, R, NB, DF], f32)
        w1s = sb("w1s", [P, NB, DF], f32)
        idxT = sb("idxT", [P, KT * P], i32)
        keyT = [sb("key0T", [P, KT * P], bf16), sb("key1T", [P, KT * P], bf16)]
        n_inside = sb("n_inside", [1, 1], i32)
        offr = sb("offr", [1, D.ngrp, 12], i32)
        dinv = sb("dinv", [P, T], f32)

        ps_slot = whole.enter_context(nc.psum_tensor("ps_slot", [P, 6, 512], f32))
        ps_proj = whole.enter_context(nc.psum_tensor("ps_proj", [P, 512], f32))
        ps_aux = whole.enter_context(nc.psum_tensor("ps_aux", [P, 512], f32))

        with ExitStack() as pro:
            names = ("ld_e", "ld_x", "ld_w", "ld_c", "const", "memx", "edge", "etp", "ecp", "epse", "offw",
                     "offrd", "wtp", "wcp", "stat", "agg", "sd", "rstd", "nbias", "h32", "hi", "r1", "mid",
                     "lo", "padm", "rel", "cnst0", "inw", "cntp", "cnt")
            S = {k: sem("p_" + k) for k in names}
            NH = 4
            XL = [(a, min(a + 6, T)) for a in range(0, T, 6)]
            s_t0 = [sem(f"p_t0_{i}") for i in range(NH)]
            s_x = [sem(f"p_x_{i}") for i in range(len(XL))]
            er = [sb(f"er{i}", [P, KT, P], i32, pro) for i in range(3)]
            ef = [sb(f"ef{i}", [P, KT, P], f32, pro) for i in range(3)]
            inw = sb("inw", [P, KT, P], f32, pro)
            cnt_in = sb("cnt_in", [P, 1], f32, pro)
            onec = sb("onec", [P, 1], f32, pro)
            chunk_id = sb("chunk_id", [P, KT], i32, pro)
            seg_i = sb("seg_i", [P, KT], i32, pro)
            small = sb("small", [P, 6, KT], f32, pro)
            relT = sb("relT", [KT, P], i32, pro)
            wld = sb("wld", [P, R, NB, DF], f32, pro)
            st6 = sb("st6", [P, T, 6], f32, pro)
            mv = sb("mv", [P, T, 2], f32, pro)
            rs = sb("rs", [P, T], f32, pro)
            nb = sb("nb", [P, T], f32, pro)
            h32 = sb("h32", [P, NH, DF], f32, pro)
            r1 = sb("r1", [P, NH, DF], f32, pro)
            hs = sb("hs", [P, NH, DF3], bf16, pro)

            full = E // (P * P)
            rest_rows = (E - full * P * P) // P
            rest = E - full * P * P - rest_rows * P
            assert full == KT - 1
            n_edma = 2 + (1 if rest else 0)
            FULLT = (N - HALF) // P

            block = pro.enter_context(nc.Block())

            @block.sync
            def _(eng):
                wait(eng, S["padm"], 3)
                for a, r in zip((dst, src, etype), er):
                    eng.dma_start(r[:, 0:full, :], a[0:full * P * P].rearrange("(k p j) -> p k j", p=P, j=P)).then_inc(S["ld_e"], 16)
                    o = full * P * P
                    eng.dma_start(r[0:rest_rows, full, :], a[o:o + rest_rows * P].rearrange("(p j) -> p j", j=P)).then_inc(S["ld_e"], 16)
                    if rest:
                        o += rest_rows * P
                        eng.dma_start(r[rest_rows:rest_rows + 1, full, 0:rest], a[o:o + rest].rearrange("(p j) -> p j", p=1)).then_inc(S["ld_e"], 16)
                wait(eng, S["rel"], 1)
                eng.dma_start(offs_d, relT[:, :]).then_inc(S["offw"], 16)
                wait(eng, S["offw"], 16)
                flat = offs_d.rearrange("(o k) p -> o (k p)", o=1)[:, 0:D.ngrp * GRP].rearrange("o (g j) -> o g j", j=GRP)
                eng.dma_start(offr[:, :, 0:GRP], flat).then_inc(S["offrd"], 16)
                wait(eng, S["offrd"], 16)

            @block.scalar
            def _(eng):
                wait(eng, S["memx"], 2)
                eng.dma_start(xres[HALF:P, 0, :], x[0:HALF, :]).then_inc(s_x[0], 16)
                for li, (a, b) in enumerate(XL):
                    lo_t, hi_t = max(a, 1), min(b, FULLT + 1)
                    if hi_t > lo_t:
                        eng.dma_start(xres[:, lo_t:hi_t, :], x[lo_t * P - HALF:hi_t * P - HALF, :].rearrange("(t p) d -> p t d", p=P)).then_inc(s_x[li], 16)
                    if b == T:
                        eng.dma_start(xres[0:D.last_rows, T - 1, :], x[N - D.last_rows:N, :]).then_inc(s_x[li], 16)
                eng.dma_start(wld[:, :, :, :], w0.rearrange("r (b p) i -> p r b i", p=P)).then_inc(S["ld_w"], 16)
                eng.dma_start(w1s[:, :, :], w1.rearrange("(b p) o -> p b o", p=P)).then_inc(S["ld_c"], 16)
                eng.dma_start(bias0[:, :], b0.rearrange("(o d) -> o d", o=1)).then_inc(S["ld_c"], 16)
                eng.dma_start(bias1[:, :], b1.rearrange("(o d) -> o d", o=1).to_broadcast([P, DF])).then_inc(S["ld_c"], 16)
                wait(eng, S["const"], 7)
                for li, (a, b) in enumerate(XL):
                    wait(eng, S["agg"], li + 1)
                    eng.activation(rs[:, a:b], mv[:, a:b, 1], ACT.Sqrt, bias=eps[:, :]).then_inc(S["sd"], 1)
                for t in range(T):
                    li = t // 6
                    k = t % NH
                    wait(eng, S["nbias"], li + 1)
                    wait(eng, S["lo"], t - NH + 1)
                    eng.activation(h32[:, k, :], xres[:, t, :], ACT.Relu, scale=rs[:, t:t + 1], bias=nb[:, t:t + 1]).then_inc(S["h32"], 1)
                    if t >= NH:
                        wait(eng, s_t0[k], 16 * (t // NH))
                    wait(eng, S["h32"], t + 1)
                    eng.activation(hs[:, k, 0:DF], h32[:, k, :], ACT.Copy).then_inc(S["hi"], 1)
                    wait(eng, S["r1"], t + 1)
                    eng.activation(hs[:, k, DF:2 * DF], r1[:, k, :], ACT.Copy).then_inc(S["mid"], 1)
                wait(eng, S["ld_c"], 48)

            @block.gpsimd
            def _(eng):
                eng.memset(er[0][:, full, :], int(PAD_DST)).then_inc(S["padm"], 1)
                eng.memset(er[1][:, full, :], 0).then_inc(S["padm"], 1)
                eng.memset(er[2][:, full, :], 0).then_inc(S["padm"], 1)
                eng.memset(xres[:, 0, :], 0.0).then_inc(S["memx"], 1)
                eng.memset(xres[:, T - 1, :], 0.0).then_inc(S["memx"], 1)
                eng.iota(chunk_id[:, :], [[P, KT]], base=0, channel_multiplier=1).then_inc(S["const"], 1)
                eng.memset(ident[:, :], 0.0).then_inc(S["cnst0"], 1)
                eng.memset(identb[:, :], 0.0).then_inc(S["cnst0"], 1)
                wait(eng, S["cnst0"], 2)
                for m in (ident, identb):
                    eng.affine_select(out=m[:, :], in_=m[:, :], compare_op=ALU.not_equal, fill=1.0, base=0,
                                      pattern=[[-1, P]], channel_multiplier=1).then_inc(S["const"], 1)
                eng.iota(iota[:, :], [[1, R * WIN]], base=0, channel_multiplier=0,
                         allow_small_or_imprecise_dtypes=True).then_inc(S["const"], 1)
                eng.memset(ones[:, :], 1.0).then_inc(S["const"], 1)
                eng.memset(onef[:, :], 1.0).then_inc(S["const"], 1)
                eng.memset(onec[:, :], 1.0)
                eng.memset(eps[:, :], 1e-5).then_inc(S["const"], 1)
                for t in range(T):
                    wait(eng, S["hi"], t + 1)
                    wait(eng, S["mid"], t + 1)
                    wait(eng, S["lo"], t + 1)
                    eng.dma_start(table0[t * P:(t + 1) * P, :], hs[:, t % NH, :]).then_inc(s_t0[t % NH], 16)
                for k in range(NH):
                    wait(eng, s_t0[k], 16 * ((T - k + NH - 1) // NH))

            @block.vector
            def _(eng):
                seg_f, base, rel, orig = (small[:, i, :] for i in range(4))
                ne = [0]

                def step(ins):
                    ne[0] += 1
                    ins.then_inc(S["epse"], 1)
                    wait(eng, S["epse"], ne[0])

                wait(eng, S["const"], 1)
                mid_c = float((D.cps - 1) // 2)
                step(eng.tensor_scalar(seg_f, chunk_id[:, :], -mid_c, 1.0 / D.cps, ALU.add, ALU.mult))
                step(eng.tensor_copy(seg_i[:, :], seg_f))
                step(eng.tensor_copy(orig, seg_i[:, :]))
                step(eng.tensor_scalar(orig, orig, float(P), float(-HALF), ALU.mult, ALU.add))
                wait(eng, S["ld_e"], 16 * 3 * n_edma)
                step(eng.tensor_copy(ef[2][:, :, :], er[0][:, :, :]))
                step(eng.tensor_reduce(base, ef[2][:, :, :], AX.X, ALU.min))
                step(eng.tensor_tensor(rel, base, orig, ALU.subtract))
                step(eng.tensor_scalar(rel, rel, 0.0, float(LIM), ALU.max, ALU.min))
                step(eng.tensor_tensor(base, rel, orig, ALU.add))
                bc = small[:, 1, :].unsqueeze(2).to_broadcast([P, KT, P])
                step(eng.tensor_tensor(ef[2][:, :, :], ef[2][:, :, :], bc, ALU.subtract))
                step(eng.tensor_scalar(ef[1][:, :, :], er[2][:, :, :], float(WIN), None, ALU.mult))
                step(eng.tensor_tensor(ef[1][:, :, :], ef[1][:, :, :], ef[2][:, :, :], ALU.add))
                eng.tensor_scalar(ef[0][:, :, :], er[1][:, :, :], float(HALF), None, ALU.add).then_inc(S["edge"], 1)
                step(eng.tensor_scalar(inw[:, :, :], ef[2][:, :, :], 0.0, None, ALU.is_ge))
                step(eng.scalar_tensor_tensor(inw[:, :, :], ef[2][:, :, :], float(WIN), inw[:, :, :], ALU.is_lt, ALU.mult))
                eng.tensor_reduce(cnt_in[:, :], inw[:, :, :], AX.XY, ALU.add).then_inc(S["inw"], 1)

                for li, (a, b) in enumerate(XL):
                    n_x = (a == 0) + (min(b, FULLT + 1) > max(a, 1)) + (b == T)
                    wait(eng, s_x[li], 16 * n_x)
                    for t in range(a, b):
                        last = eng.bn_stats(st6[:, t, :], xres[:, t, :])
                    last.then_inc(S["stat"], 1)
                    wait(eng, S["stat"], li + 1)
                    for t in range(a, b):
                        last = eng.bn_aggr(mv[:, t, :], st6[:, t, :])
                    last.then_inc(S["agg"], 1)
                for li, (a, b) in enumerate(XL):
                    wait(eng, S["sd"], li + 1)
                    eng.reciprocal(rs[:, a:b], rs[:, a:b]).then_inc(S["rstd"], 1)
                    wait(eng, S["rstd"], li + 1)
                    eng.scalar_tensor_tensor(nb[:, a:b], mv[:, a:b, 0], -1.0, rs[:, a:b], ALU.mult, ALU.mult).then_inc(S["nbias"], 1)

                copies = []
                for a, dest in ((0, idxT), (1, keyT[0]), (2, keyT[1])):
                    for q in range(0, KT, 4):
                        m = min(4, KT - q)
                        copies.append((dest[:, q * P:(q + m) * P], ps_slot[:, len(copies) % 6, 0:m * P]))
                copies.append((relT[:, :], ps_slot[0:KT, len(copies) % 6, 0:P]))
                for r in range(R):
                    copies.append((w0t[:, r, :, :].rearrange("p b o -> p (b o)"), ps_slot[:, len(copies) % 6, 0:NB * DF]))
                n_edge = len(copies) - R

                def copy(i):
                    wait(eng, S["etp"], i + 1)
                    ins = eng.tensor_copy(copies[i][0], copies[i][1])
                    ins.then_inc(S["ecp"], 1)
                    if i == n_edge - 1:
                        wait(eng, S["ecp"], i + 1)
                        eng.memset(small[:, 5, 0:1], 0.0).then_inc(S["rel"], 1)

                wait(eng, S["cntp"], 1)
                eng.tensor_copy(n_inside[:, :], ps_aux[0:1, 0:1]).then_inc(S["cnt"], 1)
                done = 0
                for t in range(T):
                    k = t % NH
                    wait(eng, S["h32"], t + 1)
                    wait(eng, S["hi"], t + 1)
                    if t >= NH:
                        wait(eng, S["mid"], t - NH + 1)
                    eng.tensor_tensor(r1[:, k, :], h32[:, k, :], hs[:, k, 0:DF], ALU.subtract).then_inc(S["r1"], 1)
                    if done < len(copies):
                        copy(done)
                        done += 1
                    wait(eng, S["r1"], t + 1)
                    wait(eng, S["mid"], t + 1)
                    eng.tensor_tensor(hs[:, k, 2 * DF:DF3], r1[:, k, :], hs[:, k, DF:2 * DF], ALU.subtract).then_inc(S["lo"], 1)
                while done < len(copies):
                    copy(done)
                    done += 1

            @block.tensor
            def _(eng):
                wait(eng, S["const"], 7)
                wait(eng, S["inw"], 1)
                eng.matmul(ps_aux[0:1, 0:1], cnt_in[:, :], onec[:, :], start=True, stop=True).then_inc(S["cntp"], 1)
                wait(eng, S["edge"], 1)
                n = 0
                for a in (0, 1, 2):
                    for q in range(0, KT, 4):
                        wait(eng, S["ecp"], n - 5)
                        for k in range(q, min(q + 4, KT)):
                            last = eng.transpose(ps_slot[:, n % 6, (k - q) * P:(k - q + 1) * P], ef[a][:, k, :], ident[:, :])
                        last.then_inc(S["etp"], 1)
                        n += 1
                wait(eng, S["ecp"], n - 5)
                eng.transpose(ps_slot[0:KT, n % 6, 0:P], small[:, 2, :], ident[:, :]).then_inc(S["etp"], 1)
                n += 1
                wait(eng, S["ld_w"], 16)
                for r in range(R):
                    wait(eng, S["ecp"], n - 5)
                    for ib in range(NB):
                        for ob in range(NB):
                            last = eng.transpose(ps_slot[:, n % 6, ib * DF + ob * P:ib * DF + (ob + 1) * P],
                                                 wld[:, r, ob, ib * P:(ib + 1) * P], ident[:, :])
                    last.then_inc(S["etp"], 1)
                    n += 1

        def shared(layer):
            return dict(table=(table0, table1)[layer], table1=table1, out=out, idxT=idxT, key=keyT[layer],
                        offr=offr, iota=iota, ones=ones, onef=onef, ident=ident, identb=identb, eps=eps, xres=xres,
                        w0t=w0t, w1s=w1s, bias0=bias0, bias1=bias1, dinv=dinv, ps_slot=ps_slot, ps_proj=ps_proj,
                        ps_aux=ps_aux, src=src, dst=dst, etype=etype)

        inside = nc.values_load(n_inside[0:1, 0:1], min_val=0, max_val=E)
        with nc.If(inside == E):
            for layer in (0, 1):
                aggregate(nc, D, layer, shared(layer))
        with nc.Else():
            for layer in (0, 1):
                aggregate_any(nc, D, layer, shared(layer))


def finishing(nc, D, layer, V, ctx, path):
    f32, bf16 = mybir.dt.float32, mybir.dt.bfloat16
    ALU, ACT = mybir.AluOpType, mybir.ActivationFunctionType
    first = layer == 0
    R = D.rel if first else 1
    NB, DF, DF3, T = D.nb, D.d, 3 * D.d, D.tiles
    xres, ps_proj, dinv = V["xres"], V["ps_proj"], V["dinv"]

    def sb(name, shape, dt):
        return ctx.enter_context(nc.sbuf_tensor(f"{name}_{path}{layer}", shape, dt))

    def sem(name):
        return ctx.enter_context(nc.semaphore(f"{path}{layer}_{name}"))

    tile_in = sb("tile_in", [P, NB, R, P], f32)
    st6 = sb("st6", [P, 6], f32)
    mv = sb("mv", [P, 2], f32)
    v2 = sb("v2", [P, 2], f32)
    r2 = sb("r2", [P, 2], f32)
    ab = sb("ab", [P, 2], f32)
    x1 = sb("x1", [P, DF], f32)
    h32 = sb("h32", [P, DF], f32)
    r1 = sb("r1", [P, DF], f32)
    hs = sb("hs", [P, DF3], bf16)
    y = sb("y", [P, DF], f32)
    z = sb("z", [P, DF], f32)

    s_mark = [sem(f"mark{i}") for i in range(2)]
    s_cpa = sem("copy_act")
    s_cpv = sem("copy_dve")
    s_proj = sem("proj")
    s_x1 = sem("x1")
    E = {k: sem("e_" + k) for k in ("stat", "agg", "cnt", "v2", "sd", "r2", "a", "ab", "h32", "hi", "r1",
                                    "mid", "lo", "st", "y", "z", "o", "self_ld", "self_mm", "deg", "keep")}

    def tile_io(eng, t):
        if first:
            wait(eng, E["hi"], t + 1)
            wait(eng, E["mid"], t + 1)
            wait_alone(eng, E["lo"], t + 1, s_mark[1])
            eng.dma_start(V["table1"][bass.ds(t * P, P), :], hs[:, :]).then_inc(E["st"], 16)
            wait_alone(eng, E["st"], 16 * (t + 1), s_mark[1])
        else:
            wait_alone(eng, E["z"], t + 1, s_mark[1])
            if isinstance(t, int) and t == 0:
                eng.dma_start(V["out"][0:HALF, :], z[HALF:P, :]).then_inc(E["o"], 16)
            elif isinstance(t, int) and t == T - 1:
                eng.dma_start(V["out"][D.n - D.last_rows:D.n, :], z[0:D.last_rows, :]).then_inc(E["o"], 16)
            else:
                eng.dma_start(V["out"][bass.ds(t * P - HALF, P), :], z[:, :]).then_inc(E["o"], 16)
            wait_alone(eng, E["o"], 16 * (t + 1), s_mark[1])

    def finish_act(eng, t):
        if not first:
            return
        wait(eng, E["v2"], t + 1)
        eng.activation(r2[:, :], v2[:, :], ACT.Sqrt).then_inc(E["sd"], 1)
        wait(eng, E["ab"], t + 1)
        eng.activation(xres[:, t, :], x1[:, :], ACT.Copy).then_inc(E["keep"], 1)
        eng.activation(h32[:, :], x1[:, :], ACT.Relu, scale=ab[:, 0:1], bias=ab[:, 1:2]).then_inc(E["h32"], 1)
        wait(eng, E["h32"], t + 1)
        wait(eng, E["st"], 16 * t)
        eng.activation(hs[:, 0:DF], h32[:, :], ACT.Copy).then_inc(E["hi"], 1)
        wait(eng, E["r1"], t + 1)
        eng.activation(hs[:, DF:2 * DF], r1[:, :], ACT.Copy).then_inc(E["mid"], 1)

    def finish_dve(eng, t):
        xt = xres[:, t, :]
        wait(eng, s_proj, t + 1)
        if first:
            wait(eng, E["keep"], t)
            eng.tensor_tensor(x1[:, :], ps_proj[:, 0:DF], xt, ALU.add).then_inc(s_x1, 1)
            wait(eng, s_x1, t + 1)
            eng.bn_stats(st6[:, :], x1[:, :]).then_inc(E["stat"], 1)
            wait(eng, E["deg"], t + 1)
            wait(eng, E["stat"], t + 1)
            eng.tensor_scalar(v2[:, 1:2], dinv[:, bass.ds(t, 1)], 1.0, None, ALU.add)
            eng.bn_aggr(mv[:, :], st6[:, :]).then_inc(E["agg"], 1)
            wait(eng, E["agg"], t + 1)
            eng.tensor_scalar(v2[:, 0:1], mv[:, 1:2], 1e-5, None, ALU.add).then_inc(E["v2"], 1)
            wait(eng, E["sd"], t + 1)
            eng.reciprocal(r2[:, :], r2[:, :]).then_inc(E["r2"], 1)
            wait(eng, E["r2"], t + 1)
            eng.tensor_scalar(dinv[:, bass.ds(t, 1)], r2[:, 1:2], 1.0, None, ALU.mult)
            eng.tensor_tensor(ab[:, 0:1], r2[:, 0:1], r2[:, 1:2], ALU.mult).then_inc(E["a"], 1)
            wait(eng, E["a"], t + 1)
            eng.scalar_tensor_tensor(ab[:, 1:2], mv[:, 0:1], -1.0, ab[:, 0:1], ALU.mult, ALU.mult).then_inc(E["ab"], 1)
            wait(eng, E["h32"], t + 1)
            wait(eng, E["hi"], t + 1)
            eng.tensor_tensor(r1[:, :], h32[:, :], hs[:, 0:DF], ALU.subtract).then_inc(E["r1"], 1)
            wait(eng, E["r1"], t + 1)
            wait(eng, E["mid"], t + 1)
            eng.tensor_tensor(hs[:, 2 * DF:DF3], r1[:, :], hs[:, DF:2 * DF], ALU.subtract).then_inc(E["lo"], 1)
        else:
            eng.scalar_tensor_tensor(y[:, :], ps_proj[:, 0:DF], dinv[:, bass.ds(t, 1)], V["bias1"][:, :],
                                     ALU.mult, ALU.add).then_inc(s_x1, 1)
            wait(eng, s_x1, t + 1)
            eng.scalar_tensor_tensor(h32[:, :], y[:, :], 0.2, y[:, :], ALU.mult, ALU.max).then_inc(E["y"], 1)
            wait(eng, E["y"], t + 1)
            wait(eng, E["o"], 16 * t)
            eng.tensor_tensor(z[:, :], h32[:, :], xt, ALU.add).then_inc(E["z"], 1)

    def project(eng, t, part, act_share=True):
        if part == 0:
            wait(eng, s_cpv, t + 1)
            if first and act_share:
                wait(eng, s_cpa, t + 1)
            wait(eng, s_x1, t)
        if first:
            if part == 0:
                eng.matmul(ps_proj[:, 0:DF], V["onef"][:, :], V["bias0"][:, :], start=True, stop=False)
            for r in range(part * R // 2, (part + 1) * R // 2):
                for b in range(NB):
                    last = eng.matmul(ps_proj[:, 0:DF], tile_in[:, b, r, :], V["w0t"][:, r, b, :], start=False,
                                      stop=(r == R - 1 and b == NB - 1))
        else:
            last = eng.matmul(ps_proj[:, 0:DF], tile_in[:, part, 0, :], V["w1s"][:, part, :],
                              start=(part == 0), stop=(part == 1))
        if part == 1:
            last.then_inc(s_proj, 1)

    return dict(tile_in=tile_in, hs=hs, E=E, s_proj=s_proj, s_x1=s_x1, s_cpv=s_cpv, s_cpa=s_cpa, s_mark=s_mark,
                tile_io=tile_io, finish_act=finish_act, finish_dve=finish_dve, project=project)


def aggregate(nc, D, layer, V):
    f32, bf16, i32 = mybir.dt.float32, mybir.dt.bfloat16, mybir.dt.int32
    ALU, ACT, AX = mybir.AluOpType, mybir.ActivationFunctionType, mybir.AxisListType
    first = layer == 0
    R = D.rel if first else 1
    NBLK = D.nb + 1 if first else D.nb
    NB, DF, DF3, T, CPS, SEGS = D.nb, D.d, 3 * D.d, D.tiles, D.cps, D.segs
    W = R * WIN
    LIM = 2 * P
    AW = LIM + WIN
    idxT, key, offr, iota, ps_slot, ps_aux, dinv = (V[k] for k in ("idxT", "key", "offr", "iota", "ps_slot", "ps_aux", "dinv"))

    with ExitStack() as ctx:
        def sb(name, shape, dt):
            return ctx.enter_context(nc.sbuf_tensor(f"{name}_{layer}", shape, dt))

        def sem(name):
            return ctx.enter_context(nc.semaphore(f"s{layer}_{name}"))

        acc = sb("acc", [P, NBLK, R, AW], f32)
        onehot = sb("onehot", [P, 3, GRP, W], bf16)
        rows = sb("rows", [P, 3, GRP, DF3], bf16)
        stage = sb("stage", [P, 3, GRP], i32)
        scr = sb("scr", [P, R, P], f32)
        F = finishing(nc, D, layer, V, ctx, "s")
        tile_in, hs, E, s_proj, s_x1, s_cpv, s_cpa, s_mark = (
            F[k] for k in ("tile_in", "hs", "E", "s_proj", "s_x1", "s_cpv", "s_cpa", "s_mark"))

        s_zero = sem("zero")
        s_stage = sem("stage")
        s_rows = [sem(f"rows{g}") for g in range(3)]
        s_oh = sem("onehot")
        s_pe = sem("chunk")
        s_acc = sem("acc")
        s_sha = sem("shift_act")
        s_shv = sem("shift_dve")
        s_tla = sem("tail_act")
        s_tlv = sem("tail_dve")
        s_bnd = sem("boundary")
        s_bndv = sem("boundary_dve")
        def cidx(s, g, j):
            return s * CPS + g * GRP + j

        def bank(g, j):
            return (g * GRP + j) % NBANK

        def last_use(g, j):
            c = g * GRP + j
            return c - NBANK if c >= NBANK else max(k for k in range(CPS) if k % NBANK == c) - CPS

        block = ctx.enter_context(nc.Block())

        @block.gpsimd
        def _(eng):
            def body(s):
                for g in range(3):
                    wait_alone(eng, s_stage, s * 3 + g + 1, s_mark[0])
                    for j in range(GRP):
                        eng.indirect_dma_start(rows[:, g, j, :], None, V["table"],
                                               bass.IndirectOffsetOnAxis(ap=stage[:, g, j:j + 1], axis=0)).then_inc(s_rows[g], 16)
            body(0)
            body(1)
            with eng.Fori(2, SEGS) as s:
                body(s)

        @block.sync
        def _(eng):
            def load_self(t):
                if not first:
                    if not isinstance(t, int) or t > 0:
                        wait_alone(eng, E["self_mm"], t, s_mark[1])
                    eng.dma_start(hs[:, :], V["table"][bass.ds(t * P, P), :]).then_inc(E["self_ld"], 16)
                    wait_alone(eng, E["self_ld"], 16 * (t + 1), s_mark[1])
            load_self(0)
            load_self(1)
            F["tile_io"](eng, 0)
            with eng.Fori(2, SEGS) as s:
                load_self(s)
                F["tile_io"](eng, s - 1)
            load_self(T - 1)
            F["tile_io"](eng, T - 2)
            F["tile_io"](eng, T - 1)

        @block.scalar
        def _(eng):
            def put_stage(s, g):
                wait(eng, s_pe, cidx(s - 1, g + 1, 0))
                eng.activation(stage[:, g, :], idxT[:, bass.ds(cidx(s, g, 0), GRP)], ACT.Copy).then_inc(s_stage, 1)

            def boundary(s):
                wait(eng, s_acc, cidx(s + 1, 0, 0))
                wait(eng, s_proj, s)
                if first:
                    eng.activation(tile_in[:, 0, :, :], acc[:, 0, :, 0:P], ACT.Copy).then_inc(s_cpa, 1)
                    wait(eng, s_cpa, s + 1)
                    eng.activation(acc[:, 0, :, 0:P], acc[:, 0, :, P:LIM], ACT.Copy).then_inc(s_sha, 1)
                    wait(eng, s_sha, s + 1)
                    eng.activation(acc[:, 0, :, P:P + WIN], acc[:, 0, :, LIM:AW], ACT.Copy).then_inc(s_tla, 1)
                    wait(eng, s_tla, s + 1)
                    eng.activation(acc[:, 0, :, P + WIN:AW], V["ident"][:, 0:1].unsqueeze(1).to_broadcast([P, R, P]), ACT.Copy,
                                   scale=0.0).then_inc(s_bnd, 1)

            def body(s):
                put_stage(s + 1, 0)
                put_stage(s + 1, 1)
                put_stage(s + 1, 2)
                boundary(s)
                if not (isinstance(s, int) and s == 0):
                    F["finish_act"](eng, s - 1)

            for g in range(3):
                put_stage(0, g)
            body(0)
            body(1)
            with eng.Fori(2, SEGS) as s:
                body(s)
            F["finish_act"](eng, T - 2)
            F["finish_act"](eng, T - 1)

        @block.vector
        def _(eng):
            def build_onehot(s, g):
                wait(eng, s_pe, cidx(s - 1, g + 1, 0))
                k = key[:, bass.ds(cidx(s, g, 0), GRP)]
                eng.tensor_tensor(onehot[:, g, :, :], iota[:, 0:W].unsqueeze(1).to_broadcast([P, GRP, W]),
                                  k.unsqueeze(2).to_broadcast([P, GRP, W]), ALU.is_equal).then_inc(s_oh, 1)

            def accumulate(s, g):
                _, off = nc.values_load_multi_w_load_instructions(
                    offr[0:1, s * 3 + g, 0:GRP], engines=(mybir.EngineType.DVE,), min_val=0, max_val=LIM,
                    skip_runtime_bounds_check_because="the window starts are clamped to 0..LIM when they are computed")
                for j in range(GRP):
                    c = cidx(s, g, j)
                    wait(eng, s_pe, c + 1)
                    wait(eng, s_acc, c)
                    win = acc[:, :, :, :].rearrange("p b r w -> p (b r) w")[:, :, bass.ds(off[j], WIN)]
                    part = ps_slot[:, bank(g, j), 0:NBLK * W].rearrange("p (q w) -> p q w", w=WIN)
                    ins = eng.tensor_tensor(win, part, win, ALU.add)
                    ins.then_inc(s_acc, 1)

            def boundary(s, shift=True):
                wait(eng, s_acc, cidx(s + 1, 0, 0) if shift else SEGS * CPS)
                wait(eng, s_proj, s)
                if first:
                    own = slice(1, NBLK) if shift else slice(0, NBLK)
                    eng.tensor_tensor(scr[:, :, :], acc[:, NB, :, 0:P],
                                      V["ident"][:, :].unsqueeze(1).to_broadcast([P, R, P]), ALU.mult).then_inc(E["cnt"], 1)
                    b0 = 1 if shift else 0
                    eng.tensor_copy(tile_in[:, b0:NB, :, :], acc[:, b0:NB, :, 0:P]).then_inc(s_cpv, 1)
                    wait(eng, E["cnt"], s + 1)
                    eng.tensor_reduce(dinv[:, bass.ds(s, 1)], scr[:, :, :].rearrange("p r w -> p (r w)"), AX.X, ALU.add).then_inc(E["deg"], 1)
                else:
                    own = slice(0, NBLK)
                    wait(eng, E["self_mm"], s + 1)
                    eng.tensor_tensor(tile_in[:, :, 0, :], acc[:, :, 0, 0:P],
                                      ps_aux[:, 0:NB * P].rearrange("p (b w) -> p b w", b=NB), ALU.add).then_inc(s_cpv, 1)
                if shift:
                    wait(eng, s_cpv, s + 1)
                    eng.tensor_copy(acc[:, own, :, 0:P], acc[:, own, :, P:LIM]).then_inc(s_shv, 1)
                    wait(eng, s_shv, s + 1)
                    eng.tensor_copy(acc[:, own, :, P:P + WIN], acc[:, own, :, LIM:AW]).then_inc(s_tlv, 1)
                    wait(eng, s_tlv, s + 1)
                    eng.memset(acc[:, own, :, P + WIN:AW], 0.0).then_inc(s_bndv, 1)

            def body(s):
                for g in range(3):
                    build_onehot(s + (g + 1) // 3, (g + 1) % 3)
                    if g == 0:
                        wait(eng, s_zero, 1)
                        if first:
                            wait(eng, s_bnd, s)
                        wait(eng, s_bndv, s)
                    accumulate(s, g)
                boundary(s)
                if not (isinstance(s, int) and s == 0):
                    F["finish_dve"](eng, s - 1)

            eng.memset(acc[:, :, :, :], 0.0).then_inc(s_zero, 1)
            build_onehot(0, 0)
            body(0)
            body(1)
            with eng.Fori(2, SEGS) as s:
                body(s)
            F["finish_dve"](eng, T - 2)
            if first:
                wait(eng, s_bnd, SEGS)
            wait(eng, s_bndv, SEGS)
            boundary(T - 1, shift=False)
            F["finish_dve"](eng, T - 1)

        @block.tensor
        def _(eng):
            def self_rows(t):
                if first:
                    return
                wait(eng, E["self_ld"], 16 * (t + 1))
                wait(eng, s_cpv, t)
                for b in range(NB):
                    for p in range(3):
                        last = eng.matmul(ps_aux[:, b * P:(b + 1) * P], hs[:, p * DF + b * P:p * DF + (b + 1) * P],
                                          V["identb"][:, :], start=(p == 0), stop=(p == 2))
                last.then_inc(E["self_mm"], 1)

            def group(s, g):
                wait(eng, s_rows[g], (s + 1) * (16 * GRP))
                wait(eng, s_oh, s * 3 + g + 1)
                for j in range(GRP):
                    wait(eng, s_acc, cidx(s, 0, 0) + last_use(g, j) + 1)
                    o = ps_slot[:, bank(g, j), :]
                    for b in range(NB):
                        for p in range(3):
                            last = eng.matmul(o[:, b * W:(b + 1) * W], rows[:, g, j, p * DF + b * P:p * DF + (b + 1) * P],
                                              onehot[:, g, j, :], start=(p == 0), stop=(p == 2))
                    if first:
                        last = eng.matmul(o[:, NB * W:(NB + 1) * W], V["ones"][:, :], onehot[:, g, j, :], start=True, stop=True)
                    last.then_inc(s_pe, 1)

            def body(s):
                self_rows(s)
                for g in range(3):
                    group(s, g)
                    if g < 2 and not (isinstance(s, int) and s == 0):
                        F["project"](eng, s - 1, g)

            body(0)
            body(1)
            with eng.Fori(2, SEGS) as s:
                body(s)
            self_rows(T - 1)
            for t in (T - 2, T - 1):
                F["project"](eng, t, 0, act_share=t < T - 1)
                F["project"](eng, t, 1)


def aggregate_any(nc, D, layer, V):
    f32, bf16, i32 = mybir.dt.float32, mybir.dt.bfloat16, mybir.dt.int32
    ALU, AX = mybir.AluOpType, mybir.AxisListType
    first = layer == 0
    R = D.rel if first else 1
    NB, DF, DF3, T, E_, CH = D.nb, D.d, 3 * D.d, D.tiles, D.e, D.chunks
    SW = DF + 4
    NROW = T * P * R
    idxT, ps_slot, ps_aux, dinv, ident = (V[k] for k in ("idxT", "ps_slot", "ps_aux", "dinv", "ident"))
    sums = nc.dram_tensor(f"sums{layer}", (NROW, SW), f32).ap()
    dst_p = nc.dram_tensor(f"dst_p{layer}", (CH * P,), i32).ap()
    typ_p = nc.dram_tensor(f"typ_p{layer}", (CH * P,), i32).ap()
    pad = CH * P - E_

    with ExitStack() as ctx:
        def sb(name, shape, dt):
            return ctx.enter_context(nc.sbuf_tensor(f"{name}_a{layer}", shape, dt))

        def sem(name):
            return ctx.enter_context(nc.semaphore(f"a{layer}_{name}"))

        F = finishing(nc, D, layer, V, ctx, "g")
        tile_in, hs, E = F["tile_in"], F["hs"], F["E"]
        padt = sb("padt", [1, 2, P], i32)
        tri = sb("tri", [P, P], f32)
        drow, trow = sb("drow", [P, P], i32), sb("trow", [P, P], i32)
        dcol, tcol = sb("dcol", [P, 1], i32), sb("tcol", [P, 1], i32)
        krow, same, dup = sb("krow", [P, P], f32), sb("same", [P, P], f32), sb("dup", [P, P], f32)
        kcol, ndup, wcol = sb("kcol", [P, 1], f32), sb("ndup", [P, 1], f32), sb("wcol", [P, 1], f32)
        idx, kidx, widx = sb("idx", [P, 1], i32), sb("kidx", [P, 1], i32), sb("widx", [P, 1], i32)
        grow = sb("grow", [P, DF3], bf16)
        vals, old = sb("vals", [P, SW], f32), sb("old", [P, SW], f32)
        big = sb("big", [P, R, SW], f32)
        selff = sb("selff", [P, DF], f32)

        s_c = sem("const")
        s_ch = sem("chain")
        s_pad, s_zero, s_copy = sem("pad"), sem("zero"), sem("copy")
        s_ld, s_idx, s_kidx, s_row, s_old = sem("ld"), sem("idx"), sem("kidx"), sem("row"), sem("old")
        s_vals, s_mm, s_new, s_put = sem("vals"), sem("mm"), sem("new"), sem("put")
        s_big, s_self, s_tp, s_tc, s_free = sem("big"), sem("self"), sem("tp"), sem("tc"), sem("free")
        SETUP, STEPS, TSTEPS = 4, 12 if first else 10, 0

        def chunks(body, eng):
            body(0)
            with eng.Fori(1, CH) as c:
                body(c)

        def tiles(body, eng):
            body(0)
            with eng.Fori(1, T - 1) as t:
                body(t)
            body(T - 1)

        with nc.Block() as block:
            @block.gpsimd
            def _(eng):
                eng.memset(tri[:, :], 1.0).then_inc(s_c, 1)
                wait(eng, s_c, 1)
                eng.affine_select(out=tri[:, :], in_=tri[:, :], compare_op=ALU.is_gt, fill=0.0, base=0,
                                  pattern=[[-1, P]], channel_multiplier=1).then_inc(s_c, 1)
                wait(eng, s_zero, 16 * T)
                wait(eng, s_ch, SETUP)

                def body(c):
                    wait_alone(eng, s_idx, c + 1, F["s_mark"][0])
                    eng.indirect_dma_start(grow[:, :], None, V["table"], bass.IndirectOffsetOnAxis(ap=idx[:, 0:1], axis=0)).then_inc(s_row, 16)
                    if not isinstance(c, int) or c > 0:
                        wait_alone(eng, s_put, 16 * c, F["s_mark"][0])
                    wait_alone(eng, s_kidx, c + 1, F["s_mark"][0])
                    eng.indirect_dma_start(old[:, :], None, sums, bass.IndirectOffsetOnAxis(ap=kidx[:, 0:1], axis=0),
                                           bounds_check=NROW - 1, oob_is_err=False).then_inc(s_old, 16)
                    wait_alone(eng, s_new, c + 1, F["s_mark"][0])
                    eng.indirect_dma_start(sums, bass.IndirectOffsetOnAxis(ap=widx[:, 0:1], axis=0), old[:, :], None,
                                           bounds_check=NROW - 1, oob_is_err=False).then_inc(s_put, 16)
                chunks(body, eng)
                wait(eng, s_put, 16 * CH)

            @block.sync
            def _(eng):
                wait(eng, s_ch, SETUP)
                for i, (a, b) in enumerate(((V["dst"], dst_p), (V["etype"], typ_p))):
                    eng.dma_start(b[0:E_], a).then_inc(s_copy, 16)
                    eng.dma_start(b[E_:CH * P].rearrange("(o p) -> o p", o=1), padt[:, i, 0:pad]).then_inc(s_copy, 16)
                with eng.Fori(0, T) as t:
                    eng.dma_start(sums[bass.ds(t * (P * R), P * R), :].rearrange("(p r) w -> p (r w)", r=R),
                                  big[:, :, :].rearrange("p r w -> p (r w)")).then_inc(s_zero, 16)
                wait(eng, s_zero, 16 * T)
                wait(eng, s_copy, 64)

                def body(c):
                    if not isinstance(c, int) or c > 0:
                        wait(eng, s_ld, 64 * c)
                        wait_alone(eng, s_new, c, F["s_mark"][1])
                    for a, row, col in ((dst_p, drow, dcol), (typ_p, trow, tcol)):
                        part = a[bass.ds(c * P, P)]
                        eng.dma_start(row[:, :], part.rearrange("(o p) -> o p", o=1).to_broadcast([P, P])).then_inc(s_ld, 16)
                        eng.dma_start(col[:, :], part.rearrange("(p o) -> p o", o=1)).then_inc(s_ld, 16)
                chunks(body, eng)
                wait(eng, s_ld, 64 * CH)

            @block.vector
            def _(eng):
                n = [0]

                def step(ins, at=0):
                    n[0] += 1
                    ins.then_inc(s_ch, 1)
                    wait(eng, s_ch, at + n[0])

                step(eng.memset(big[:, :, :], 0.0))
                step(eng.memset(padt[:, 0, :], int(PAD_DST)))
                step(eng.memset(padt[:, 1, :], 0))
                eng.memset(vals[:, DF + 1:SW], 0.0)
                eng.memset(vals[:, DF:DF + 1], 1.0)
                step(eng.memset(old[:, :], 0.0))
                assert n[0] == SETUP
                wait(eng, s_c, 2)

                def body(c):
                    n[0] = 0
                    at = SETUP + c * STEPS
                    wait(eng, s_row, 16 * c)
                    eng.tensor_scalar(idx[:, :], idxT[:, bass.ds(c, 1)], 1.0, None, ALU.mult).then_inc(s_idx, 1)
                    wait(eng, s_ld, 64 * (c + 1))
                    step(eng.tensor_scalar(krow[:, :], drow[:, :], float(R), None, ALU.mult), at)
                    step(eng.tensor_scalar(kcol[:, :], dcol[:, :], float(R), None, ALU.mult), at)
                    if first:
                        step(eng.tensor_tensor(krow[:, :], krow[:, :], trow[:, :], ALU.add), at)
                        step(eng.tensor_tensor(kcol[:, :], kcol[:, :], tcol[:, :], ALU.add), at)
                    wait(eng, s_put, 16 * c)
                    eng.tensor_scalar(kidx[:, :], kcol[:, :], float(HALF * R), None, ALU.add).then_inc(s_kidx, 1)
                    step(eng.tensor_scalar(same[:, :], krow[:, :], kcol[:, :], None, ALU.is_equal), at)
                    step(eng.tensor_tensor(dup[:, :], same[:, :], tri[:, :], ALU.mult), at)
                    step(eng.tensor_reduce(ndup[:, :], dup[:, :], AX.X, ALU.add), at)
                    step(eng.tensor_scalar(ndup[:, :], ndup[:, :], 1.0, 4e6, ALU.min, ALU.mult), at)
                    step(eng.scalar_tensor_tensor(wcol[:, :], kcol[:, :], float(HALF * R), ndup[:, :], ALU.add, ALU.add), at)
                    step(eng.tensor_copy(widx[:, :], wcol[:, :]), at)
                    wait(eng, s_row, 16 * (c + 1))
                    step(eng.tensor_tensor(vals[:, 0:DF], grow[:, 0:DF], grow[:, DF:2 * DF], ALU.add), at)
                    step(eng.tensor_tensor(vals[:, 0:DF], vals[:, 0:DF], grow[:, 2 * DF:DF3], ALU.add), at)
                    assert n[0] == STEPS
                    eng.sem_inc(s_vals, 1)
                    wait(eng, s_old, 16 * (c + 1))
                    wait(eng, s_mm, c + 1)
                    eng.tensor_tensor(old[:, :], ps_aux[:, 0:SW], old[:, :], ALU.add).then_inc(s_new, 1)
                chunks(body, eng)

            @block.tensor
            def _(eng):
                def body(c):
                    wait(eng, s_vals, c + 1)
                    eng.matmul(ps_aux[:, 0:SW], same[:, :], vals[:, :], start=True, stop=True).then_inc(s_mm, 1)
                chunks(body, eng)

        with nc.Block() as block:
            @block.sync
            def _(eng):
                def body(t):
                    wait_alone(eng, s_free, t + 1, F["s_mark"][1])
                    eng.dma_start(big[:, :, :].rearrange("p r w -> p (r w)"),
                                  sums[bass.ds(t * (P * R), P * R), :].rearrange("(p r) w -> p (r w)", r=R)).then_inc(s_big, 16)
                    if not first:
                        eng.dma_start(hs[:, :], V["table"][bass.ds(t * P, P), :]).then_inc(s_self, 16)
                    F["tile_io"](eng, t)
                tiles(body, eng)
                wait(eng, s_big, 16 * T)
                if not first:
                    wait(eng, s_self, 16 * T)

            @block.tensor
            def _(eng):
                def body(t):
                    wait(eng, s_new, CH + 1 + t)
                    for i in range(R * NB):
                        r, b = divmod(i, NB)
                        last = eng.transpose(ps_slot[:, i // 4, (i % 4) * P:(i % 4 + 1) * P], big[:, r, b * P:(b + 1) * P], ident[:, :])
                    last.then_inc(s_tp, 1)
                    for part in range(2):
                        F["project"](eng, t, part, act_share=False)
                tiles(body, eng)

            @block.scalar
            def _(eng):
                tiles(lambda t: F["finish_act"](eng, t), eng)

            @block.vector
            def _(eng):
                eng.sem_inc(s_free, 1)

                def body(t):
                    wait(eng, s_big, 16 * (t + 1))
                    if first:
                        eng.tensor_reduce(dinv[:, bass.ds(t, 1)], big[:, :, DF], AX.X, ALU.add).then_inc(E["deg"], 1)
                        eng.sem_inc(s_new, 1)
                    else:
                        wait(eng, s_self, 16 * (t + 1))
                        eng.tensor_tensor(selff[:, :], hs[:, 0:DF], hs[:, DF:2 * DF], ALU.add).then_inc(E["cnt"], 1)
                        wait(eng, E["cnt"], t + 1)
                        eng.tensor_tensor(selff[:, :], selff[:, :], hs[:, 2 * DF:DF3], ALU.add).then_inc(E["stat"], 1)
                        wait(eng, E["stat"], t + 1)
                        eng.tensor_tensor(big[:, 0, 0:DF], big[:, 0, 0:DF], selff[:, :], ALU.add).then_inc(s_new, 1)
                    wait(eng, s_tp, t + 1)
                    tin = tile_in[:, :, :, :].rearrange("p b r w -> p r b w")
                    per = 4 // NB
                    for q in range(-(-R // per)):
                        m = min(per, R - q * per)
                        last = eng.tensor_copy(tin[:, q * per:q * per + m, :, :],
                                               ps_slot[:, q, 0:m * NB * P].rearrange("p (r b w) -> p r b w", r=m, b=NB))
                    last.then_inc(F["s_cpv"], 1)
                    F["finish_dve"](eng, t)
                    eng.sem_inc(s_free, 1)
                tiles(body, eng)


_INS = ['x', 'src', 'dst', 'edge_type_8', 'L0_gnn_weight', 'L0_gnn_bias', 'L1_gnn_W', 'L1_gnn_b']


def kernel(**inputs):
    import numpy as _np
    import concourse.bacc as _bacc
    from concourse import mybir as _mybir
    from concourse.bass_utils import run_bass_kernel_spmd as _run

    nc = _bacc.Bacc("TRN2", target_bir_lowering=False, num_devices=1)
    arrays, args = {}, []
    for name in _INS:
        a = _np.ascontiguousarray(inputs[name])
        arrays[f"in_{name}_dram"] = a
        args.append(nc.dram_tensor(f"in_{name}_dram", a.shape, _mybir.dt.from_np(a.dtype), kind="ExternalInput").ap())
    shape = tuple(inputs['x'].shape)
    args.append(nc.dram_tensor("out_0_dram", shape, _mybir.dt.float32, kind="ExternalOutput").ap())
    program(nc, *args)
    r = _run(nc, [arrays], core_ids=[0])
    return r.results[0]["out_0_dram"]
```

```python
import concourse.bass as bass
from concourse import mybir
from contextlib import ExitStack

P = 128
LOT = 3
WIN = 16
HALF = 64
LOTS = 11
GROUPS = ((0, 4), (4, 8), (8, 11))
NBANK = 6
NBANK1 = 3
SUB = 8
SPAN = 4
PAD_DST = 60000.0


class Dims:

    def __init__(self, n, e, d, rel):
        self.n, self.e, self.d, self.rel = n, e, d, rel
        self.nb = d // P
        self.cps = LOT * LOTS
        self.chunks = -(-e // P)
        self.segs = -(-self.chunks // self.cps)
        self.tiles = -(-(n + HALF) // P)
        self.kt = -(-(self.segs + 1) * LOTS // P)
        self.ncol = self.kt * P * LOT
        self.tg = self.tiles // 2
        self.td = self.tiles - self.tg
        self.nsub = self.td * P // SUB
        self.last_rows = n - (P * (self.tiles - 1) - HALF)


def wait(eng, sem, value):
    if isinstance(value, int) and value <= 0:
        return
    eng.wait_ge(sem, value)


def wait_alone(eng, sem, value, mark):
    eng.wait_ge(sem, value)
    eng.sem_inc(mark, 1)


def program(nc, x, src, dst, etype, w0, b0, w1, b1, out):
    f32, bf16, i32 = mybir.dt.float32, mybir.dt.bfloat16, mybir.dt.int32
    ALU, ACT, AX = mybir.AluOpType, mybir.ActivationFunctionType, mybir.AxisListType
    D = Dims(x.shape[0], src.shape[0], x.shape[1], w0.shape[0])
    N, E, DF, R, NB, KT, T = D.n, D.e, D.d, D.rel, D.nb, D.kt, D.tiles
    DF3 = 3 * DF
    LIM = 2 * P

    table0 = nc.dram_tensor("table0", (T * P, DF3), bf16).ap()
    table1 = nc.dram_tensor("table1", (T * P, DF3), bf16).ap()
    x1_d = nc.dram_tensor("x1_d", (T * P, DF), f32).ap()
    ends_d = nc.dram_tensor("ends_d", (2, D.ncol + SPAN), f32).ap()
    offs_d = nc.dram_tensor("offs_d", (KT, P), i32).ap()

    whole = ExitStack()
    with whole:
        def sb(name, shape, dt, ctx=whole):
            return ctx.enter_context(nc.sbuf_tensor(name, shape, dt))

        def sem(name, ctx=whole):
            return ctx.enter_context(nc.semaphore(name))

        ident = sb("ident", [P, P], f32)
        identb = sb("identb", [P, P], bf16)
        ones = sb("ones", [P, P], bf16)
        onef = sb("onef", [1, P], f32)
        iota = sb("iota", [P, R * WIN], bf16)
        LE = LOT * P
        eps = sb("eps", [P, 1], f32)
        bias0 = sb("bias0", [1, DF], f32)
        bias1 = sb("bias1", [P, DF], f32)
        WEND = T * DF + R * NB * DF
        arena = sb("arena", [P, max(WEND + D.ncol // 2, T * DF3 // 2)], f32)
        xres = arena[:, 0:T * DF].rearrange("p (t d) -> p t d", d=DF)
        w0t = arena[:, T * DF:WEND].rearrange("p (r b d) -> p r b d", r=R, b=NB)
        hs_all = arena[:, 0:T * DF3 // 2].bitcast(bf16).rearrange("p (t d) -> p t d", d=DF3)
        mkey = sb("mkey", [P, D.ncol], f32)
        klo = sb("klo", [P, D.ncol], f32)
        subr = sb("subr", [1, D.td, P // SUB], i32)
        w1s = sb("w1s", [P, NB, DF], f32)
        idxT = sb("idxT", [P, D.ncol], i32)
        keyT = [arena[:, WEND:WEND + D.ncol // 2].bitcast(bf16), sb("key1T", [P, D.ncol], bf16)[:, :]]
        n_inside = sb("n_inside", [1, 1], i32)
        offr = sb("offr", [1, D.segs, 12], i32)
        dinv = sb("dinv", [P, T], f32)

        ps_slot = whole.enter_context(nc.psum_tensor("ps_slot", [P, 6, 512], f32))
        ps_proj = whole.enter_context(nc.psum_tensor("ps_proj", [P, 512], f32))
        ps_aux = whole.enter_context(nc.psum_tensor("ps_aux", [P, 512], f32))

        with ExitStack() as pro:
            names = ("ld_e", "ld_x", "ld_w", "ld_c", "const", "memx", "edge", "etp", "ecp", "epse", "offw",
                     "offrd", "wtp", "wcp", "stat", "agg", "sd", "rstd", "nbias", "h32", "hi", "r1", "mid",
                     "lo", "padm", "rel", "cnst0", "inw", "cntp", "cnt", "ends", "endw",
                     "near", "bad", "wst", "below", "subp", "subc", "padf")
            S = {k: sem("p_" + k) for k in names}
            NH = 4
            XL = [(a, min(a + 6, T)) for a in range(0, T, 6)]
            s_t0 = [sem(f"p_t0_{i}") for i in range(NH)]
            s_x = [sem(f"p_x_{i}") for i in range(len(XL))]
            er = [sb(f"er{i}", [P, KT, LE], i32, pro) for i in range(3)]
            ef = [sb(f"ef{i}", [P, KT, LE], f32, pro) for i in range(4)]
            flat = [e[:, :, :].rearrange("p k j -> p (k j)") for e in er]
            inw, wid = ef[3], flat[1]
            dstT = flat[0].bitcast(f32)
            KC = KT * LOT
            ends = sb("ends", [P, 2, KC], f32, pro)
            near = sb("near", [P, 3, KC], f32, pro)
            bad = sb("bad", [P, 3, KC], f32, pro)
            wf = sb("wf", [P, 2, KC], f32, pro)
            wi = sb("wi", [P, 2, KC], i32, pro)
            padf = sb("padf", [2, SPAN], f32, pro)
            nbad = sb("nbad", [P, 2], f32, pro)
            wst_i = sb("wst_i", [P, D.nsub], i32, pro)
            wst = sb("wst", [P, D.nsub], f32, pro)
            cnt_in = sb("cnt_in", [P, 1], f32, pro)
            onec = sb("onec", [P, 1], f32, pro)
            chunk_id = sb("chunk_id", [P, KT], i32, pro)
            seg_i = sb("seg_i", [P, KT], i32, pro)
            small = sb("small", [P, 6, KT], f32, pro)
            relT = sb("relT", [KT, P], i32, pro)
            wld = sb("wld", [P, R, NB, DF], f32, pro)
            below = wld[:, :, :, :].rearrange("p r b i -> p (r b i)").bitcast(bf16)[:, 0:KC * D.nsub].rearrange("p (c w) -> p c w", w=D.nsub)
            st6 = sb("st6", [P, T, 6], f32, pro)
            mv = sb("mv", [P, T, 2], f32, pro)
            rs = sb("rs", [P, T], f32, pro)
            nb = sb("nb", [P, T], f32, pro)
            h32 = sb("h32", [P, NH, DF], f32, pro)
            r1 = sb("r1", [P, NH, DF], f32, pro)
            hs = sb("hs", [P, NH, DF3], bf16, pro)

            full = E // (P * LE)
            rest_rows = (E - full * P * LE) // LE
            rest = E - full * P * LE - rest_rows * LE
            assert full == KT - 1
            n_edma = 2 + (1 if rest else 0)
            FULLT = (N - HALF) // P

            block = pro.enter_context(nc.Block())

            @block.sync
            def _(eng):
                wait(eng, S["padm"], 3)
                for a, r in zip((dst, src, etype), er):
                    eng.dma_start(r[:, 0:full, :], a[0:full * P * LE].rearrange("(k p j) -> p k j", p=P, j=LE)).then_inc(S["ld_e"], 16)
                    o = full * P * LE
                    eng.dma_start(r[0:rest_rows, full, :], a[o:o + rest_rows * LE].rearrange("(p j) -> p j", j=LE)).then_inc(S["ld_e"], 16)
                    if rest:
                        o += rest_rows * LE
                        eng.dma_start(r[rest_rows:rest_rows + 1, full, 0:rest], a[o:o + rest].rearrange("(p j) -> p j", p=1)).then_inc(S["ld_e"], 16)
                wait(eng, S["ends"], 1)
                wait(eng, S["padf"], 1)
                eng.dma_start(ends_d[:, D.ncol:D.ncol + SPAN], padf[:, :]).then_inc(S["endw"], 16)
                for i in range(2):
                    eng.dma_start(ends_d[i, 0:D.ncol].rearrange("(k p q) -> p k q", p=P, q=LOT),
                                  ends[:, i, :].rearrange("p (k q) -> p k q", q=LOT)).then_inc(S["endw"], 16)
                wait(eng, S["endw"], 48)
                for i, (r, o) in enumerate(((1, 0), (0, 1), (0, SPAN))):
                    eng.dma_start(near[:, i, :], ends_d[r, o:o + D.ncol].rearrange("(p c) -> p c", p=P)).then_inc(S["near"], 16)
                def window_starts():
                    wait(eng, S["rel"], 1)
                    eng.dma_start(offs_d, relT[:, :]).then_inc(S["offw"], 16)
                    wait(eng, S["offw"], 16)
                    row = offs_d.rearrange("(o k) p -> o (k p)", o=1)[:, 0:D.segs * LOTS].rearrange("o (s j) -> o s j", j=LOTS)
                    eng.dma_start(offr[:, :, 0:LOTS], row).then_inc(S["offrd"], 16)

                for t in range(T):
                    wait(eng, S["hi"], t + 1)
                    wait(eng, S["mid"], t + 1)
                    wait(eng, S["lo"], t + 1)
                    eng.dma_start(table0[t * P:(t + 1) * P, :], hs[:, t % NH, :]).then_inc(s_t0[t % NH], 16)
                    if t == min(4 * KT + NH + 1, T - 1):
                        window_starts()
                for k in range(NH):
                    wait(eng, s_t0[k], 16 * ((T - k + NH - 1) // NH))
                wait(eng, S["offrd"], 16)
                wait(eng, S["near"], 48)

            @block.scalar
            def _(eng):
                wait(eng, S["memx"], 2)
                eng.dma_start(xres[HALF:P, 0, :], x[0:HALF, :]).then_inc(s_x[0], 16)
                for li, (a, b) in enumerate(XL):
                    lo_t, hi_t = max(a, 1), min(b, FULLT + 1)
                    if hi_t > lo_t:
                        eng.dma_start(xres[:, lo_t:hi_t, :], x[lo_t * P - HALF:hi_t * P - HALF, :].rearrange("(t p) d -> p t d", p=P)).then_inc(s_x[li], 16)
                    if b == T:
                        eng.dma_start(xres[0:D.last_rows, T - 1, :], x[N - D.last_rows:N, :]).then_inc(s_x[li], 16)
                eng.dma_start(wld[:, :, :, :], w0.rearrange("r (b p) i -> p r b i", p=P)).then_inc(S["ld_w"], 16)
                eng.dma_start(w1s[:, :, :], w1.rearrange("(b p) o -> p b o", p=P)).then_inc(S["ld_c"], 16)
                eng.dma_start(bias0[:, :], b0.rearrange("(o d) -> o d", o=1)).then_inc(S["ld_c"], 16)
                eng.dma_start(bias1[:, :], b1.rearrange("(o d) -> o d", o=1).to_broadcast([P, DF])).then_inc(S["ld_c"], 16)
                wait(eng, S["const"], 7)
                for li, (a, b) in enumerate(XL):
                    wait(eng, S["agg"], li + 1)
                    eng.activation(rs[:, a:b], mv[:, a:b, 1], ACT.Sqrt, bias=eps[:, :]).then_inc(S["sd"], 1)
                for t in range(T):
                    li = t // 6
                    k = t % NH
                    wait(eng, S["nbias"], li + 1)
                    wait(eng, S["lo"], t - NH + 1)
                    eng.activation(h32[:, k, :], xres[:, t, :], ACT.Relu, scale=rs[:, t:t + 1], bias=nb[:, t:t + 1]).then_inc(S["h32"], 1)
                    if t >= NH:
                        wait(eng, s_t0[k], 16 * (t // NH))
                    wait(eng, S["h32"], t + 1)
                    eng.activation(hs[:, k, 0:DF], h32[:, k, :], ACT.Copy).then_inc(S["hi"], 1)
                    wait(eng, S["r1"], t + 1)
                    eng.activation(hs[:, k, DF:2 * DF], r1[:, k, :], ACT.Copy).then_inc(S["mid"], 1)
                wait(eng, S["ld_c"], 48)

            @block.gpsimd
            def _(eng):
                eng.memset(er[0][:, full, :], int(PAD_DST)).then_inc(S["padm"], 1)
                eng.memset(er[1][:, full, :], 0).then_inc(S["padm"], 1)
                eng.memset(er[2][:, full, :], 0).then_inc(S["padm"], 1)
                eng.memset(xres[:, 0, :], 0.0).then_inc(S["memx"], 1)
                eng.memset(xres[:, T - 1, :], 0.0).then_inc(S["memx"], 1)
                eng.iota(chunk_id[:, :], [[P, KT]], base=0, channel_multiplier=1).then_inc(S["const"], 1)
                eng.memset(ident[:, :], 0.0).then_inc(S["cnst0"], 1)
                eng.memset(identb[:, :], 0.0).then_inc(S["cnst0"], 1)
                wait(eng, S["cnst0"], 2)
                for m in (ident, identb):
                    eng.affine_select(out=m[:, :], in_=m[:, :], compare_op=ALU.not_equal, fill=1.0, base=0,
                                      pattern=[[-1, P]], channel_multiplier=1).then_inc(S["const"], 1)
                eng.iota(iota[:, :], [[1, R * WIN]], base=0, channel_multiplier=0,
                         allow_small_or_imprecise_dtypes=True).then_inc(S["const"], 1)
                eng.memset(ones[:, :], 1.0).then_inc(S["const"], 1)
                eng.memset(onef[:, :], 1.0).then_inc(S["const"], 1)
                eng.memset(onec[:, :], 1.0)
                eng.memset(eps[:, :], 1e-5).then_inc(S["const"], 1)
                eng.memset(padf[:, :], PAD_DST).then_inc(S["padf"], 1)
                eng.iota(wst_i[:, :], [[SUB, D.nsub]], base=D.tg * P - HALF, channel_multiplier=0).then_inc(S["wst"], 1)
                for t in range(T):
                    k = t % NH
                    wait(eng, S["r1"], t + 1)
                    wait(eng, S["mid"], t + 1)
                    if t >= NH:
                        wait(eng, s_t0[k], 16 * (t // NH))
                    eng.tensor_tensor(hs[:, k, 2 * DF:DF3], r1[:, k, :], hs[:, k, DF:2 * DF], ALU.subtract).then_inc(S["lo"], 1)

            @block.vector
            def _(eng):
                seg_f, base, rel, orig = (small[:, i, :] for i in range(4))
                ne = [0]

                def step(ins):
                    ne[0] += 1
                    ins.then_inc(S["epse"], 1)
                    wait(eng, S["epse"], ne[0])

                wait(eng, S["const"], 1)
                mid_c = float((LOTS - 1) // 2)
                step(eng.tensor_scalar(seg_f, chunk_id[:, :], -mid_c, 1.0 / LOTS, ALU.add, ALU.mult))
                step(eng.tensor_copy(seg_i[:, :], seg_f))
                step(eng.tensor_copy(orig, seg_i[:, :]))
                step(eng.tensor_scalar(orig, orig, float(P), float(-HALF), ALU.mult, ALU.add))
                wait(eng, S["ld_e"], 16 * 3 * n_edma)
                step(eng.tensor_copy(ef[3][:, :, :], er[0][:, :, :]))
                chunks = ef[3][:, :, :].rearrange("p k (q j) -> p (k q) j", q=LOT)
                step(eng.tensor_reduce(ends[:, 0, :], chunks, AX.X, ALU.min))
                eng.tensor_reduce(ends[:, 1, :], chunks, AX.X, ALU.max).then_inc(S["ends"], 1)
                wait(eng, S["ends"], 1)
                step(eng.tensor_reduce(base, ends[:, 0, :].rearrange("p (k q) -> p k q", q=LOT), AX.X, ALU.min))
                step(eng.tensor_tensor(rel, base, orig, ALU.subtract))
                step(eng.tensor_scalar(rel, rel, 0.0, float(LIM), ALU.max, ALU.min))
                step(eng.tensor_tensor(base, rel, orig, ALU.add))
                bc = small[:, 1, :].unsqueeze(2).to_broadcast([P, KT, LE])
                step(eng.tensor_tensor(ef[2][:, :, :], ef[3][:, :, :], bc, ALU.subtract))
                step(eng.tensor_scalar(ef[1][:, :, :], er[2][:, :, :], float(WIN), None, ALU.mult))
                step(eng.tensor_tensor(ef[1][:, :, :], ef[1][:, :, :], ef[2][:, :, :], ALU.add))
                eng.tensor_scalar(ef[0][:, :, :], er[1][:, :, :], float(HALF), None, ALU.add).then_inc(S["edge"], 1)
                for li, (a, b) in enumerate(XL):
                    n_x = (a == 0) + (min(b, FULLT + 1) > max(a, 1)) + (b == T)
                    wait(eng, s_x[li], 16 * n_x)
                    for t in range(a, b):
                        last = eng.bn_stats(st6[:, t, :], xres[:, t, :])
                    last.then_inc(S["stat"], 1)
                    wait(eng, S["stat"], li + 1)
                    for t in range(a, b):
                        last = eng.bn_aggr(mv[:, t, :], st6[:, t, :])
                    last.then_inc(S["agg"], 1)
                for li, (a, b) in enumerate(XL):
                    wait(eng, S["sd"], li + 1)
                    eng.reciprocal(rs[:, a:b], rs[:, a:b]).then_inc(S["rstd"], 1)
                    wait(eng, S["rstd"], li + 1)
                    eng.scalar_tensor_tensor(nb[:, a:b], mv[:, a:b, 0], -1.0, rs[:, a:b], ALU.mult, ALU.mult).then_inc(S["nbias"], 1)

                copies = []
                for dest in (idxT[:, :], dstT, keyT[0], keyT[1]):
                    for k in range(KT):
                        d = dest[:, k * P * LOT:(k + 1) * P * LOT].rearrange("p (l q) -> p q l", q=LOT)
                        copies.append((d, ps_slot[:, len(copies) % 6, 0:LE].rearrange("p (q l) -> p q l", q=LOT)))
                copies.append((relT[:, :], ps_slot[0:KT, len(copies) % 6, 0:P]))
                for r in range(R):
                    copies.append((w0t[:, r, :, :].rearrange("p b o -> p (b o)"), ps_slot[:, len(copies) % 6, 0:NB * DF]))
                n_edge = len(copies) - R

                def copy(i):
                    wait(eng, S["etp"], i + 1)
                    ins = eng.tensor_copy(copies[i][0], copies[i][1])
                    ins.then_inc(S["ecp"], 1)
                    if i == n_edge - 1:
                        wait(eng, S["ecp"], i + 1)
                        eng.memset(small[:, 5, 0:1], 0.0).then_inc(S["rel"], 1)

                done = 0
                for t in range(T):
                    k = t % NH
                    wait(eng, S["h32"], t + 1)
                    wait(eng, S["hi"], t + 1)
                    if t >= NH:
                        wait(eng, S["mid"], t - NH + 1)
                    eng.tensor_tensor(r1[:, k, :], h32[:, k, :], hs[:, k, 0:DF], ALU.subtract).then_inc(S["r1"], 1)
                    if done < len(copies):
                        copy(done)
                        done += 1
                while done < len(copies):
                    copy(done)
                    done += 1

                wait(eng, S["ecp"], 2 * KT)
                step(eng.tensor_scalar(wid, idxT[:, :], -(P - 1) / 2.0, 1.0 / P, ALU.add, ALU.mult))
                step(eng.scalar_tensor_tensor(klo[:, :], wid, -float(P), idxT[:, :], ALU.mult, ALU.add))
                step(eng.tensor_scalar(mkey[:, :], wid, float(SUB), None, ALU.mult))
                step(eng.tensor_scalar(wid, dstT, HALF - (SUB - 1) / 2.0, 1.0 / SUB, ALU.add, ALU.mult))
                step(eng.scalar_tensor_tensor(klo[:, :], wid, float(P), klo[:, :], ALU.mult, ALU.add))
                step(eng.scalar_tensor_tensor(mkey[:, :], wid, -float(SUB), mkey[:, :], ALU.mult, ALU.add))
                step(eng.scalar_tensor_tensor(mkey[:, :], dstT, float(HALF), mkey[:, :], ALU.add, ALU.add))

                wait(eng, S["wst"], 1)
                step(eng.tensor_copy(wst[:, :], wst_i[:, :]))
                for i in range(KC):
                    last = eng.tensor_scalar(below[:, i, :], wst[:, :], ends[:, 1, i:i + 1], None, ALU.is_gt)
                last.then_inc(S["below"], 1)

                step(eng.tensor_scalar(inw[:, :, :], ef[2][:, :, :], 0.0, None, ALU.is_ge))
                step(eng.scalar_tensor_tensor(inw[:, :, :], ef[2][:, :, :], float(WIN), inw[:, :, :], ALU.is_lt, ALU.mult))
                step(eng.tensor_reduce(nbad[:, 0:1], inw[:, :, :], AX.XY, ALU.add))
                wait(eng, S["near"], 48)
                step(eng.tensor_tensor(bad[:, 0, :], near[:, 1, :], near[:, 0, :], ALU.is_lt))
                step(eng.tensor_scalar(wi[:, :, :], near[:, 0::2, :], HALF - (SUB - 1) / 2.0, 1.0 / SUB, ALU.add, ALU.mult))
                step(eng.tensor_copy(wf[:, :, :], wi[:, :, :]))
                step(eng.tensor_tensor(bad[:, 1, :], wf[:, 1, :], wf[:, 0, :], ALU.is_le))
                step(eng.scalar_tensor_tensor(bad[:, 1, :], near[:, 2, :], PAD_DST, bad[:, 1, :], ALU.is_lt, ALU.mult))
                step(eng.tensor_tensor(bad[:, 2, :], ends[:, 1, :], ends[:, 0, :], ALU.is_le))
                step(eng.scalar_tensor_tensor(bad[:, 2, :], ends[:, 0, :], PAD_DST, bad[:, 2, :], ALU.is_lt, ALU.mult))
                step(eng.tensor_reduce(nbad[:, 1:2], bad[:, :, :], AX.XY, ALU.add))
                eng.tensor_tensor(cnt_in[:, :], nbad[:, 0:1], nbad[:, 1:2], ALU.subtract).then_inc(S["inw"], 1)
                wait(eng, S["cntp"], 1)
                eng.tensor_scalar(n_inside[:, :], ps_aux[0:1, 0:1], 0.0, None, ALU.max).then_inc(S["cnt"], 1)
                wait(eng, S["subp"], 1)
                eng.tensor_copy(subr[:, :, :].rearrange("o t w -> o (t w)"), ps_proj[0:1, 0:D.nsub]).then_inc(S["subc"], 1)

            @block.tensor
            def _(eng):
                wait(eng, S["const"], 7)
                wait(eng, S["edge"], 1)
                n = 0
                for a in (0, 3, 1, 2):
                    for k in range(KT):
                        wait(eng, S["ecp"], n - 5)
                        for q in range(LOT):
                            last = eng.transpose(ps_slot[:, n % 6, q * P:(q + 1) * P], ef[a][:, k, q * P:(q + 1) * P], ident[:, :])
                        last.then_inc(S["etp"], 1)
                        n += 1
                wait(eng, S["ecp"], n - 5)
                eng.transpose(ps_slot[0:KT, n % 6, 0:P], small[:, 2, :], ident[:, :]).then_inc(S["etp"], 1)
                n += 1
                wait(eng, S["ld_w"], 16)
                for r in range(R):
                    wait(eng, S["ecp"], n - 5)
                    for ib in range(NB):
                        for ob in range(NB):
                            last = eng.transpose(ps_slot[:, n % 6, ib * DF + ob * P:ib * DF + (ob + 1) * P],
                                                 wld[:, r, ob, ib * P:(ib + 1) * P], ident[:, :])
                    last.then_inc(S["etp"], 1)
                    n += 1
                wait(eng, S["below"], 1)
                for i in range(KC):
                    last = eng.matmul(ps_proj[0:1, 0:D.nsub], ones[:, 0:1], below[:, i, :], start=(i == 0), stop=(i == KC - 1))
                last.then_inc(S["subp"], 1)
                wait(eng, S["inw"], 1)
                eng.matmul(ps_aux[0:1, 0:1], cnt_in[:, :], onec[:, :], start=True, stop=True).then_inc(S["cntp"], 1)

        def shared(layer):
            return dict(table=(table0, table1)[layer], table1=table1, out=out, idxT=idxT, key=keyT[layer], key_dst=keyT[1],
                        offr=offr, iota=iota, ones=ones, onef=onef, ident=ident, identb=identb, eps=eps, xres=xres,
                        w0t=w0t, w1s=w1s, bias0=bias0, bias1=bias1, dinv=dinv, ps_slot=ps_slot, ps_proj=ps_proj,
                        ps_aux=ps_aux, src=src, dst=dst, etype=etype, x1_d=x1_d, hs_all=hs_all, mkey=mkey, klo=klo, subr=subr)

        inside = nc.values_load(n_inside[0:1, 0:1], min_val=0, max_val=E)
        with nc.If(inside == E):
            aggregate_relations(nc, D, shared(0))
            aggregate_mixed(nc, D, shared(1))
        with nc.Else():
            for layer in (0, 1):
                aggregate_any(nc, D, layer, shared(layer))


def finishing(nc, D, layer, V, ctx, path):
    f32, bf16 = mybir.dt.float32, mybir.dt.bfloat16
    ALU, ACT = mybir.AluOpType, mybir.ActivationFunctionType
    first = layer == 0
    R = D.rel if first else 1
    NB, DF, DF3, T = D.nb, D.d, 3 * D.d, D.tiles
    xres, ps_proj, dinv = V["xres"], V["ps_proj"], V["dinv"]

    def sb(name, shape, dt):
        return ctx.enter_context(nc.sbuf_tensor(f"{name}_{path}{layer}", shape, dt))

    def sem(name):
        return ctx.enter_context(nc.semaphore(f"{path}{layer}_{name}"))

    tile_in = sb("tile_in", [P, NB, R, P], f32)
    st6 = sb("st6", [P, 6], f32)
    mv = sb("mv", [P, 2], f32)
    v2 = sb("v2", [P, 2], f32)
    r2 = sb("r2", [P, 2], f32)
    ab = sb("ab", [P, 2], f32)
    x1 = sb("x1", [P, DF], f32)
    h32 = sb("h32", [P, DF], f32)
    r1 = sb("r1", [P, DF], f32) if first else None
    hs = sb("hs", [P, DF3], bf16) if first or path == "g" else None
    y = sb("y", [P, DF], f32)
    z = sb("z", [P, DF], f32)

    s_mark = [sem(f"mark{i}") for i in range(2)]
    s_cpa = sem("copy_act")
    s_cpv = sem("copy_dve")
    s_proj = sem("proj")
    s_x1 = sem("x1")
    E = {k: sem("e_" + k) for k in ("stat", "agg", "cnt", "v2", "sd", "r2", "a", "ab", "h32", "hi", "r1",
                                    "mid", "lo", "st", "y", "z", "o", "self_mm", "deg", "xin")}

    def tile_io(eng, t, n=None):
        n = t if n is None else n
        if first:
            wait(eng, E["hi"], n + 1)
            wait(eng, E["mid"], n + 1)
            wait_alone(eng, E["lo"], n + 1, s_mark[1])
            eng.dma_start(V["table1"][bass.ds(t * P, P), :], hs[:, :]).then_inc(E["st"], 16)
            eng.dma_start(V["x1_d"][bass.ds(t * P, P), :], x1[:, :]).then_inc(E["st"], 16)
            wait_alone(eng, E["st"], 32 * (n + 1), s_mark[1])
        else:
            eng.dma_start(x1[:, :], V["x1_d"][bass.ds(t * P, P), :]).then_inc(E["xin"], 16)
            wait_alone(eng, E["z"], n + 1, s_mark[1])
            if isinstance(t, int) and t == 0:
                eng.dma_start(V["out"][0:HALF, :], z[HALF:P, :]).then_inc(E["o"], 16)
            elif isinstance(t, int) and t == T - 1:
                eng.dma_start(V["out"][D.n - D.last_rows:D.n, :], z[0:D.last_rows, :]).then_inc(E["o"], 16)
            else:
                eng.dma_start(V["out"][bass.ds(t * P - HALF, P), :], z[:, :]).then_inc(E["o"], 16)
            wait(eng, E["xin"], 16 * (n + 1))
            wait_alone(eng, E["o"], 16 * (n + 1), s_mark[1])

    def finish_act(eng, t):
        if not first:
            return
        wait(eng, E["v2"], t + 1)
        eng.activation(r2[:, :], v2[:, :], ACT.Sqrt).then_inc(E["sd"], 1)
        wait(eng, E["ab"], t + 1)
        eng.activation(h32[:, :], x1[:, :], ACT.Relu, scale=ab[:, 0:1], bias=ab[:, 1:2]).then_inc(E["h32"], 1)
        wait(eng, E["h32"], t + 1)
        wait(eng, E["st"], 32 * t)
        eng.activation(hs[:, 0:DF], h32[:, :], ACT.Copy).then_inc(E["hi"], 1)
        wait(eng, E["r1"], t + 1)
        eng.activation(hs[:, DF:2 * DF], r1[:, :], ACT.Copy).then_inc(E["mid"], 1)

    def finish_dve(eng, t, n=None):
        n = t if n is None else n
        wait(eng, s_proj, n + 1)
        if first:
            wait(eng, E["st"], 32 * t)
            eng.tensor_tensor(x1[:, :], ps_proj[:, 0:DF], xres[:, t, :], ALU.add).then_inc(s_x1, 1)
            wait(eng, s_x1, t + 1)
            eng.bn_stats(st6[:, :], x1[:, :]).then_inc(E["stat"], 1)
            wait(eng, E["deg"], t + 1)
            wait(eng, E["stat"], t + 1)
            eng.tensor_scalar(v2[:, 1:2], dinv[:, bass.ds(t, 1)], 1.0, None, ALU.add)
            eng.bn_aggr(mv[:, :], st6[:, :]).then_inc(E["agg"], 1)
            wait(eng, E["agg"], t + 1)
            eng.tensor_scalar(v2[:, 0:1], mv[:, 1:2], 1e-5, None, ALU.add).then_inc(E["v2"], 1)
            wait(eng, E["sd"], t + 1)
            eng.reciprocal(r2[:, :], r2[:, :]).then_inc(E["r2"], 1)
            wait(eng, E["r2"], t + 1)
            eng.tensor_scalar(dinv[:, bass.ds(t, 1)], r2[:, 1:2], 1.0, None, ALU.mult)
            eng.tensor_tensor(ab[:, 0:1], r2[:, 0:1], r2[:, 1:2], ALU.mult).then_inc(E["a"], 1)
            wait(eng, E["a"], t + 1)
            eng.scalar_tensor_tensor(ab[:, 1:2], mv[:, 0:1], -1.0, ab[:, 0:1], ALU.mult, ALU.mult).then_inc(E["ab"], 1)
            wait(eng, E["h32"], t + 1)
            wait(eng, E["hi"], t + 1)
            eng.tensor_tensor(r1[:, :], h32[:, :], hs[:, 0:DF], ALU.subtract).then_inc(E["r1"], 1)
            wait(eng, E["r1"], t + 1)
            wait(eng, E["mid"], t + 1)
            eng.tensor_tensor(hs[:, 2 * DF:DF3], r1[:, :], hs[:, DF:2 * DF], ALU.subtract).then_inc(E["lo"], 1)
        else:
            eng.scalar_tensor_tensor(y[:, :], ps_proj[:, 0:DF], dinv[:, bass.ds(t, 1)], V["bias1"][:, :],
                                     ALU.mult, ALU.add).then_inc(s_x1, 1)
            wait(eng, s_x1, n + 1)
            eng.scalar_tensor_tensor(h32[:, :], y[:, :], 0.2, y[:, :], ALU.mult, ALU.max).then_inc(E["y"], 1)
            wait(eng, E["y"], n + 1)
            wait(eng, E["xin"], 16 * (n + 1))
            wait(eng, E["o"], 16 * n)
            eng.tensor_tensor(z[:, :], h32[:, :], x1[:, :], ALU.add).then_inc(E["z"], 1)

    def project(eng, t, part, act_share=True):
        if part == 0:
            wait(eng, s_cpv, t + 1)
            if first and act_share:
                wait(eng, s_cpa, t + 1)
            wait(eng, s_x1, t)
        if first:
            if part == 0:
                eng.matmul(ps_proj[:, 0:DF], V["onef"][:, :], V["bias0"][:, :], start=True, stop=False)
            for r in range(part * R // 2, (part + 1) * R // 2):
                for b in range(NB):
                    last = eng.matmul(ps_proj[:, 0:DF], tile_in[:, b, r, :], V["w0t"][:, r, b, :], start=False,
                                      stop=(r == R - 1 and b == NB - 1))
        else:
            last = eng.matmul(ps_proj[:, 0:DF], tile_in[:, part, 0, :], V["w1s"][:, part, :],
                              start=(part == 0), stop=(part == 1))
        if part == 1:
            last.then_inc(s_proj, 1)

    return dict(tile_in=tile_in, hs=hs, E=E, s_proj=s_proj, s_x1=s_x1, s_cpv=s_cpv, s_cpa=s_cpa, s_mark=s_mark,
                tile_io=tile_io, finish_act=finish_act, finish_dve=finish_dve, project=project)


def aggregate_relations(nc, D, V):
    f32, bf16, i32 = mybir.dt.float32, mybir.dt.bfloat16, mybir.dt.int32
    ALU, ACT, AX = mybir.AluOpType, mybir.ActivationFunctionType, mybir.AxisListType
    layer = 0
    R = D.rel
    NQ = D.nb * R + 1
    AQ = R
    NB, DF, DF3, T, CPS, SEGS = D.nb, D.d, 3 * D.d, D.tiles, D.cps, D.segs
    W = R * WIN
    LIM = 2 * P
    AW = LIM + WIN
    idxT, key, offr, iota, ps_slot, ps_aux, dinv = (V[k] for k in ("idxT", "key", "offr", "iota", "ps_slot", "ps_aux", "dinv"))

    with ExitStack() as ctx:
        def sb(name, shape, dt):
            return ctx.enter_context(nc.sbuf_tensor(f"{name}_{layer}", shape, dt))

        def sem(name):
            return ctx.enter_context(nc.semaphore(f"s{layer}_{name}"))

        acc = sb("acc", [P, NQ, AW], f32)
        onehot = sb("onehot", [P, CPS, W], bf16)
        onedst = sb("onedst", [P, CPS, WIN], bf16)
        rows = sb("rows", [P, CPS, DF3], bf16)
        stage = sb("stage", [P, CPS], i32)
        scr = sb("scr", [P, P], f32)
        F = finishing(nc, D, layer, V, ctx, "s")
        tile_in, hs, E, s_proj, s_x1, s_cpv, s_cpa, s_mark = (
            F[k] for k in ("tile_in", "hs", "E", "s_proj", "s_x1", "s_cpv", "s_cpa", "s_mark"))

        s_zero = sem("zero")
        s_stage = sem("stage")
        s_rows = [sem(f"rows{g}") for g in range(3)]
        s_oh = sem("onehot")
        s_pe = sem("lot")
        s_acc = sem("acc")
        s_sha = sem("shift_act")
        s_shv = sem("shift_dve")
        s_tla = sem("tail_act")
        s_tlv = sem("tail_dve")
        s_bnd = sem("boundary")
        s_bndv = sem("boundary_dve")
        def chunks_of(g):
            return range(LOT * GROUPS[g][0], LOT * GROUPS[g][1])

        def last_use(j):
            return j - NBANK if j >= NBANK else max(k for k in range(LOTS) if k % NBANK == j) - LOTS

        block = ctx.enter_context(nc.Block())

        @block.gpsimd
        def _(eng):
            def body(s):
                for g in range(3):
                    wait_alone(eng, s_stage, s * 3 + g + 1, s_mark[0])
                    for c in chunks_of(g):
                        eng.indirect_dma_start(rows[:, c, :], None, V["table"],
                                               bass.IndirectOffsetOnAxis(ap=stage[:, c:c + 1], axis=0)).then_inc(s_rows[g], 16)
            body(0)
            body(1)
            with eng.Fori(2, SEGS) as s:
                body(s)

        @block.sync
        def _(eng):
            F["tile_io"](eng, 0)
            with eng.Fori(2, SEGS) as s:
                F["tile_io"](eng, s - 1)
            F["tile_io"](eng, T - 2)
            F["tile_io"](eng, T - 1)

        @block.scalar
        def _(eng):
            def put_stage(s, g):
                wait(eng, s_pe, (s - 1) * LOTS + GROUPS[g][1])
                r = chunks_of(g)
                eng.activation(stage[:, r.start:r.stop], idxT[:, bass.ds(s * CPS + r.start, len(r))], ACT.Copy).then_inc(s_stage, 1)

            def boundary(s):
                wait(eng, s_acc, (s + 1) * LOTS)
                wait(eng, s_proj, s)
                eng.activation(tile_in[:, 0, :, :], acc[:, 0:AQ, 0:P], ACT.Copy).then_inc(s_cpa, 1)
                wait(eng, s_cpa, s + 1)
                eng.activation(acc[:, 0:AQ, 0:P], acc[:, 0:AQ, P:LIM], ACT.Copy).then_inc(s_sha, 1)
                wait(eng, s_sha, s + 1)
                eng.activation(acc[:, 0:AQ, P:P + WIN], acc[:, 0:AQ, LIM:AW], ACT.Copy).then_inc(s_tla, 1)
                wait(eng, s_tla, s + 1)
                eng.activation(acc[:, 0:AQ, P + WIN:AW], V["ident"][:, 0:1].unsqueeze(1).to_broadcast([P, R, P]), ACT.Copy,
                               scale=0.0).then_inc(s_bnd, 1)

            def body(s):
                put_stage(s + 1, 0)
                put_stage(s + 1, 1)
                put_stage(s + 1, 2)
                boundary(s)
                if not (isinstance(s, int) and s == 0):
                    F["finish_act"](eng, s - 1)

            for g in range(3):
                put_stage(0, g)
            body(0)
            body(1)
            with eng.Fori(2, SEGS) as s:
                body(s)
            F["finish_act"](eng, T - 2)
            F["finish_act"](eng, T - 1)

        @block.vector
        def _(eng):
            def build_onehot(s, g):
                wait(eng, s_pe, (s - 1) * LOTS + GROUPS[g][1])
                r = chunks_of(g)
                last = None
                for hot, keys, w in ((onehot, key, W), (onedst, V["key_dst"], WIN)):
                    if hot is not None:
                        k = keys[:, bass.ds(s * CPS + r.start, len(r))]
                        last = eng.tensor_tensor(hot[:, r.start:r.stop, :], iota[:, 0:w].unsqueeze(1).to_broadcast([P, len(r), w]),
                                                 k.unsqueeze(2).to_broadcast([P, len(r), w]), ALU.is_equal)
                last.then_inc(s_oh, 1)

            def starts(s):
                return nc.values_load_multi_w_load_instructions(
                    offr[0:1, s, 0:LOTS], engines=(mybir.EngineType.DVE,), min_val=0, max_val=LIM,
                    skip_runtime_bounds_check_because="the window starts are clamped to 0..LIM when they are computed")[1]

            def accumulate(s, g, off):
                for j in range(*GROUPS[g]):
                    c = s * LOTS + j
                    wait(eng, s_pe, c + 1)
                    wait(eng, s_acc, c)
                    win = acc[:, :, bass.ds(off[j], WIN)]
                    part = ps_slot[:, j % NBANK, 0:NQ * WIN].rearrange("p (q w) -> p q w", w=WIN)
                    eng.tensor_tensor(win, part, win, ALU.add).then_inc(s_acc, 1)

            def boundary(s, shift=True):
                wait(eng, s_acc, (s + 1) * LOTS if shift else SEGS * LOTS)
                wait(eng, s_proj, s)
                own = slice(AQ if shift else 0, NQ)
                eng.tensor_tensor(scr[:, :], acc[:, NQ - 1, 0:P], V["ident"][:, :], ALU.mult).then_inc(E["cnt"], 1)
                b0 = 1 if shift else 0
                eng.tensor_copy(tile_in[:, b0:NB, :, :].rearrange("p b r w -> p (b r) w"), acc[:, b0 * R:NB * R, 0:P]).then_inc(s_cpv, 1)
                wait(eng, E["cnt"], s + 1)
                eng.tensor_reduce(dinv[:, bass.ds(s, 1)], scr[:, :], AX.X, ALU.add).then_inc(E["deg"], 1)
                if shift:
                    wait(eng, s_cpv, s + 1)
                    eng.tensor_copy(acc[:, own, 0:P], acc[:, own, P:LIM]).then_inc(s_shv, 1)
                    wait(eng, s_shv, s + 1)
                    eng.tensor_copy(acc[:, own, P:P + WIN], acc[:, own, LIM:AW]).then_inc(s_tlv, 1)
                    wait(eng, s_tlv, s + 1)
                    eng.memset(acc[:, own, P + WIN:AW], 0.0).then_inc(s_bndv, 1)

            def body(s):
                off = starts(s)
                for g in range(3):
                    build_onehot(s + (g + 1) // 3, (g + 1) % 3)
                    if g == 0:
                        wait(eng, s_zero, 1)
                        wait(eng, s_bnd, s)
                        wait(eng, s_bndv, s)
                    accumulate(s, g, off)
                boundary(s)
                if not (isinstance(s, int) and s == 0):
                    F["finish_dve"](eng, s - 1)

            eng.memset(acc[:, :, :], 0.0).then_inc(s_zero, 1)
            build_onehot(0, 0)
            body(0)
            body(1)
            with eng.Fori(2, SEGS) as s:
                body(s)
            F["finish_dve"](eng, T - 2)
            wait(eng, s_bnd, SEGS)
            wait(eng, s_bndv, SEGS)
            boundary(T - 1, shift=False)
            F["finish_dve"](eng, T - 1)

        @block.tensor
        def _(eng):
            def group(s, g):
                wait(eng, s_rows[g], (s + 1) * (16 * len(chunks_of(g))))
                wait(eng, s_oh, s * 3 + g + 1)
                for j in range(*GROUPS[g]):
                    wait(eng, s_acc, s * LOTS + last_use(j) + 1)
                    o = ps_slot[:, j % NBANK, :]
                    lot = range(j * LOT, (j + 1) * LOT)
                    for b in range(NB):
                        for c in lot:
                            for p in range(3):
                                last = eng.matmul(o[:, b * W:(b + 1) * W], rows[:, c, p * DF + b * P:p * DF + (b + 1) * P],
                                                  onehot[:, c, :], start=(c == lot[0] and p == 0), stop=(c == lot[-1] and p == 2))
                    for c in lot:
                        last = eng.matmul(o[:, NB * W:NB * W + WIN], V["ones"][:, :], onedst[:, c, :],
                                          start=(c == lot[0]), stop=(c == lot[-1]))
                    last.then_inc(s_pe, 1)

            def body(s):
                for g in range(3):
                    group(s, g)
                    if g < 2 and not (isinstance(s, int) and s == 0):
                        F["project"](eng, s - 1, g)

            body(0)
            body(1)
            with eng.Fori(2, SEGS) as s:
                body(s)
            for t in (T - 2, T - 1):
                F["project"](eng, t, 0, act_share=t < T - 1)
                F["project"](eng, t, 1)


def aggregate_mixed(nc, D, V):
    f32, bf16, f16, i32 = mybir.dt.float32, mybir.dt.bfloat16, mybir.dt.float16, mybir.dt.int32
    ALU, ACT = mybir.AluOpType, mybir.ActivationFunctionType
    NB, DF, DF3, T, CPS, TG = D.nb, D.d, 3 * D.d, D.tiles, D.cps, D.tg
    assert D.td == TG and TG >= 4
    LIM = 2 * P
    AW = LIM + WIN
    NW = P // SUB
    MW = T * SUB
    COUNT_BANKS = (NBANK1, NBANK1 + 1)
    SUM_BANK = NBANK1 + 2
    idxT, key, offr, iota, ps_slot, ps_aux, hs_all = (
        V[k] for k in ("idxT", "key", "offr", "iota", "ps_slot", "ps_aux", "hs_all"))

    with ExitStack() as ctx:
        def sb(name, shape, dt):
            return ctx.enter_context(nc.sbuf_tensor(f"{name}_1", shape, dt))

        def sem(name):
            return ctx.enter_context(nc.semaphore(f"s1_{name}"))

        acc = sb("acc", [P, NB, AW], f32)
        onehot = sb("onehot", [P, CPS, WIN], bf16)
        rows = sb("rows", [P, CPS, DF3], bf16)
        stage = sb("stage", [P, CPS], i32)
        iota_m = sb("iota_m", [P, MW], f16)
        kk = sb("kk", [P, D.nsub], f32)
        hot_lo = sb("hot_lo", [P, 2, SPAN, P], bf16)
        hot_m = sb("hot_m", [P, 2, SPAN, MW], bf16)
        counts = [sb(f"counts{i}", [P, T, P], bf16) for i in range(2)]
        dsum = sb("dsum", [P, DF], f32)
        F = finishing(nc, D, 1, V, ctx, "s")
        tile_in, E, s_proj, s_cpv, s_mark = (F[k] for k in ("tile_in", "E", "s_proj", "s_cpv", "s_mark"))

        s_zero = sem("zero")
        s_iota = sem("iota")
        s_all = [sem("all0"), sem("all")]
        s_stage = sem("stage")
        s_rows = [sem(f"rows{g}") for g in range(3)]
        s_oh = sem("onehot")
        s_pe = sem("lot")
        s_acc = sem("acc")
        s_shv = sem("shift_dve")
        s_tlv = sem("tail_dve")
        s_bndv = sem("boundary_dve")
        s_hot = sem("hot")
        s_cnt = sem("counted")
        s_ev = sem("evacuated")
        s_sum = sem("dense_sum")
        s_ds = sem("dsum")
        s_dt = sem("dsum_t")

        def chunks_of(g):
            return range(LOT * GROUPS[g][0], LOT * GROUPS[g][1])

        def last_use(j):
            return j - NBANK1 if j >= NBANK1 else max(k for k in range(LOTS) if k % NBANK1 == j) - LOTS

        def at_least(s, k):
            return not isinstance(s, int) or s >= k

        def steps(body, eng):
            body(0, 0)
            body(1, 1)
            pairs = (TG - 2) // 2
            with eng.Fori(2, 2 + 2 * pairs, 2) as s:
                body(s, 0)
                body(s + 1, 1)
            if (TG - 2) % 2:
                body(TG - 1, (TG - 1) % 2)

        def gathered(s):
            return s - 1, (2 * s - 3 if at_least(s, 2) else 0)

        def dense(s):
            return TG + s - 2, (2 * TG - 1 if isinstance(s, int) and s > TG else 2 * s - 2)

        ALL = [(a, min(a + 10, T)) for a in range(0, T, 10)]
        AFTER = {NW // 3: 0, 2 * NW // 3: 1, NW - 1: 2}
        block = ctx.enter_context(nc.Block())

        @block.gpsimd
        def _(eng):
            eng.iota(iota_m[:, :], [[1, MW]], base=0, channel_multiplier=0,
                     allow_small_or_imprecise_dtypes=True).then_inc(s_iota, 1)
            eng.iota(kk[:, :], [[P, D.nsub]], base=TG * NW * P, channel_multiplier=0,
                     allow_small_or_imprecise_dtypes=True).then_inc(s_iota, 1)

            def body(s, _):
                for g in range(3):
                    wait_alone(eng, s_stage, s * 3 + g + 1, s_mark[0])
                    for c in chunks_of(g):
                        eng.indirect_dma_start(rows[:, c, :], None, V["table"],
                                               bass.IndirectOffsetOnAxis(ap=stage[:, c:c + 1], axis=0)).then_inc(s_rows[g], 16)
            steps(body, eng)

        @block.sync
        def _(eng):
            for a, b in ALL:
                eng.dma_start(hs_all[:, a:b, :], V["table"][a * P:b * P, :].rearrange("(t p) d -> p t d", p=P)).then_inc(s_all[min(a, 1)], 16)
            F["tile_io"](eng, 0, 0)
            with eng.Fori(2, TG) as s:
                F["tile_io"](eng, *gathered(s))
                F["tile_io"](eng, *dense(s))
            F["tile_io"](eng, *gathered(TG))
            F["tile_io"](eng, *dense(TG))
            F["tile_io"](eng, *dense(TG + 1))

        @block.scalar
        def _(eng):
            def put_stage(s, g):
                wait(eng, s_pe, (s - 1) * LOTS + GROUPS[g][1])
                r = chunks_of(g)
                eng.activation(stage[:, r.start:r.stop], idxT[:, bass.ds(s * CPS + r.start, len(r))], ACT.Copy).then_inc(s_stage, 1)

            def copy_sum(s):
                wait(eng, s_sum, s - 1)
                wait(eng, s_dt, s - 1)
                eng.activation(dsum[:, :], ps_slot[:, SUM_BANK, 0:DF], ACT.Copy).then_inc(s_ds, 1)

            def body(s, buf):
                if at_least(s, 2):
                    copy_sum(s)
                for w in range(NW):
                    if w == 0:
                        wait(eng, s_sum, s - 1)
                    wait(eng, s_cnt, s * NW + w + 1)
                    eng.activation(counts[buf][:, :, w * SUB:(w + 1) * SUB],
                                   ps_slot[:, COUNT_BANKS[w % 2], 0:MW].rearrange("p (t d) -> p t d", d=SUB), ACT.Copy).then_inc(s_ev, 1)
                    if w in AFTER:
                        put_stage(s + 1, AFTER[w])

            for g in range(3):
                put_stage(0, g)
            steps(body, eng)
            copy_sum(TG)
            copy_sum(TG + 1)

        @block.vector
        def _(eng):
            def build_onehot(s, g):
                wait(eng, s_pe, (s - 1) * LOTS + GROUPS[g][1])
                r = chunks_of(g)
                k = key[:, bass.ds(s * CPS + r.start, len(r))]
                eng.tensor_tensor(onehot[:, r.start:r.stop, :], iota[:, 0:WIN].unsqueeze(1).to_broadcast([P, len(r), WIN]),
                                  k.unsqueeze(2).to_broadcast([P, len(r), WIN]), ALU.is_equal).then_inc(s_oh, 1)

            def values(a, most, why):
                return nc.values_load_multi_w_load_instructions(
                    a, engines=(mybir.EngineType.DVE,), min_val=0, max_val=most, skip_runtime_bounds_check_because=why)[1]

            def accumulate(s, g, off):
                for i, j in enumerate(range(*GROUPS[g])):
                    c = s * LOTS + j
                    wait(eng, s_pe, c + 1)
                    wait(eng, s_acc, c)
                    win = acc[:, :, bass.ds(off[i], WIN)]
                    part = ps_slot[:, j % NBANK1, 0:NB * WIN].rearrange("p (q w) -> p q w", w=WIN)
                    eng.tensor_tensor(win, part, win, ALU.add).then_inc(s_acc, 1)

            def build_hot(s, w, first_chunk):
                wait(eng, s_cnt, s * NW + w - 1)
                for j in range(SPAN):
                    eng.tensor_scalar(hot_lo[:, w % 2, j, :], iota[:, :], kk[:, bass.ds(s * NW + w, 1)],
                                      V["klo"][:, bass.ds(first_chunk + j, 1)], ALU.add, ALU.is_equal)
                    last = eng.tensor_scalar(hot_m[:, w % 2, j, :], iota_m[:, :], V["mkey"][:, bass.ds(first_chunk + j, 1)], None,
                                             ALU.is_equal)
                last.then_inc(s_hot, 1)

            def boundary(s, n):
                wait(eng, s_acc, (s + 1) * LOTS)
                wait(eng, s_proj, n)
                wait(eng, E["self_mm"], s + 1)
                eng.tensor_tensor(tile_in[:, :, 0, :], acc[:, :, 0:P],
                                  ps_aux[:, 0:NB * P].rearrange("p (b w) -> p b w", b=NB), ALU.add).then_inc(s_cpv, 1)
                wait(eng, s_cpv, n + 1)
                eng.tensor_copy(acc[:, :, 0:P], acc[:, :, P:LIM]).then_inc(s_shv, 1)
                wait(eng, s_shv, s + 1)
                eng.tensor_copy(acc[:, :, P:P + WIN], acc[:, :, LIM:AW]).then_inc(s_tlv, 1)
                wait(eng, s_tlv, s + 1)
                eng.memset(acc[:, :, P + WIN:AW], 0.0).then_inc(s_bndv, 1)

            def take_dense(s):
                t, n = dense(s)
                wait(eng, s_proj, n)
                wait(eng, s_dt, s)
                eng.tensor_copy(tile_in[:, :, 0, :], ps_aux[:, 0:NB * P].rearrange("p (b w) -> p b w", b=NB)).then_inc(s_cpv, 1)

            def body(s, _):
                for w in range(NW):
                    if w % 4 == 0:
                        firsts = values(V["subr"][0:1, s, w:w + 4], D.chunks, "counts of chunks")
                    build_hot(s, w, firsts[w % 4])
                    if w == 1 and at_least(s, 1):
                        F["finish_dve"](eng, *gathered(s))
                    if w == 3 and at_least(s, 2):
                        take_dense(s)
                    if w == 5 and at_least(s, 2):
                        F["finish_dve"](eng, *dense(s))
                    for g in range(3):
                        if w == min({v: k for k, v in AFTER.items()}[g] + 1, NW - 1):
                            build_onehot(s + (g + 1) // 3, (g + 1) % 3)
                            if g == 0:
                                wait(eng, s_bndv, s)
                            off = values(offr[0:1, s, GROUPS[g][0]:GROUPS[g][1]], LIM, "the window starts are clamped to 0..LIM")
                            accumulate(s, g, off)
                boundary(s, 2 * s - 1 if at_least(s, 1) else 0)

            eng.memset(acc[:, :, :], 0.0).then_inc(s_zero, 1)
            wait(eng, s_zero, 1)
            wait(eng, s_iota, 2)
            build_onehot(0, 0)
            steps(body, eng)
            F["finish_dve"](eng, *gathered(TG))
            for s in (TG, TG + 1):
                take_dense(s)
                F["finish_dve"](eng, *dense(s))

        @block.tensor
        def _(eng):
            def self_rows(s, buf):
                if not at_least(s, 1):
                    wait(eng, s_all[0], 16)
                    wait(eng, s_all[1], 16 * (len(ALL) - 1))
                wait(eng, s_cpv, (2 * s - 1) if at_least(s, 2) else s)
                for b in range(NB):
                    for p in range(3):
                        last = eng.matmul(ps_aux[:, b * P:(b + 1) * P], hs_all[:, s, p * DF + b * P:p * DF + (b + 1) * P],
                                          V["identb"][:, :], start=(p == 0), stop=(p == 2))
                last.then_inc(E["self_mm"], 1)

            def group(s, g):
                wait(eng, s_rows[g], (s + 1) * (16 * len(chunks_of(g))))
                wait(eng, s_oh, s * 3 + g + 1)
                for j in range(*GROUPS[g]):
                    wait(eng, s_acc, s * LOTS + last_use(j) + 1)
                    o = ps_slot[:, j % NBANK1, :]
                    lot = range(j * LOT, (j + 1) * LOT)
                    for b in range(NB):
                        for c in lot:
                            for p in range(3):
                                last = eng.matmul(o[:, b * WIN:(b + 1) * WIN], rows[:, c, p * DF + b * P:p * DF + (b + 1) * P],
                                                  onehot[:, c, :], start=(c == lot[0] and p == 0), stop=(c == lot[-1] and p == 2))
                    last.then_inc(s_pe, 1)

            def count(s, w):
                wait(eng, s_hot, s * NW + w + 1)
                wait(eng, s_ev, s * NW + w - 1)
                for j in range(SPAN):
                    last = eng.matmul(ps_slot[:, COUNT_BANKS[w % 2], 0:MW], hot_lo[:, w % 2, j, :], hot_m[:, w % 2, j, :],
                                      start=(j == 0), stop=(j == SPAN - 1))
                last.then_inc(s_cnt, 1)

            def multiply(s, buf, w):
                if w == 0:
                    wait(eng, s_ev, s * NW)
                    wait(eng, s_ds, s - 1)
                o = ps_slot[:, SUM_BANK, 0:DF]
                for t in range(w * T // NW, (w + 1) * T // NW):
                    for p in range(3):
                        eng.matmul(o, counts[1 - buf][:, t, :], hs_all[:, t, p * DF:(p + 1) * DF], start=(t == 0 and p == 0), stop=False)
                if w == NW - 1:
                    for p in range(3):
                        last = eng.matmul(o, V["identb"][:, :], hs_all[:, TG + s - 1, p * DF:(p + 1) * DF], start=False, stop=(p == 2))
                    last.then_inc(s_sum, 1)

            def project(n):
                for part in range(NB):
                    F["project"](eng, n, part)

            def transpose_sum(s):
                wait(eng, s_ds, s - 1)
                wait(eng, s_cpv, dense(s)[1])
                for b in range(NB):
                    last = eng.transpose(ps_aux[:, b * P:(b + 1) * P], dsum[:, b * P:(b + 1) * P], V["ident"][:, :])
                last.then_inc(s_dt, 1)

            def body(s, buf):
                for w in range(NW):
                    count(s, w)
                    if w == 0 and at_least(s, 1):
                        project(gathered(s)[1])
                    if w == 1 and at_least(s, 2):
                        transpose_sum(s)
                    if at_least(s, 1):
                        multiply(s, buf, w)
                    if w == 4 and at_least(s, 2):
                        project(dense(s)[1])
                    if w == 5:
                        self_rows(s, buf)
                    if w in AFTER:
                        group(s, AFTER[w])

            eng.sem_inc(s_dt, 1)
            steps(body, eng)
            project(gathered(TG)[1])
            transpose_sum(TG)
            for w in range(NW):
                multiply(TG, TG % 2, w)
            project(dense(TG)[1])
            transpose_sum(TG + 1)
            project(dense(TG + 1)[1])


def aggregate_any(nc, D, layer, V):
    f32, bf16, i32 = mybir.dt.float32, mybir.dt.bfloat16, mybir.dt.int32
    ALU, AX = mybir.AluOpType, mybir.AxisListType
    first = layer == 0
    R = D.rel if first else 1
    NB, DF, DF3, T, E_, CH = D.nb, D.d, 3 * D.d, D.tiles, D.e, D.chunks
    SW = DF + 4
    NROW = T * P * R
    idxT, ps_slot, ps_aux, dinv, ident = (V[k] for k in ("idxT", "ps_slot", "ps_aux", "dinv", "ident"))
    sums = nc.dram_tensor(f"sums{layer}", (NROW, SW), f32).ap()
    dst_p = nc.dram_tensor(f"dst_p{layer}", (CH * P,), i32).ap()
    typ_p = nc.dram_tensor(f"typ_p{layer}", (CH * P,), i32).ap()
    pad = CH * P - E_

    with ExitStack() as ctx:
        def sb(name, shape, dt):
            return ctx.enter_context(nc.sbuf_tensor(f"{name}_a{layer}", shape, dt))

        def sem(name):
            return ctx.enter_context(nc.semaphore(f"a{layer}_{name}"))

        F = finishing(nc, D, layer, V, ctx, "g")
        tile_in, hs, E = F["tile_in"], F["hs"], F["E"]
        padt = sb("padt", [1, 2, P], i32)
        tri = sb("tri", [P, P], f32)
        drow, trow = sb("drow", [P, P], i32), sb("trow", [P, P], i32)
        dcol, tcol = sb("dcol", [P, 1], i32), sb("tcol", [P, 1], i32)
        krow, same, dup = sb("krow", [P, P], f32), sb("same", [P, P], f32), sb("dup", [P, P], f32)
        kcol, ndup, wcol = sb("kcol", [P, 1], f32), sb("ndup", [P, 1], f32), sb("wcol", [P, 1], f32)
        idx, kidx, widx = sb("idx", [P, 1], i32), sb("kidx", [P, 1], i32), sb("widx", [P, 1], i32)
        grow = sb("grow", [P, DF3], bf16)
        vals, old = sb("vals", [P, SW], f32), sb("old", [P, SW], f32)
        big = sb("big", [P, R, SW], f32)
        selff = sb("selff", [P, DF], f32)

        s_c = sem("const")
        s_ch = sem("chain")
        s_pad, s_zero, s_copy = sem("pad"), sem("zero"), sem("copy")
        s_ld, s_idx, s_kidx, s_row, s_old = sem("ld"), sem("idx"), sem("kidx"), sem("row"), sem("old")
        s_vals, s_mm, s_new, s_put = sem("vals"), sem("mm"), sem("new"), sem("put")
        s_big, s_self, s_tp, s_tc, s_free = sem("big"), sem("self"), sem("tp"), sem("tc"), sem("free")
        SETUP, STEPS, TSTEPS = 4, 12 if first else 10, 0

        def chunks(body, eng):
            body(0)
            with eng.Fori(1, CH) as c:
                body(c)

        def tiles(body, eng):
            body(0)
            with eng.Fori(1, T - 1) as t:
                body(t)
            body(T - 1)

        with nc.Block() as block:
            @block.gpsimd
            def _(eng):
                eng.memset(tri[:, :], 1.0).then_inc(s_c, 1)
                wait(eng, s_c, 1)
                eng.affine_select(out=tri[:, :], in_=tri[:, :], compare_op=ALU.is_gt, fill=0.0, base=0,
                                  pattern=[[-1, P]], channel_multiplier=1).then_inc(s_c, 1)
                wait(eng, s_zero, 16 * T)
                wait(eng, s_ch, SETUP)

                def body(c):
                    wait_alone(eng, s_idx, c + 1, F["s_mark"][0])
                    eng.indirect_dma_start(grow[:, :], None, V["table"], bass.IndirectOffsetOnAxis(ap=idx[:, 0:1], axis=0)).then_inc(s_row, 16)
                    if not isinstance(c, int) or c > 0:
                        wait_alone(eng, s_put, 16 * c, F["s_mark"][0])
                    wait_alone(eng, s_kidx, c + 1, F["s_mark"][0])
                    eng.indirect_dma_start(old[:, :], None, sums, bass.IndirectOffsetOnAxis(ap=kidx[:, 0:1], axis=0),
                                           bounds_check=NROW - 1, oob_is_err=False).then_inc(s_old, 16)
                    wait_alone(eng, s_new, c + 1, F["s_mark"][0])
                    eng.indirect_dma_start(sums, bass.IndirectOffsetOnAxis(ap=widx[:, 0:1], axis=0), old[:, :], None,
                                           bounds_check=NROW - 1, oob_is_err=False).then_inc(s_put, 16)
                chunks(body, eng)
                wait(eng, s_put, 16 * CH)

            @block.sync
            def _(eng):
                wait(eng, s_ch, SETUP)
                for i, (a, b) in enumerate(((V["dst"], dst_p), (V["etype"], typ_p))):
                    eng.dma_start(b[0:E_], a).then_inc(s_copy, 16)
                    eng.dma_start(b[E_:CH * P].rearrange("(o p) -> o p", o=1), padt[:, i, 0:pad]).then_inc(s_copy, 16)
                with eng.Fori(0, T) as t:
                    eng.dma_start(sums[bass.ds(t * (P * R), P * R), :].rearrange("(p r) w -> p (r w)", r=R),
                                  big[:, :, :].rearrange("p r w -> p (r w)")).then_inc(s_zero, 16)
                wait(eng, s_zero, 16 * T)
                wait(eng, s_copy, 64)

                def body(c):
                    if not isinstance(c, int) or c > 0:
                        wait(eng, s_ld, 64 * c)
                        wait_alone(eng, s_new, c, F["s_mark"][1])
                    for a, row, col in ((dst_p, drow, dcol), (typ_p, trow, tcol)):
                        part = a[bass.ds(c * P, P)]
                        eng.dma_start(row[:, :], part.rearrange("(o p) -> o p", o=1).to_broadcast([P, P])).then_inc(s_ld, 16)
                        eng.dma_start(col[:, :], part.rearrange("(p o) -> p o", o=1)).then_inc(s_ld, 16)
                chunks(body, eng)
                wait(eng, s_ld, 64 * CH)

            @block.vector
            def _(eng):
                n = [0]

                def step(ins, at=0):
                    n[0] += 1
                    ins.then_inc(s_ch, 1)
                    wait(eng, s_ch, at + n[0])

                step(eng.memset(big[:, :, :], 0.0))
                step(eng.memset(padt[:, 0, :], int(PAD_DST)))
                step(eng.memset(padt[:, 1, :], 0))
                eng.memset(vals[:, DF + 1:SW], 0.0)
                eng.memset(vals[:, DF:DF + 1], 1.0)
                step(eng.memset(old[:, :], 0.0))
                assert n[0] == SETUP
                wait(eng, s_c, 2)

                def body(c):
                    n[0] = 0
                    at = SETUP + c * STEPS
                    wait(eng, s_row, 16 * c)
                    eng.tensor_scalar(idx[:, :], idxT[:, bass.ds(c, 1)], 1.0, None, ALU.mult).then_inc(s_idx, 1)
                    wait(eng, s_ld, 64 * (c + 1))
                    step(eng.tensor_scalar(krow[:, :], drow[:, :], float(R), None, ALU.mult), at)
                    step(eng.tensor_scalar(kcol[:, :], dcol[:, :], float(R), None, ALU.mult), at)
                    if first:
                        step(eng.tensor_tensor(krow[:, :], krow[:, :], trow[:, :], ALU.add), at)
                        step(eng.tensor_tensor(kcol[:, :], kcol[:, :], tcol[:, :], ALU.add), at)
                    wait(eng, s_put, 16 * c)
                    eng.tensor_scalar(kidx[:, :], kcol[:, :], float(HALF * R), None, ALU.add).then_inc(s_kidx, 1)
                    step(eng.tensor_scalar(same[:, :], krow[:, :], kcol[:, :], None, ALU.is_equal), at)
                    step(eng.tensor_tensor(dup[:, :], same[:, :], tri[:, :], ALU.mult), at)
                    step(eng.tensor_reduce(ndup[:, :], dup[:, :], AX.X, ALU.add), at)
                    step(eng.tensor_scalar(ndup[:, :], ndup[:, :], 1.0, 4e6, ALU.min, ALU.mult), at)
                    step(eng.scalar_tensor_tensor(wcol[:, :], kcol[:, :], float(HALF * R), ndup[:, :], ALU.add, ALU.add), at)
                    step(eng.tensor_copy(widx[:, :], wcol[:, :]), at)
                    wait(eng, s_row, 16 * (c + 1))
                    step(eng.tensor_tensor(vals[:, 0:DF], grow[:, 0:DF], grow[:, DF:2 * DF], ALU.add), at)
                    step(eng.tensor_tensor(vals[:, 0:DF], vals[:, 0:DF], grow[:, 2 * DF:DF3], ALU.add), at)
                    assert n[0] == STEPS
                    eng.sem_inc(s_vals, 1)
                    wait(eng, s_old, 16 * (c + 1))
                    wait(eng, s_mm, c + 1)
                    eng.tensor_tensor(old[:, :], ps_aux[:, 0:SW], old[:, :], ALU.add).then_inc(s_new, 1)
                chunks(body, eng)

            @block.tensor
            def _(eng):
                def body(c):
                    wait(eng, s_vals, c + 1)
                    eng.matmul(ps_aux[:, 0:SW], same[:, :], vals[:, :], start=True, stop=True).then_inc(s_mm, 1)
                chunks(body, eng)

        with nc.Block() as block:
            @block.sync
            def _(eng):
                def body(t):
                    wait_alone(eng, s_free, t + 1, F["s_mark"][1])
                    eng.dma_start(big[:, :, :].rearrange("p r w -> p (r w)"),
                                  sums[bass.ds(t * (P * R), P * R), :].rearrange("(p r) w -> p (r w)", r=R)).then_inc(s_big, 16)
                    if not first:
                        eng.dma_start(hs[:, :], V["table"][bass.ds(t * P, P), :]).then_inc(s_self, 16)
                    F["tile_io"](eng, t)
                tiles(body, eng)
                wait(eng, s_big, 16 * T)
                if not first:
                    wait(eng, s_self, 16 * T)

            @block.tensor
            def _(eng):
                def body(t):
                    wait(eng, s_new, CH + 1 + t)
                    for i in range(R * NB):
                        r, b = divmod(i, NB)
                        last = eng.transpose(ps_slot[:, i // 4, (i % 4) * P:(i % 4 + 1) * P], big[:, r, b * P:(b + 1) * P], ident[:, :])
                    last.then_inc(s_tp, 1)
                    for part in range(2):
                        F["project"](eng, t, part, act_share=False)
                tiles(body, eng)

            @block.scalar
            def _(eng):
                tiles(lambda t: F["finish_act"](eng, t), eng)

            @block.vector
            def _(eng):
                eng.sem_inc(s_free, 1)

                def body(t):
                    wait(eng, s_big, 16 * (t + 1))
                    if first:
                        eng.tensor_reduce(dinv[:, bass.ds(t, 1)], big[:, :, DF], AX.X, ALU.add).then_inc(E["deg"], 1)
                        eng.sem_inc(s_new, 1)
                    else:
                        wait(eng, s_self, 16 * (t + 1))
                        eng.tensor_tensor(selff[:, :], hs[:, 0:DF], hs[:, DF:2 * DF], ALU.add).then_inc(E["cnt"], 1)
                        wait(eng, E["cnt"], t + 1)
                        eng.tensor_tensor(selff[:, :], selff[:, :], hs[:, 2 * DF:DF3], ALU.add).then_inc(E["stat"], 1)
                        wait(eng, E["stat"], t + 1)
                        eng.tensor_tensor(big[:, 0, 0:DF], big[:, 0, 0:DF], selff[:, :], ALU.add).then_inc(s_new, 1)
                    wait(eng, s_tp, t + 1)
                    tin = tile_in[:, :, :, :].rearrange("p b r w -> p r b w")
                    per = 4 // NB
                    for q in range(-(-R // per)):
                        m = min(per, R - q * per)
                        last = eng.tensor_copy(tin[:, q * per:q * per + m, :, :],
                                               ps_slot[:, q, 0:m * NB * P].rearrange("p (r b w) -> p r b w", r=m, b=NB))
                    last.then_inc(F["s_cpv"], 1)
                    F["finish_dve"](eng, t)
                    eng.sem_inc(s_free, 1)
                tiles(body, eng)


_INS = ['x', 'src', 'dst', 'edge_type_8', 'L0_gnn_weight', 'L0_gnn_bias', 'L1_gnn_W', 'L1_gnn_b']


def kernel(**inputs):
    import numpy as _np
    import concourse.bacc as _bacc
    from concourse import mybir as _mybir
    from concourse.bass_utils import run_bass_kernel_spmd as _run

    nc = _bacc.Bacc("TRN2", target_bir_lowering=False, num_devices=1)
    arrays, args = {}, []
    for name in _INS:
        a = _np.ascontiguousarray(inputs[name])
        arrays[f"in_{name}_dram"] = a
        args.append(nc.dram_tensor(f"in_{name}_dram", a.shape, _mybir.dt.from_np(a.dtype), kind="ExternalInput").ap())
    shape = tuple(inputs['x'].shape)
    args.append(nc.dram_tensor("out_0_dram", shape, _mybir.dt.float32, kind="ExternalOutput").ap())
    program(nc, *args)
    r = _run(nc, [arrays], core_ids=[0])
    return r.results[0]["out_0_dram"]
```

```python
import concourse.bass as bass
from concourse import mybir
from contextlib import ExitStack

P = 128
LOT = 3
WIN = 16
HALF = 64
LOTS = 11
GROUPS = ((0, 4), (4, 8), (8, 11))
NBANK = 6
NBANK1 = 3
SUB = 8
SPAN = 4
PAD_DST = 60000.0


class Dims:

    def __init__(self, n, e, d, rel):
        self.n, self.e, self.d, self.rel = n, e, d, rel
        self.nb = d // P
        self.cps = LOT * LOTS
        self.chunks = -(-e // P)
        self.segs = -(-self.chunks // self.cps)
        self.tiles = -(-(n + HALF) // P)
        self.kt = -(-(self.segs + 1) * LOTS // P)
        self.ncol = self.kt * P * LOT
        self.tg = self.tiles // 2 + 1
        self.td = self.tiles - self.tg
        self.nsub = self.td * P // SUB
        self.early = (self.tiles - 2) * 2 // 3
        self.last_rows = n - (P * (self.tiles - 1) - HALF)


def wait(eng, sem, value):
    if isinstance(value, int) and value <= 0:
        return
    eng.wait_ge(sem, value)


def wait_alone(eng, sem, value, mark):
    eng.wait_ge(sem, value)
    eng.sem_inc(mark, 1)


def program(nc, x, src, dst, etype, w0, b0, w1, b1, out):
    f32, bf16, i32 = mybir.dt.float32, mybir.dt.bfloat16, mybir.dt.int32
    ALU, ACT, AX = mybir.AluOpType, mybir.ActivationFunctionType, mybir.AxisListType
    D = Dims(x.shape[0], src.shape[0], x.shape[1], w0.shape[0])
    N, E, DF, R, NB, KT, T = D.n, D.e, D.d, D.rel, D.nb, D.kt, D.tiles
    DF3 = 3 * DF
    LIM = 2 * P

    table0 = nc.dram_tensor("table0", (T * P, DF3), bf16).ap()
    table1 = nc.dram_tensor("table1", (T * P, DF3), bf16).ap()
    x1_d = nc.dram_tensor("x1_d", (T * P, DF), f32).ap()
    ends_d = nc.dram_tensor("ends_d", (2, D.ncol + SPAN), f32).ap()
    offs_d = nc.dram_tensor("offs_d", (KT, P), i32).ap()

    whole = ExitStack()
    with whole:
        def sb(name, shape, dt, ctx=whole):
            return ctx.enter_context(nc.sbuf_tensor(name, shape, dt))

        def sem(name, ctx=whole):
            return ctx.enter_context(nc.semaphore(name))

        ident = sb("ident", [P, P], f32)
        identb = sb("identb", [P, P], bf16)
        ones = sb("ones", [P, P], bf16)
        onef = sb("onef", [1, P], f32)
        iota = sb("iota", [P, R * WIN], bf16)
        LE = LOT * P
        eps = sb("eps", [P, 1], f32)
        bias0 = sb("bias0", [1, DF], f32)
        bias1 = sb("bias1", [P, DF], f32)
        WEND = T * DF + R * NB * DF
        arena = sb("arena", [P, max(WEND + D.ncol // 2, T * DF3 // 2)], f32)
        xres = arena[:, 0:T * DF].rearrange("p (t d) -> p t d", d=DF)
        w0t = arena[:, T * DF:WEND].rearrange("p (r b d) -> p r b d", r=R, b=NB)
        hs_all = arena[:, 0:T * DF3 // 2].bitcast(bf16).rearrange("p (t d) -> p t d", d=DF3)
        mkey = sb("mkey", [P, D.ncol], f32)
        klo = sb("klo", [P, D.ncol], f32)
        subr = sb("subr", [1, D.td + 1, P // SUB], i32)
        w1s = sb("w1s", [P, NB, DF], f32)
        idxT = sb("idxT", [P, D.ncol], i32)
        keyT = [arena[:, WEND:WEND + D.ncol // 2].bitcast(bf16), sb("key1T", [P, D.ncol], bf16)[:, :]]
        n_inside = sb("n_inside", [1, 1], i32)
        offr = sb("offr", [1, D.segs, 12], i32)
        dinv = sb("dinv", [P, T], f32)
        s_early = sem("early")

        ps_slot = whole.enter_context(nc.psum_tensor("ps_slot", [P, 6, 512], f32))
        ps_proj = whole.enter_context(nc.psum_tensor("ps_proj", [P, 512], f32))
        ps_aux = whole.enter_context(nc.psum_tensor("ps_aux", [P, 512], f32))

        with ExitStack() as pro:
            names = ("ld_e", "ld_w", "ld_c", "const", "memx", "edge", "etp", "ecp", "epse", "offw",
                     "offrd", "stat", "agg", "sd", "rstd", "nbias", "h32", "hi", "r1", "mid",
                     "lo", "padm", "rel", "cnst0", "inw", "cntp", "cnt", "ends", "endw",
                     "near", "wst", "below", "subp", "subc", "padf")
            S = {k: sem("p_" + k) for k in names}
            NH = 6
            XL = [(a, min(a + 6, T)) for a in range(0, T, 6)]
            s_t0 = [sem(f"p_t0_{i}") for i in range(NH)]
            s_x = [sem(f"p_x_{i}") for i in range(len(XL))]
            er = [sb(f"er{i}", [P, KT, LE], i32, pro) for i in range(3)]
            ef01 = sb("ef01", [P, 2, KT, LE], f32, pro)
            ef = [ef01[:, 0, :, :], ef01[:, 1, :, :]] + [sb(f"ef{i}", [P, KT, LE], f32, pro)[:, :, :] for i in (2, 3)]
            flat = [e[:, :, :].rearrange("p k j -> p (k j)") for e in er]
            inw, wid = ef[3], flat[1]
            dstT = flat[0].bitcast(f32)
            KC = KT * LOT
            ends = sb("ends", [P, 2, KC], f32, pro)
            near = sb("near", [P, 3, KC], f32, pro)
            bad = sb("bad", [P, 3, KC], f32, pro)
            wf = sb("wf", [P, 2, KC], f32, pro)
            wi = sb("wi", [P, 2, KC], i32, pro)
            padf = sb("padf", [2, SPAN], f32, pro)
            nbad = sb("nbad", [P, 2], f32, pro)
            wst_i = sb("wst_i", [P, D.nsub], i32, pro)
            wst = sb("wst", [P, D.nsub], f32, pro)
            cnt_in = sb("cnt_in", [P, 1], f32, pro)
            onec = sb("onec", [P, 1], f32, pro)
            chunk_id = sb("chunk_id", [P, KT], i32, pro)
            seg_i = sb("seg_i", [P, KT], i32, pro)
            small = sb("small", [P, 6, KT], f32, pro)
            relT = sb("relT", [KT, P], i32, pro)
            wld = sb("wld", [P, R, NB, DF], f32, pro)
            below = ef01[:, :, :, :].rearrange("p a k j -> p (a k j)").bitcast(bf16)[:, 0:KC * D.nsub].rearrange("p (c w) -> p c w", w=D.nsub)
            st6 = sb("st6", [P, T, 6], f32, pro)
            mv = sb("mv", [P, T, 2], f32, pro)
            rs = sb("rs", [P, T], f32, pro)
            nb = sb("nb", [P, T], f32, pro)
            h32 = sb("h32", [P, NH, DF], f32, pro)
            r1 = sb("r1", [P, NH, DF], f32, pro)
            hs = sb("hs", [P, NH, DF3], bf16, pro)

            full = E // (P * LE)
            rest_rows = (E - full * P * LE) // LE
            rest = E - full * P * LE - rest_rows * LE
            assert full == KT - 1
            n_edma = 2 + (1 if rest else 0)
            FULLT = (N - HALF) // P

            block = pro.enter_context(nc.Block())

            @block.sync
            def _(eng):
                wait(eng, S["padm"], 3)
                for a, r in zip((dst, src, etype), er):
                    eng.dma_start(r[:, 0:full, :], a[0:full * P * LE].rearrange("(k p j) -> p k j", p=P, j=LE)).then_inc(S["ld_e"], 16)
                    o = full * P * LE
                    eng.dma_start(r[0:rest_rows, full, :], a[o:o + rest_rows * LE].rearrange("(p j) -> p j", j=LE)).then_inc(S["ld_e"], 16)
                    if rest:
                        o += rest_rows * LE
                        eng.dma_start(r[rest_rows:rest_rows + 1, full, 0:rest], a[o:o + rest].rearrange("(p j) -> p j", p=1)).then_inc(S["ld_e"], 16)

                def compare_ends():
                    wait(eng, S["ends"], 1)
                    wait(eng, S["padf"], 1)
                    eng.dma_start(ends_d[:, D.ncol:D.ncol + SPAN], padf[:, :]).then_inc(S["endw"], 16)
                    for i in range(2):
                        eng.dma_start(ends_d[i, 0:D.ncol].rearrange("(k p q) -> p k q", p=P, q=LOT),
                                      ends[:, i, :].rearrange("p (k q) -> p k q", q=LOT)).then_inc(S["endw"], 16)
                    wait(eng, S["endw"], 48)
                    for i, (r, o) in enumerate(((1, 0), (0, 1), (0, SPAN))):
                        eng.dma_start(near[:, i, :], ends_d[r, o:o + D.ncol].rearrange("(p c) -> p c", p=P)).then_inc(S["near"], 16)

                def window_starts():
                    wait(eng, S["rel"], 1)
                    eng.dma_start(offs_d, relT[:, :]).then_inc(S["offw"], 16)
                    wait(eng, S["offw"], 16)
                    row = offs_d.rearrange("(o k) p -> o (k p)", o=1)[:, 0:D.segs * LOTS].rearrange("o (s j) -> o s j", j=LOTS)
                    eng.dma_start(offr[:, :, 0:LOTS], row).then_inc(S["offrd"], 16)

                for t in range(T):
                    wait(eng, S["hi"], t + 1)
                    wait(eng, S["mid"], t + 1)
                    wait(eng, S["lo"], t + 1)
                    eng.dma_start(table0[t * P:(t + 1) * P, :], hs[:, t % NH, :]).then_inc(s_t0[t % NH], 16)
                    if t == NH + 2:
                        compare_ends()
                window_starts()
                for k in range(NH):
                    wait(eng, s_t0[k], 16 * ((T - k + NH - 1) // NH))
                wait(eng, S["offrd"], 16)
                wait(eng, S["near"], 48)

            @block.scalar
            def _(eng):
                wait(eng, S["memx"], 2)
                eng.dma_start(xres[HALF:P, 0, :], x[0:HALF, :]).then_inc(s_x[0], 16)
                for li, (a, b) in enumerate(XL):
                    lo_t, hi_t = max(a, 1), min(b, FULLT + 1)
                    if hi_t > lo_t:
                        eng.dma_start(xres[:, lo_t:hi_t, :], x[lo_t * P - HALF:hi_t * P - HALF, :].rearrange("(t p) d -> p t d", p=P)).then_inc(s_x[li], 16)
                    if b == T:
                        eng.dma_start(xres[0:D.last_rows, T - 1, :], x[N - D.last_rows:N, :]).then_inc(s_x[li], 16)
                wait(eng, S["const"], 7)
                def second(t):
                    wait(eng, S["r1"], t + 1)
                    eng.activation(hs[:, t % NH, DF:2 * DF], r1[:, t % NH, :], ACT.Copy).then_inc(S["mid"], 1)

                for li in range(len(XL) + 1):
                    if li < len(XL):
                        a, b = XL[li]
                        wait(eng, S["agg"], li + 1)
                        eng.activation(rs[:, a:b], mv[:, a:b, 1], ACT.Sqrt, bias=eps[:, :]).then_inc(S["sd"], 1)
                    if li == 0:
                        continue
                    if li == 2:
                        eng.dma_start(wld[:, :, :, :], w0.rearrange("r (b p) i -> p r b i", p=P)).then_inc(S["ld_w"], 16)
                        eng.dma_start(w1s[:, :, :], w1.rearrange("(b p) o -> p b o", p=P)).then_inc(S["ld_c"], 16)
                        eng.dma_start(bias0[:, :], b0.rearrange("(o d) -> o d", o=1)).then_inc(S["ld_c"], 16)
                        eng.dma_start(bias1[:, :], b1.rearrange("(o d) -> o d", o=1).to_broadcast([P, DF])).then_inc(S["ld_c"], 16)
                    wait(eng, S["nbias"], li)
                    for t in range(*XL[li - 1]):
                        k = t % NH
                        wait(eng, S["lo"], t - NH + 1)
                        eng.activation(h32[:, k, :], xres[:, t, :], ACT.Relu, scale=rs[:, t:t + 1], bias=nb[:, t:t + 1]).then_inc(S["h32"], 1)
                        if t >= NH:
                            wait(eng, s_t0[k], 16 * (t // NH))
                        wait(eng, S["h32"], t + 1)
                        eng.activation(hs[:, k, 0:DF], h32[:, k, :], ACT.Copy).then_inc(S["hi"], 1)
                        if t > 0:
                            second(t - 1)
                second(T - 1)
                wait(eng, S["ld_c"], 48)

            @block.gpsimd
            def _(eng):
                eng.memset(er[0][:, full, :], int(PAD_DST)).then_inc(S["padm"], 1)
                eng.memset(er[1][:, full, :], 0).then_inc(S["padm"], 1)
                eng.memset(er[2][:, full, :], 0).then_inc(S["padm"], 1)
                eng.memset(xres[:, 0, :], 0.0).then_inc(S["memx"], 1)
                eng.memset(xres[:, T - 1, :], 0.0).then_inc(S["memx"], 1)
                eng.iota(chunk_id[:, :], [[P, KT]], base=0, channel_multiplier=1).then_inc(S["const"], 1)
                eng.memset(ident[:, :], 0.0).then_inc(S["cnst0"], 1)
                eng.memset(identb[:, :], 0.0).then_inc(S["cnst0"], 1)
                wait(eng, S["cnst0"], 2)
                for m in (ident, identb):
                    eng.affine_select(out=m[:, :], in_=m[:, :], compare_op=ALU.not_equal, fill=1.0, base=0,
                                      pattern=[[-1, P]], channel_multiplier=1).then_inc(S["const"], 1)
                eng.iota(iota[:, :], [[1, R * WIN]], base=0, channel_multiplier=0,
                         allow_small_or_imprecise_dtypes=True).then_inc(S["const"], 1)
                eng.memset(ones[:, :], 1.0).then_inc(S["const"], 1)
                eng.memset(onef[:, :], 1.0).then_inc(S["const"], 1)
                eng.memset(onec[:, :], 1.0)
                eng.memset(eps[:, :], 1e-5).then_inc(S["const"], 1)
                eng.memset(padf[:, :], PAD_DST).then_inc(S["padf"], 1)
                eng.iota(wst_i[:, :], [[SUB, D.nsub]], base=D.tg * P - HALF, channel_multiplier=0).then_inc(S["wst"], 1)
                def third(t):
                    k = t % NH
                    wait(eng, S["mid"], t + 1)
                    eng.tensor_tensor(hs[:, k, 2 * DF:DF3], r1[:, k, :], hs[:, k, DF:2 * DF], ALU.subtract).then_inc(S["lo"], 1)

                for t in range(T):
                    k = t % NH
                    wait(eng, S["hi"], t + 1)
                    eng.tensor_tensor(r1[:, k, :], h32[:, k, :], hs[:, k, 0:DF], ALU.subtract).then_inc(S["r1"], 1)
                    if t > 0:
                        third(t - 1)
                third(T - 1)

            @block.vector
            def _(eng):
                seg_f, base, rel, orig = (small[:, i, :] for i in range(4))
                ne = [0]

                def step(ins):
                    ne[0] += 1
                    ins.then_inc(S["epse"], 1)
                    wait(eng, S["epse"], ne[0])

                def edge_keys():
                    wait(eng, S["const"], 1)
                    mid_c = float((LOTS - 1) // 2)
                    step(eng.tensor_scalar(seg_f, chunk_id[:, :], -mid_c, 1.0 / LOTS, ALU.add, ALU.mult))
                    step(eng.tensor_copy(seg_i[:, :], seg_f))
                    step(eng.tensor_copy(orig, seg_i[:, :]))
                    step(eng.tensor_scalar(orig, orig, float(P), float(-HALF), ALU.mult, ALU.add))
                    wait(eng, S["ld_e"], 16 * 3 * n_edma)
                    step(eng.tensor_copy(ef[3][:, :, :], er[0][:, :, :]))
                    chunks = ef[3][:, :, :].rearrange("p k (q j) -> p (k q) j", q=LOT)
                    step(eng.tensor_reduce(ends[:, 0, :], chunks, AX.X, ALU.min))
                    eng.tensor_reduce(ends[:, 1, :], chunks, AX.X, ALU.max).then_inc(S["ends"], 1)
                    wait(eng, S["ends"], 1)
                    step(eng.tensor_reduce(base, ends[:, 0, :].rearrange("p (k q) -> p k q", q=LOT), AX.X, ALU.min))
                    step(eng.tensor_tensor(rel, base, orig, ALU.subtract))
                    step(eng.tensor_scalar(rel, rel, 0.0, float(LIM), ALU.max, ALU.min))
                    step(eng.tensor_tensor(base, rel, orig, ALU.add))
                    bc = small[:, 1, :].unsqueeze(2).to_broadcast([P, KT, LE])
                    step(eng.tensor_tensor(ef[2][:, :, :], ef[3][:, :, :], bc, ALU.subtract))
                    step(eng.tensor_scalar(ef[1][:, :, :], er[2][:, :, :], float(WIN), None, ALU.mult))
                    step(eng.tensor_tensor(ef[1][:, :, :], ef[1][:, :, :], ef[2][:, :, :], ALU.add))
                    eng.tensor_scalar(ef[0][:, :, :], er[1][:, :, :], float(HALF), None, ALU.add).then_inc(S["edge"], 1)

                def stats(li):
                    a, b = XL[li]
                    n_x = (a == 0) + (min(b, FULLT + 1) > max(a, 1)) + (b == T)
                    wait(eng, s_x[li], 16 * n_x)
                    for t in range(a, b):
                        last = eng.bn_stats(st6[:, t, :], xres[:, t, :])
                    last.then_inc(S["stat"], 1)
                    wait(eng, S["stat"], li + 1)
                    for t in range(a, b):
                        last = eng.bn_aggr(mv[:, t, :], st6[:, t, :])
                    last.then_inc(S["agg"], 1)

                def scales(li):
                    a, b = XL[li]
                    wait(eng, S["sd"], li + 1)
                    eng.reciprocal(rs[:, a:b], rs[:, a:b]).then_inc(S["rstd"], 1)
                    wait(eng, S["rstd"], li + 1)
                    eng.scalar_tensor_tensor(nb[:, a:b], mv[:, a:b, 0], -1.0, rs[:, a:b], ALU.mult, ALU.mult).then_inc(S["nbias"], 1)

                copies = []
                for dest in (idxT[:, :], dstT, keyT[0], keyT[1]):
                    for k in range(KT):
                        d = dest[:, k * P * LOT:(k + 1) * P * LOT].rearrange("p (l q) -> p q l", q=LOT)
                        copies.append((d, ps_slot[:, len(copies) % 6, 0:LE].rearrange("p (q l) -> p q l", q=LOT)))
                copies.append((relT[:, :], ps_slot[0:KT, len(copies) % 6, 0:P]))
                for r in range(R):
                    copies.append((w0t[:, r, :, :].rearrange("p b o -> p (b o)"), ps_slot[:, len(copies) % 6, 0:NB * DF]))
                n_edge = len(copies) - R

                def copy(i):
                    wait(eng, S["etp"], i + 1)
                    ins = eng.tensor_copy(copies[i][0], copies[i][1])
                    ins.then_inc(S["ecp"], 1)
                    if i == n_edge - 1:
                        wait(eng, S["ecp"], i + 1)
                        eng.memset(small[:, 5, 0:1], 0.0).then_inc(S["rel"], 1)

                def checks():
                    wait(eng, S["ecp"], 2 * KT)
                    step(eng.tensor_scalar(wid, idxT[:, :], -(P - 1) / 2.0, 1.0 / P, ALU.add, ALU.mult))
                    yield
                    step(eng.scalar_tensor_tensor(klo[:, :], wid, -float(P), idxT[:, :], ALU.mult, ALU.add))
                    yield
                    step(eng.tensor_scalar(mkey[:, :], wid, float(SUB), None, ALU.mult))
                    yield
                    step(eng.tensor_scalar(wid, dstT, HALF - (SUB - 1) / 2.0, 1.0 / SUB, ALU.add, ALU.mult))
                    yield
                    step(eng.scalar_tensor_tensor(klo[:, :], wid, float(P), klo[:, :], ALU.mult, ALU.add))
                    yield
                    step(eng.scalar_tensor_tensor(mkey[:, :], wid, -float(SUB), mkey[:, :], ALU.mult, ALU.add))
                    yield
                    step(eng.scalar_tensor_tensor(mkey[:, :], dstT, float(HALF), mkey[:, :], ALU.add, ALU.add))
                    yield

                    wait(eng, S["wst"], 1)
                    wait(eng, S["etp"], 3 * KT)
                    step(eng.tensor_copy(wst[:, :], wst_i[:, :]))
                    yield
                    for i in range(KC):
                        last = eng.tensor_scalar(below[:, i, :], wst[:, :], ends[:, 1, i:i + 1], None, ALU.is_gt)
                    last.then_inc(S["below"], 1)
                    yield

                    step(eng.tensor_scalar(inw[:, :, :], ef[2][:, :, :], 0.0, None, ALU.is_ge))
                    yield
                    step(eng.scalar_tensor_tensor(inw[:, :, :], ef[2][:, :, :], float(WIN), inw[:, :, :], ALU.is_lt, ALU.mult))
                    yield
                    step(eng.tensor_reduce(nbad[:, 0:1], inw[:, :, :], AX.XY, ALU.add))
                    yield
                    wait(eng, S["near"], 48)
                    step(eng.tensor_tensor(bad[:, 0, :], near[:, 1, :], near[:, 0, :], ALU.is_lt))
                    yield
                    step(eng.tensor_scalar(wi[:, :, :], near[:, 0::2, :], HALF - (SUB - 1) / 2.0, 1.0 / SUB, ALU.add, ALU.mult))
                    yield
                    step(eng.tensor_copy(wf[:, :, :], wi[:, :, :]))
                    yield
                    step(eng.tensor_tensor(bad[:, 1, :], wf[:, 1, :], wf[:, 0, :], ALU.is_le))
                    yield
                    step(eng.scalar_tensor_tensor(bad[:, 1, :], near[:, 2, :], PAD_DST, bad[:, 1, :], ALU.is_lt, ALU.mult))
                    yield
                    step(eng.tensor_tensor(bad[:, 2, :], ends[:, 1, :], ends[:, 0, :], ALU.is_le))
                    yield
                    step(eng.scalar_tensor_tensor(bad[:, 2, :], ends[:, 0, :], PAD_DST, bad[:, 2, :], ALU.is_lt, ALU.mult))
                    yield
                    step(eng.tensor_reduce(nbad[:, 1:2], bad[:, :, :], AX.XY, ALU.add))
                    yield
                    eng.tensor_tensor(cnt_in[:, :], nbad[:, 0:1], nbad[:, 1:2], ALU.subtract).then_inc(S["inw"], 1)
                EARLY = min(4, len(XL) - 1)
                later = checks()
                done = 0
                for li in range(len(XL)):
                    if li == EARLY:
                        edge_keys()
                    stats(li)
                    if 0 < li <= EARLY:
                        scales(li - 1)
                    for _ in range(5 if li >= EARLY else 0):
                        if done < len(copies):
                            copy(done)
                            done += 1
                    for _ in range(3 if done >= 3 * KT else 0):
                        next(later)
                    if li > EARLY:
                        scales(li - 1)
                scales(len(XL) - 1)
                while done < len(copies):
                    copy(done)
                    done += 1
                for _ in later:
                    pass
                wait(eng, S["cntp"], 1)
                eng.tensor_scalar(n_inside[:, :], ps_aux[0:1, 0:1], 0.0, None, ALU.max).then_inc(S["cnt"], 1)
                wait(eng, S["subp"], 1)
                eng.tensor_copy(subr[:, 0:D.td, :].rearrange("o t w -> o (t w)"), ps_proj[0:1, 0:D.nsub]).then_inc(S["subc"], 1)

            @block.tensor
            def _(eng):
                wait(eng, S["const"], 7)
                wait(eng, S["edge"], 1)
                n = 0
                for a in (0, 3, 1, 2):
                    for k in range(KT):
                        wait(eng, S["ecp"], n - 5)
                        for q in range(LOT):
                            last = eng.transpose(ps_slot[:, n % 6, q * P:(q + 1) * P], ef[a][:, k, q * P:(q + 1) * P], ident[:, :])
                        last.then_inc(S["etp"], 1)
                        n += 1
                wait(eng, S["ecp"], n - 5)
                eng.transpose(ps_slot[0:KT, n % 6, 0:P], small[:, 2, :], ident[:, :]).then_inc(S["etp"], 1)
                n += 1
                wait(eng, S["ld_w"], 16)
                for r in range(R):
                    wait(eng, S["ecp"], n - 5)
                    for ib in range(NB):
                        for ob in range(NB):
                            last = eng.transpose(ps_slot[:, n % 6, ib * DF + ob * P:ib * DF + (ob + 1) * P],
                                                 wld[:, r, ob, ib * P:(ib + 1) * P], ident[:, :])
                    last.then_inc(S["etp"], 1)
                    n += 1
                wait(eng, S["below"], 1)
                for i in range(KC):
                    last = eng.matmul(ps_proj[0:1, 0:D.nsub], ones[:, 0:1], below[:, i, :], start=(i == 0), stop=(i == KC - 1))
                last.then_inc(S["subp"], 1)
                wait(eng, S["inw"], 1)
                eng.matmul(ps_aux[0:1, 0:1], cnt_in[:, :], onec[:, :], start=True, stop=True).then_inc(S["cntp"], 1)

        def shared(layer):
            return dict(table=(table0, table1)[layer], table1=table1, out=out, idxT=idxT, key=keyT[layer], key_dst=keyT[1],
                        offr=offr, iota=iota, ones=ones, onef=onef, ident=ident, identb=identb, eps=eps, xres=xres,
                        w0t=w0t, w1s=w1s, bias0=bias0, bias1=bias1, dinv=dinv, ps_slot=ps_slot, ps_proj=ps_proj,
                        ps_aux=ps_aux, src=src, dst=dst, etype=etype, x1_d=x1_d, hs_all=hs_all, mkey=mkey, klo=klo, subr=subr, s_early=s_early)

        inside = nc.values_load(n_inside[0:1, 0:1], min_val=0, max_val=E)
        with nc.If(inside == E):
            aggregate_relations(nc, D, shared(0))
            aggregate_mixed(nc, D, shared(1))
        with nc.Else():
            for layer in (0, 1):
                aggregate_any(nc, D, layer, shared(layer))


def finishing(nc, D, layer, V, ctx, path):
    f32, bf16 = mybir.dt.float32, mybir.dt.bfloat16
    ALU, ACT = mybir.AluOpType, mybir.ActivationFunctionType
    first = layer == 0
    R = D.rel if first else 1
    NB, DF, DF3, T = D.nb, D.d, 3 * D.d, D.tiles
    xres, ps_proj, dinv = V["xres"], V["ps_proj"], V["dinv"]

    def sb(name, shape, dt):
        return ctx.enter_context(nc.sbuf_tensor(f"{name}_{path}{layer}", shape, dt))

    def sem(name):
        return ctx.enter_context(nc.semaphore(f"{path}{layer}_{name}"))

    tile_in = sb("tile_in", [P, NB, R, P], f32)
    st6 = sb("st6", [P, 6], f32)
    mv = sb("mv", [P, 2], f32)
    v2 = sb("v2", [P, 2], f32)
    r2 = sb("r2", [P, 2], f32)
    ab = sb("ab", [P, 2], f32)
    x1 = sb("x1", [P, DF], f32)
    h32 = sb("h32", [P, DF], f32)
    r1 = sb("r1", [P, DF], f32) if first else None
    hs = sb("hs", [P, DF3], bf16) if first or path == "g" else None
    y = sb("y", [P, DF], f32)
    z = sb("z", [P, DF], f32)

    s_mark = [sem(f"mark{i}") for i in range(2)]
    s_cpa = sem("copy_act")
    s_cpv = sem("copy_dve")
    s_proj = sem("proj")
    s_x1 = sem("x1")
    E = {k: sem("e_" + k) for k in ("stat", "agg", "cnt", "v2", "sd", "r2", "a", "ab", "h32", "hi", "r1",
                                    "mid", "lo", "st", "y", "z", "o", "self_mm", "deg", "xin")}

    def tile_io(eng, t, n=None):
        n = t if n is None else n
        if first:
            wait(eng, E["hi"], n + 1)
            wait(eng, E["mid"], n + 1)
            wait_alone(eng, E["lo"], n + 1, s_mark[1])
            eng.dma_start(V["table1"][bass.ds(t * P, P), :], hs[:, :]).then_inc(E["st"], 16)
            eng.dma_start(V["x1_d"][bass.ds(t * P, P), :], x1[:, :]).then_inc(E["st"], 16)
            wait_alone(eng, E["st"], 32 * (n + 1), s_mark[1])
        else:
            eng.dma_start(x1[:, :], V["x1_d"][bass.ds(t * P, P), :]).then_inc(E["xin"], 16)
            wait_alone(eng, E["z"], n + 1, s_mark[1])
            if isinstance(t, int) and t == 0:
                eng.dma_start(V["out"][0:HALF, :], z[HALF:P, :]).then_inc(E["o"], 16)
            elif isinstance(t, int) and t == T - 1:
                eng.dma_start(V["out"][D.n - D.last_rows:D.n, :], z[0:D.last_rows, :]).then_inc(E["o"], 16)
            else:
                eng.dma_start(V["out"][bass.ds(t * P - HALF, P), :], z[:, :]).then_inc(E["o"], 16)
            wait(eng, E["xin"], 16 * (n + 1))
            wait_alone(eng, E["o"], 16 * (n + 1), s_mark[1])

    def finish_act(eng, t):
        if not first:
            return
        wait(eng, E["v2"], t + 1)
        eng.activation(r2[:, :], v2[:, :], ACT.Sqrt).then_inc(E["sd"], 1)
        wait(eng, E["ab"], t + 1)
        eng.activation(h32[:, :], x1[:, :], ACT.Relu, scale=ab[:, 0:1], bias=ab[:, 1:2]).then_inc(E["h32"], 1)
        wait(eng, E["h32"], t + 1)
        wait(eng, E["st"], 32 * t)
        eng.activation(hs[:, 0:DF], h32[:, :], ACT.Copy).then_inc(E["hi"], 1)
        wait(eng, E["r1"], t + 1)
        eng.activation(hs[:, DF:2 * DF], r1[:, :], ACT.Copy).then_inc(E["mid"], 1)

    def finish_dve(eng, t, n=None):
        n = t if n is None else n
        if first:
            wait(eng, s_proj, n + 1)
            wait(eng, E["st"], 32 * t)
            eng.tensor_tensor(x1[:, :], ps_proj[:, 0:DF], xres[:, t, :], ALU.add).then_inc(s_x1, 1)
            wait(eng, s_x1, t + 1)
            eng.bn_stats(st6[:, :], x1[:, :]).then_inc(E["stat"], 1)
            wait(eng, E["deg"], t + 1)
            wait(eng, E["stat"], t + 1)
            eng.tensor_scalar(v2[:, 1:2], dinv[:, bass.ds(t, 1)], 1.0, None, ALU.add)
            eng.bn_aggr(mv[:, :], st6[:, :]).then_inc(E["agg"], 1)
            wait(eng, E["agg"], t + 1)
            eng.tensor_scalar(v2[:, 0:1], mv[:, 1:2], 1e-5, None, ALU.add).then_inc(E["v2"], 1)
            wait(eng, E["sd"], t + 1)
            eng.reciprocal(r2[:, :], r2[:, :]).then_inc(E["r2"], 1)
            wait(eng, E["r2"], t + 1)
            eng.tensor_scalar(dinv[:, bass.ds(t, 1)], r2[:, 1:2], 1.0, None, ALU.mult)
            eng.tensor_tensor(ab[:, 0:1], r2[:, 0:1], r2[:, 1:2], ALU.mult).then_inc(E["a"], 1)
            wait(eng, E["a"], t + 1)
            eng.scalar_tensor_tensor(ab[:, 1:2], mv[:, 0:1], -1.0, ab[:, 0:1], ALU.mult, ALU.mult).then_inc(E["ab"], 1)
            wait(eng, E["h32"], t + 1)
            wait(eng, E["hi"], t + 1)
            eng.tensor_tensor(r1[:, :], h32[:, :], hs[:, 0:DF], ALU.subtract).then_inc(E["r1"], 1)
            wait(eng, E["r1"], t + 1)
            wait(eng, E["mid"], t + 1)
            eng.tensor_tensor(hs[:, 2 * DF:DF3], r1[:, :], hs[:, DF:2 * DF], ALU.subtract).then_inc(E["lo"], 1)
        else:
            for step in finish_steps(eng, t, n):
                step()

    def finish_steps(eng, t, n):
        def scale():
            wait(eng, s_proj, n + 1)
            eng.scalar_tensor_tensor(y[:, :], ps_proj[:, 0:DF], dinv[:, bass.ds(t, 1)], V["bias1"][:, :],
                                     ALU.mult, ALU.add).then_inc(s_x1, 1)

        def leaky():
            wait(eng, s_x1, n + 1)
            eng.scalar_tensor_tensor(h32[:, :], y[:, :], 0.2, y[:, :], ALU.mult, ALU.max).then_inc(E["y"], 1)

        def residual():
            wait(eng, E["y"], n + 1)
            wait(eng, E["xin"], 16 * (n + 1))
            wait(eng, E["o"], 16 * n)
            eng.tensor_tensor(z[:, :], h32[:, :], x1[:, :], ALU.add).then_inc(E["z"], 1)

        return [scale, leaky, residual]

    def project(eng, t, part, act_share=True):
        if part == 0:
            wait(eng, s_cpv, t + 1)
            if first and act_share:
                wait(eng, s_cpa, t + 1)
            wait(eng, s_x1, t)
        if first:
            if part == 0:
                eng.matmul(ps_proj[:, 0:DF], V["onef"][:, :], V["bias0"][:, :], start=True, stop=False)
            for r in range(part * R // 2, (part + 1) * R // 2):
                for b in range(NB):
                    last = eng.matmul(ps_proj[:, 0:DF], tile_in[:, b, r, :], V["w0t"][:, r, b, :], start=False,
                                      stop=(r == R - 1 and b == NB - 1))
        else:
            last = eng.matmul(ps_proj[:, 0:DF], tile_in[:, part, 0, :], V["w1s"][:, part, :],
                              start=(part == 0), stop=(part == 1))
        if part == 1:
            last.then_inc(s_proj, 1)

    return dict(tile_in=tile_in, hs=hs, E=E, s_proj=s_proj, s_x1=s_x1, s_cpv=s_cpv, s_cpa=s_cpa, s_mark=s_mark,
                tile_io=tile_io, finish_act=finish_act, finish_dve=finish_dve, finish_steps=finish_steps, project=project)


def aggregate_relations(nc, D, V):
    f32, bf16, i32 = mybir.dt.float32, mybir.dt.bfloat16, mybir.dt.int32
    ALU, ACT, AX = mybir.AluOpType, mybir.ActivationFunctionType, mybir.AxisListType
    layer = 0
    R = D.rel
    NQ = D.nb * R + 1
    AQ = R
    NB, DF, DF3, T, CPS, SEGS = D.nb, D.d, 3 * D.d, D.tiles, D.cps, D.segs
    W = R * WIN
    LIM = 2 * P
    AW = LIM + WIN
    idxT, key, offr, iota, ps_slot, dinv = (V[k] for k in ("idxT", "key", "offr", "iota", "ps_slot", "dinv"))

    with ExitStack() as ctx:
        def sb(name, shape, dt):
            return ctx.enter_context(nc.sbuf_tensor(f"{name}_{layer}", shape, dt))

        def sem(name):
            return ctx.enter_context(nc.semaphore(f"s{layer}_{name}"))

        acc = sb("acc", [P, NQ, AW], f32)
        onehot = sb("onehot", [P, CPS, W], bf16)
        onedst = sb("onedst", [P, CPS, WIN], bf16)
        rows = sb("rows", [P, CPS, DF3], bf16)
        stage = sb("stage", [P, CPS], i32)
        scr = sb("scr", [P, P], f32)
        F = finishing(nc, D, layer, V, ctx, "s")
        tile_in, E, s_proj, s_cpv, s_cpa, s_mark = (F[k] for k in ("tile_in", "E", "s_proj", "s_cpv", "s_cpa", "s_mark"))

        s_zero = sem("zero")
        s_stage = sem("stage")
        s_rows = [sem(f"rows{g}") for g in range(3)]
        s_oh = sem("onehot")
        s_pe = sem("lot")
        s_acc = sem("acc")
        s_sha = sem("shift_act")
        s_shv = sem("shift_dve")
        s_tla = sem("tail_act")
        s_tlv = sem("tail_dve")
        s_bnd = sem("boundary")
        s_bndv = sem("boundary_dve")
        def chunks_of(g):
            return range(LOT * GROUPS[g][0], LOT * GROUPS[g][1])

        def last_use(j):
            return j - NBANK if j >= NBANK else max(k for k in range(LOTS) if k % NBANK == j) - LOTS

        block = ctx.enter_context(nc.Block())

        @block.gpsimd
        def _(eng):
            def body(s):
                for g in range(3):
                    wait_alone(eng, s_stage, s * 3 + g + 1, s_mark[0])
                    for c in chunks_of(g):
                        eng.indirect_dma_start(rows[:, c, :], None, V["table"],
                                               bass.IndirectOffsetOnAxis(ap=stage[:, c:c + 1], axis=0)).then_inc(s_rows[g], 16)
            body(0)
            body(1)
            with eng.Fori(2, SEGS) as s:
                body(s)

        @block.sync
        def _(eng):
            F["tile_io"](eng, 0)
            with eng.Fori(2, SEGS) as s:
                F["tile_io"](eng, s - 1)
            def load_rows(a):
                b = min(a + 8, D.early)
                eng.dma_start(V["hs_all"][:, a:b, :], V["table1"][a * P:b * P, :].rearrange("(t p) d -> p t d", p=P)).then_inc(V["s_early"], 16)
            starts = list(range(0, D.early, 8))
            for a in starts[0:2]:
                load_rows(a)
            F["tile_io"](eng, T - 2)
            F["tile_io"](eng, T - 1)
            for a in starts[2:]:
                load_rows(a)

        @block.scalar
        def _(eng):
            def put_stage(s, g):
                wait(eng, s_pe, (s - 1) * LOTS + GROUPS[g][1])
                r = chunks_of(g)
                eng.activation(stage[:, r.start:r.stop], idxT[:, bass.ds(s * CPS + r.start, len(r))], ACT.Copy).then_inc(s_stage, 1)

            def boundary(s):
                wait(eng, s_acc, (s + 1) * LOTS)
                wait(eng, s_proj, s)
                eng.activation(tile_in[:, 0, :, :], acc[:, 0:AQ, 0:P], ACT.Copy).then_inc(s_cpa, 1)
                wait(eng, s_cpa, s + 1)
                eng.activation(acc[:, 0:AQ, 0:P], acc[:, 0:AQ, P:LIM], ACT.Copy).then_inc(s_sha, 1)
                wait(eng, s_sha, s + 1)
                eng.activation(acc[:, 0:AQ, P:P + WIN], acc[:, 0:AQ, LIM:AW], ACT.Copy).then_inc(s_tla, 1)
                wait(eng, s_tla, s + 1)
                eng.activation(acc[:, 0:AQ, P + WIN:AW], V["ident"][:, 0:1].unsqueeze(1).to_broadcast([P, R, P]), ACT.Copy,
                               scale=0.0).then_inc(s_bnd, 1)

            def body(s):
                put_stage(s + 1, 0)
                put_stage(s + 1, 1)
                put_stage(s + 1, 2)
                boundary(s)
                if not (isinstance(s, int) and s == 0):
                    F["finish_act"](eng, s - 1)

            for g in range(3):
                put_stage(0, g)
            body(0)
            body(1)
            with eng.Fori(2, SEGS) as s:
                body(s)
            F["finish_act"](eng, T - 2)
            F["finish_act"](eng, T - 1)

        @block.vector
        def _(eng):
            def build_onehot(s, g):
                wait(eng, s_pe, (s - 1) * LOTS + GROUPS[g][1])
                r = chunks_of(g)
                last = None
                for hot, keys, w in ((onehot, key, W), (onedst, V["key_dst"], WIN)):
                    k = keys[:, bass.ds(s * CPS + r.start, len(r))]
                    last = eng.tensor_tensor(hot[:, r.start:r.stop, :], iota[:, 0:w].unsqueeze(1).to_broadcast([P, len(r), w]),
                                             k.unsqueeze(2).to_broadcast([P, len(r), w]), ALU.is_equal)
                last.then_inc(s_oh, 1)

            def starts(s):
                return nc.values_load_multi_w_load_instructions(
                    offr[0:1, s, 0:LOTS], engines=(mybir.EngineType.DVE,), min_val=0, max_val=LIM,
                    skip_runtime_bounds_check_because="the window starts are clamped to 0..LIM when they are computed")[1]

            def accumulate(s, g, off):
                for j in range(*GROUPS[g]):
                    c = s * LOTS + j
                    wait(eng, s_pe, c + 1)
                    wait(eng, s_acc, c)
                    win = acc[:, :, bass.ds(off[j], WIN)]
                    part = ps_slot[:, j % NBANK, 0:NQ * WIN].rearrange("p (q w) -> p q w", w=WIN)
                    eng.tensor_tensor(win, part, win, ALU.add).then_inc(s_acc, 1)

            def boundary(s, shift=True):
                wait(eng, s_acc, (s + 1) * LOTS if shift else SEGS * LOTS)
                wait(eng, s_proj, s)
                own = slice(AQ if shift else 0, NQ)
                eng.tensor_tensor(scr[:, :], acc[:, NQ - 1, 0:P], V["ident"][:, :], ALU.mult).then_inc(E["cnt"], 1)
                b0 = 1 if shift else 0
                eng.tensor_copy(tile_in[:, b0:NB, :, :].rearrange("p b r w -> p (b r) w"), acc[:, b0 * R:NB * R, 0:P]).then_inc(s_cpv, 1)
                wait(eng, E["cnt"], s + 1)
                eng.tensor_reduce(dinv[:, bass.ds(s, 1)], scr[:, :], AX.X, ALU.add).then_inc(E["deg"], 1)
                if shift:
                    wait(eng, s_cpv, s + 1)
                    eng.tensor_copy(acc[:, own, 0:P], acc[:, own, P:LIM]).then_inc(s_shv, 1)
                    wait(eng, s_shv, s + 1)
                    eng.tensor_copy(acc[:, own, P:P + WIN], acc[:, own, LIM:AW]).then_inc(s_tlv, 1)
                    wait(eng, s_tlv, s + 1)
                    eng.memset(acc[:, own, P + WIN:AW], 0.0).then_inc(s_bndv, 1)

            def body(s):
                off = starts(s)
                for g in range(3):
                    build_onehot(s + (g + 1) // 3, (g + 1) % 3)
                    if g == 0:
                        wait(eng, s_zero, 1)
                        wait(eng, s_bnd, s)
                        wait(eng, s_bndv, s)
                    accumulate(s, g, off)
                boundary(s)
                if not (isinstance(s, int) and s == 0):
                    F["finish_dve"](eng, s - 1)

            eng.memset(acc[:, :, :], 0.0).then_inc(s_zero, 1)
            build_onehot(0, 0)
            body(0)
            body(1)
            with eng.Fori(2, SEGS) as s:
                body(s)
            wait(eng, s_bnd, SEGS)
            wait(eng, s_bndv, SEGS)
            boundary(T - 1, shift=False)
            F["finish_dve"](eng, T - 2)
            F["finish_dve"](eng, T - 1)

        @block.tensor
        def _(eng):
            def group(s, g):
                wait(eng, s_rows[g], (s + 1) * (16 * len(chunks_of(g))))
                wait(eng, s_oh, s * 3 + g + 1)
                for j in range(*GROUPS[g]):
                    wait(eng, s_acc, s * LOTS + last_use(j) + 1)
                    o = ps_slot[:, j % NBANK, :]
                    lot = range(j * LOT, (j + 1) * LOT)
                    for b in range(NB):
                        for c in lot:
                            for p in range(3):
                                last = eng.matmul(o[:, b * W:(b + 1) * W], rows[:, c, p * DF + b * P:p * DF + (b + 1) * P],
                                                  onehot[:, c, :], start=(c == lot[0] and p == 0), stop=(c == lot[-1] and p == 2))
                    for c in lot:
                        last = eng.matmul(o[:, NB * W:NB * W + WIN], V["ones"][:, :], onedst[:, c, :],
                                          start=(c == lot[0]), stop=(c == lot[-1]))
                    last.then_inc(s_pe, 1)

            def body(s):
                for g in range(3):
                    group(s, g)
                    if g < 2 and not (isinstance(s, int) and s == 0):
                        F["project"](eng, s - 1, g)

            body(0)
            body(1)
            with eng.Fori(2, SEGS) as s:
                body(s)
            for t in (T - 2, T - 1):
                F["project"](eng, t, 0, act_share=t < T - 1)
                F["project"](eng, t, 1)


def aggregate_mixed(nc, D, V):
    f32, bf16, f16, i32 = mybir.dt.float32, mybir.dt.bfloat16, mybir.dt.float16, mybir.dt.int32
    ALU, ACT = mybir.AluOpType, mybir.ActivationFunctionType
    NB, DF, DF3, T, CPS, TG, TD = D.nb, D.d, 3 * D.d, D.tiles, D.cps, D.tg, D.td
    assert TG == TD + 2 and TD >= 4
    LIM = 2 * P
    AW = LIM + WIN
    NW = P // SUB
    MW = T * SUB
    COUNT_BANKS = (NBANK1, NBANK1 + 1)
    SUM_BANK = NBANK1 + 2
    idxT, key, offr, iota, ps_slot, ps_aux, hs_all = (
        V[k] for k in ("idxT", "key", "offr", "iota", "ps_slot", "ps_aux", "hs_all"))

    with ExitStack() as ctx:
        def sb(name, shape, dt):
            return ctx.enter_context(nc.sbuf_tensor(f"{name}_1", shape, dt))

        def sem(name):
            return ctx.enter_context(nc.semaphore(f"s1_{name}"))

        acc = sb("acc", [P, NB, AW], f32)
        onehot = sb("onehot", [P, CPS, WIN], bf16)
        rows = sb("rows", [P, CPS, DF3], bf16)
        stage = sb("stage", [P, CPS], i32)
        iota_m = sb("iota_m", [P, MW], f16)
        kk = sb("kk", [P, D.nsub + NW], f32)
        hot_lo = sb("hot_lo", [P, 2, SPAN, P], bf16)
        hot_m = sb("hot_m", [P, 2, SPAN, MW], bf16)
        counts = [sb(f"counts{i}", [P, T, P], bf16) for i in range(2)]
        lo_key = sb("lo_key", [P, 2, SPAN], f32)
        dsum = sb("dsum", [P, DF], f32)
        F = finishing(nc, D, 1, V, ctx, "s")
        tile_in, E, s_proj, s_cpv, s_mark = (F[k] for k in ("tile_in", "E", "s_proj", "s_cpv", "s_mark"))

        s_zero = sem("zero")
        s_iota = sem("iota")
        s_all = sem("all")
        s_stage = sem("stage")
        s_rows = [sem(f"rows{g}") for g in range(3)]
        s_oh = sem("onehot")
        s_pe = sem("lot")
        s_acc = sem("acc")
        s_shv = sem("shift_dve")
        s_tlv = sem("tail_dve")
        s_bndv = sem("boundary_dve")
        s_lo = sem("lo_key")
        s_hot = sem("hot")
        s_cnt = sem("counted")
        s_ev = sem("evacuated")
        s_sum = sem("dense_sum")
        s_ds = sem("dsum")
        s_dt = sem("dsum_t")

        def chunks_of(g):
            return range(LOT * GROUPS[g][0], LOT * GROUPS[g][1])

        def last_use(j):
            return j - NBANK1 if j >= NBANK1 else max(k for k in range(LOTS) if k % NBANK1 == j) - LOTS

        def at_least(s, k):
            return not isinstance(s, int) or s >= k

        FINISH_AT = (2, 3, 4, 7, 8, 9)

        def counting(s):
            return not isinstance(s, int) or s < TD

        def multiplying(s):
            return at_least(s, 1) and (not isinstance(s, int) or s <= TD)

        def steps(body, eng):
            body(0, 0)
            body(1, 1)
            end = 2 + (TD - 2) // 2 * 2
            with eng.Fori(2, end, 2) as s:
                body(s, 0)
                body(s + 1, 1)
            for s in range(end, TG):
                body(s, s % 2)

        def gathered(s):
            return s - 1, (2 * s - 3 if at_least(s, 2) else 0)

        def dense(s):
            return TG + s - 2, 2 * s - 2

        ALL = [(a, min(a + 6, T)) for a in range(D.early, T, 6)]
        LOT_AT = NW - 2 - LOTS
        GROUP_OF = {j: g for g in range(3) for j in range(*GROUPS[g])}

        def lots_after(s, w):
            if at_least(s, 1):
                return [w - LOT_AT] if 0 <= w - LOT_AT < LOTS else []
            return [j for j in range(LOTS) if NW // 2 + j * (NW // 2 - 1) // LOTS == w]

        def groups_done(s, w):
            return [g for g in range(3) if GROUPS[g][1] - 1 in lots_after(s, w)]
        LAST = T // 8
        SHARE = [w * (T - LAST) // NW for w in range(NW)] + [T]
        block = ctx.enter_context(nc.Block())

        @block.gpsimd
        def _(eng):
            eng.iota(iota_m[:, :], [[1, MW]], base=0, channel_multiplier=0,
                     allow_small_or_imprecise_dtypes=True).then_inc(s_iota, 1)
            eng.iota(kk[:, :], [[P, D.nsub + NW]], base=TG * NW * P, channel_multiplier=0,
                     allow_small_or_imprecise_dtypes=True).then_inc(s_iota, 1)

            def body(s, _):
                for g in range(3):
                    wait_alone(eng, s_stage, s * 3 + g + 1, s_mark[0])
                    for c in chunks_of(g):
                        eng.indirect_dma_start(rows[:, c, :], None, V["table"],
                                               bass.IndirectOffsetOnAxis(ap=stage[:, c:c + 1], axis=0)).then_inc(s_rows[g], 16)
            steps(body, eng)

        @block.sync
        def _(eng):
            wait(eng, s_rows[0], 16 * len(chunks_of(0)))
            for a, b in ALL:
                eng.dma_start(hs_all[:, a:b, :], V["table"][a * P:b * P, :].rearrange("(t p) d -> p t d", p=P)).then_inc(s_all, 16)
            F["tile_io"](eng, 0, 0)
            with eng.Fori(2, TG - 1) as s:
                F["tile_io"](eng, *gathered(s))
                F["tile_io"](eng, *dense(s))
            F["tile_io"](eng, *gathered(TG - 1))
            F["tile_io"](eng, *dense(TG - 1))
            F["tile_io"](eng, *gathered(TG))

        @block.scalar
        def _(eng):
            def put_stage(s, g):
                wait(eng, s_pe, (s - 1) * LOTS + GROUPS[g][1])
                r = chunks_of(g)
                eng.activation(stage[:, r.start:r.stop], idxT[:, bass.ds(s * CPS + r.start, len(r))], ACT.Copy).then_inc(s_stage, 1)

            def copy_sum(s):
                wait(eng, s_sum, s - 1)
                wait(eng, s_dt, s - 1)
                eng.activation(dsum[:, :], ps_slot[:, SUM_BANK, 0:DF], ACT.Copy).then_inc(s_ds, 1)

            def take_dense(s):
                wait(eng, s_proj, dense(s)[1])
                wait(eng, s_dt, s)
                eng.activation(tile_in[:, :, 0, :], ps_aux[:, 0:NB * P].rearrange("p (b w) -> p b w", b=NB), ACT.Copy).then_inc(s_cpv, 1)

            def body(s, buf):
                if at_least(s, 2):
                    copy_sum(s)
                for w in range(NW):
                    if counting(s):
                        if w == 0:
                            wait(eng, s_sum, s - 1)
                        wait(eng, s_cnt, s * NW + w + 1)
                        eng.activation(counts[buf][:, :, w * SUB:(w + 1) * SUB],
                                       ps_slot[:, COUNT_BANKS[w % 2], 0:MW].rearrange("p (t d) -> p t d", d=SUB), ACT.Copy).then_inc(s_ev, 1)
                    for g in groups_done(s, w):
                        put_stage(s + 1, g)
                    if w == 2 and at_least(s, 2):
                        take_dense(s)

            for g in range(3):
                put_stage(0, g)
            steps(body, eng)

        @block.vector
        def _(eng):
            def build_onehot(s, g):
                wait(eng, s_pe, (s - 1) * LOTS + GROUPS[g][1])
                r = chunks_of(g)
                k = key[:, bass.ds(s * CPS + r.start, len(r))]
                eng.tensor_tensor(onehot[:, r.start:r.stop, :], iota[:, 0:WIN].unsqueeze(1).to_broadcast([P, len(r), WIN]),
                                  k.unsqueeze(2).to_broadcast([P, len(r), WIN]), ALU.is_equal).then_inc(s_oh, 1)

            def values(a, most, why):
                return nc.values_load_multi_w_load_instructions(
                    a, engines=(mybir.EngineType.DVE,), min_val=0, max_val=most, skip_runtime_bounds_check_because=why)[1]

            def accumulate(s, j, off):
                c = s * LOTS + j
                wait(eng, s_pe, c + 1)
                wait(eng, s_acc, c)
                win = acc[:, :, bass.ds(off, WIN)]
                part = ps_slot[:, j % NBANK1, 0:NB * WIN].rearrange("p (q w) -> p q w", w=WIN)
                eng.tensor_tensor(win, part, win, ALU.add).then_inc(s_acc, 1)

            def build_hot(s, w, first_chunk):
                wait(eng, s_cnt, s * NW + w - 1)
                eng.tensor_scalar(lo_key[:, w % 2, :], V["klo"][:, bass.ds(first_chunk, SPAN)], kk[:, bass.ds(s * NW + w, 1)], None,
                                  ALU.subtract).then_inc(s_lo, 1)
                for j in range(SPAN):
                    eng.tensor_scalar(hot_m[:, w % 2, j, :], iota_m[:, :], V["mkey"][:, bass.ds(first_chunk + j, 1)], None, ALU.is_equal)
                wait(eng, s_lo, s * NW + w + 1)
                eng.tensor_tensor(hot_lo[:, w % 2, :, :], iota[:, :].unsqueeze(1).to_broadcast([P, SPAN, P]),
                                  lo_key[:, w % 2, :].unsqueeze(2).to_broadcast([P, SPAN, P]), ALU.is_equal).then_inc(s_hot, 1)

            def boundary(s, n):
                wait(eng, s_acc, (s + 1) * LOTS)
                wait(eng, s_proj, n)
                wait(eng, E["self_mm"], s + 1)
                eng.tensor_tensor(tile_in[:, :, 0, :], acc[:, :, 0:P],
                                  ps_aux[:, 0:NB * P].rearrange("p (b w) -> p b w", b=NB), ALU.add).then_inc(s_cpv, 1)
                wait(eng, s_cpv, n + 1)
                eng.tensor_copy(acc[:, :, 0:P], acc[:, :, P:LIM]).then_inc(s_shv, 1)
                wait(eng, s_shv, s + 1)
                eng.tensor_copy(acc[:, :, P:P + WIN], acc[:, :, LIM:AW]).then_inc(s_tlv, 1)
                wait(eng, s_tlv, s + 1)
                eng.memset(acc[:, :, P + WIN:AW], 0.0).then_inc(s_bndv, 1)

            def body(s, _):
                off = values(offr[0:1, s, 0:LOTS], LIM, "the window starts are clamped to 0..LIM when they are computed")
                finish = (F["finish_steps"](eng, *gathered(s)) if at_least(s, 1) else []) + (
                    F["finish_steps"](eng, *dense(s)) if at_least(s, 2) else [])
                for w in range(NW):
                    if w % 8 == 0 and counting(s):
                        firsts = values(V["subr"][0:1, s, w:w + 8], D.chunks, "they count chunks")
                    if counting(s):
                        build_hot(s, w, firsts[w % 8])
                    if w in FINISH_AT and FINISH_AT.index(w) < len(finish):
                        finish[FINISH_AT.index(w)]()
                    if w == LOT_AT:
                        build_onehot(s, 1)
                    for j in lots_after(s, w - 1):
                        if j == 0:
                            wait(eng, s_bndv, s)
                        accumulate(s, j, off[j])
                        if j + 1 in (GROUPS[1][0], GROUPS[2][0]):
                            g = GROUP_OF[j + 1]
                            build_onehot(s + (g + 1) // 3, (g + 1) % 3)
                boundary(s, 2 * s - 1 if at_least(s, 1) else 0)

            eng.memset(acc[:, :, :], 0.0).then_inc(s_zero, 1)
            wait(eng, s_zero, 1)
            wait(eng, s_iota, 2)
            build_onehot(0, 0)
            steps(body, eng)
            F["finish_dve"](eng, *gathered(TG))

        @block.tensor
        def _(eng):
            def self_rows(s, buf):
                if not at_least(s, 1):
                    wait(eng, V["s_early"], 16 * -(-D.early // 8))
                wait(eng, s_cpv, (2 * s - 1) if at_least(s, 2) else s)
                for b in range(NB):
                    for p in range(3):
                        last = eng.matmul(ps_aux[:, b * P:(b + 1) * P], hs_all[:, s, p * DF + b * P:p * DF + (b + 1) * P],
                                          V["identb"][:, :], start=(p == 0), stop=(p == 2))
                last.then_inc(E["self_mm"], 1)

            def sum_lot(s, j):
                g = GROUP_OF[j]
                if j == GROUPS[g][0]:
                    wait(eng, s_rows[g], (s + 1) * (16 * len(chunks_of(g))))
                    wait(eng, s_oh, s * 3 + g + 1)
                wait(eng, s_acc, s * LOTS + last_use(j) + 1)
                o = ps_slot[:, j % NBANK1, :]
                lot = range(j * LOT, (j + 1) * LOT)
                for b in range(NB):
                    for c in lot:
                        for p in range(3):
                            last = eng.matmul(o[:, b * WIN:(b + 1) * WIN], rows[:, c, p * DF + b * P:p * DF + (b + 1) * P],
                                              onehot[:, c, :], start=(c == lot[0] and p == 0), stop=(c == lot[-1] and p == 2))
                last.then_inc(s_pe, 1)

            def count(s, w):
                wait(eng, s_hot, s * NW + w + 1)
                wait(eng, s_ev, s * NW + w - 1)
                for j in range(SPAN):
                    last = eng.matmul(ps_slot[:, COUNT_BANKS[w % 2], 0:MW], hot_lo[:, w % 2, j, :], hot_m[:, w % 2, j, :],
                                      start=(j == 0), stop=(j == SPAN - 1))
                last.then_inc(s_cnt, 1)

            def multiply(s, buf, w):
                if w == 0:
                    if not at_least(s, 2):
                        wait(eng, s_all, 16 * len(ALL))
                    wait(eng, s_ev, s * NW)
                    wait(eng, s_ds, s - 1)
                o = ps_slot[:, SUM_BANK, 0:DF]
                for t in range(SHARE[w], SHARE[w + 1]):
                    for p in range(3):
                        eng.matmul(o, counts[1 - buf][:, t, :], hs_all[:, t, p * DF:(p + 1) * DF], start=(t == 0 and p == 0), stop=False)
                if w == NW - 1:
                    for p in range(3):
                        last = eng.matmul(o, V["identb"][:, :], hs_all[:, TG + s - 1, p * DF:(p + 1) * DF], start=False, stop=(p == 2))
                    last.then_inc(s_sum, 1)

            def project(n):
                for part in range(NB):
                    F["project"](eng, n, part)

            def transpose_sum(s):
                wait(eng, s_ds, s - 1)
                wait(eng, s_cpv, dense(s)[1])
                for b in range(NB):
                    last = eng.transpose(ps_aux[:, b * P:(b + 1) * P], dsum[:, b * P:(b + 1) * P], V["ident"][:, :])
                last.then_inc(s_dt, 1)

            def body(s, buf):
                for w in range(NW):
                    if counting(s):
                        count(s, w)
                    if w == 0 and at_least(s, 1):
                        project(gathered(s)[1])
                    if w == 1 and at_least(s, 2):
                        transpose_sum(s)
                    for j in lots_after(s, w):
                        sum_lot(s, j)
                    if multiplying(s):
                        multiply(s, buf, w)
                    if w == 4 and at_least(s, 2):
                        project(dense(s)[1])
                    if w == (5 if at_least(s, 1) else NW - 1):
                        self_rows(s, buf)

            eng.sem_inc(s_dt, 1)
            steps(body, eng)
            project(gathered(TG)[1])


def aggregate_any(nc, D, layer, V):
    f32, bf16, i32 = mybir.dt.float32, mybir.dt.bfloat16, mybir.dt.int32
    ALU, AX = mybir.AluOpType, mybir.AxisListType
    first = layer == 0
    R = D.rel if first else 1
    NB, DF, DF3, T, E_, CH = D.nb, D.d, 3 * D.d, D.tiles, D.e, D.chunks
    SW = DF + 4
    NROW = T * P * R
    idxT, ps_slot, ps_aux, dinv, ident = (V[k] for k in ("idxT", "ps_slot", "ps_aux", "dinv", "ident"))
    sums = nc.dram_tensor(f"sums{layer}", (NROW, SW), f32).ap()
    dst_p = nc.dram_tensor(f"dst_p{layer}", (CH * P,), i32).ap()
    typ_p = nc.dram_tensor(f"typ_p{layer}", (CH * P,), i32).ap()
    pad = CH * P - E_

    with ExitStack() as ctx:
        def sb(name, shape, dt):
            return ctx.enter_context(nc.sbuf_tensor(f"{name}_a{layer}", shape, dt))

        def sem(name):
            return ctx.enter_context(nc.semaphore(f"a{layer}_{name}"))

        F = finishing(nc, D, layer, V, ctx, "g")
        tile_in, hs, E = F["tile_in"], F["hs"], F["E"]
        padt = sb("padt", [1, 2, P], i32)
        tri = sb("tri", [P, P], f32)
        drow, trow = sb("drow", [P, P], i32), sb("trow", [P, P], i32)
        dcol, tcol = sb("dcol", [P, 1], i32), sb("tcol", [P, 1], i32)
        krow, same, dup = sb("krow", [P, P], f32), sb("same", [P, P], f32), sb("dup", [P, P], f32)
        kcol, ndup, wcol = sb("kcol", [P, 1], f32), sb("ndup", [P, 1], f32), sb("wcol", [P, 1], f32)
        idx, kidx, widx = sb("idx", [P, 1], i32), sb("kidx", [P, 1], i32), sb("widx", [P, 1], i32)
        grow = sb("grow", [P, DF3], bf16)
        vals, old = sb("vals", [P, SW], f32), sb("old", [P, SW], f32)
        big = sb("big", [P, R, SW], f32)
        selff = sb("selff", [P, DF], f32)

        s_c = sem("const")
        s_ch = sem("chain")
        s_zero, s_copy = sem("zero"), sem("copy")
        s_ld, s_idx, s_kidx, s_row, s_old = sem("ld"), sem("idx"), sem("kidx"), sem("row"), sem("old")
        s_vals, s_mm, s_new, s_put = sem("vals"), sem("mm"), sem("new"), sem("put")
        s_big, s_self, s_tp, s_free = sem("big"), sem("self"), sem("tp"), sem("free")
        SETUP, STEPS = 4, 12 if first else 10

        def chunks(body, eng):
            body(0)
            with eng.Fori(1, CH) as c:
                body(c)

        def tiles(body, eng):
            body(0)
            with eng.Fori(1, T - 1) as t:
                body(t)
            body(T - 1)

        with nc.Block() as block:
            @block.gpsimd
            def _(eng):
                eng.memset(tri[:, :], 1.0).then_inc(s_c, 1)
                wait(eng, s_c, 1)
                eng.affine_select(out=tri[:, :], in_=tri[:, :], compare_op=ALU.is_gt, fill=0.0, base=0,
                                  pattern=[[-1, P]], channel_multiplier=1).then_inc(s_c, 1)
                wait(eng, s_zero, 16 * T)
                wait(eng, s_ch, SETUP)

                def body(c):
                    wait_alone(eng, s_idx, c + 1, F["s_mark"][0])
                    eng.indirect_dma_start(grow[:, :], None, V["table"], bass.IndirectOffsetOnAxis(ap=idx[:, 0:1], axis=0)).then_inc(s_row, 16)
                    if not isinstance(c, int) or c > 0:
                        wait_alone(eng, s_put, 16 * c, F["s_mark"][0])
                    wait_alone(eng, s_kidx, c + 1, F["s_mark"][0])
                    eng.indirect_dma_start(old[:, :], None, sums, bass.IndirectOffsetOnAxis(ap=kidx[:, 0:1], axis=0),
                                           bounds_check=NROW - 1, oob_is_err=False).then_inc(s_old, 16)
                    wait_alone(eng, s_new, c + 1, F["s_mark"][0])
                    eng.indirect_dma_start(sums, bass.IndirectOffsetOnAxis(ap=widx[:, 0:1], axis=0), old[:, :], None,
                                           bounds_check=NROW - 1, oob_is_err=False).then_inc(s_put, 16)
                chunks(body, eng)
                wait(eng, s_put, 16 * CH)

            @block.sync
            def _(eng):
                wait(eng, s_ch, SETUP)
                for i, (a, b) in enumerate(((V["dst"], dst_p), (V["etype"], typ_p))):
                    eng.dma_start(b[0:E_], a).then_inc(s_copy, 16)
                    eng.dma_start(b[E_:CH * P].rearrange("(o p) -> o p", o=1), padt[:, i, 0:pad]).then_inc(s_copy, 16)
                with eng.Fori(0, T) as t:
                    eng.dma_start(sums[bass.ds(t * (P * R), P * R), :].rearrange("(p r) w -> p (r w)", r=R),
                                  big[:, :, :].rearrange("p r w -> p (r w)")).then_inc(s_zero, 16)
                wait(eng, s_zero, 16 * T)
                wait(eng, s_copy, 64)

                def body(c):
                    if not isinstance(c, int) or c > 0:
                        wait(eng, s_ld, 64 * c)
                        wait_alone(eng, s_new, c, F["s_mark"][1])
                    for a, row, col in ((dst_p, drow, dcol), (typ_p, trow, tcol)):
                        part = a[bass.ds(c * P, P)]
                        eng.dma_start(row[:, :], part.rearrange("(o p) -> o p", o=1).to_broadcast([P, P])).then_inc(s_ld, 16)
                        eng.dma_start(col[:, :], part.rearrange("(p o) -> p o", o=1)).then_inc(s_ld, 16)
                chunks(body, eng)
                wait(eng, s_ld, 64 * CH)

            @block.vector
            def _(eng):
                n = [0]

                def step(ins, at=0):
                    n[0] += 1
                    ins.then_inc(s_ch, 1)
                    wait(eng, s_ch, at + n[0])

                step(eng.memset(big[:, :, :], 0.0))
                step(eng.memset(padt[:, 0, :], int(PAD_DST)))
                step(eng.memset(padt[:, 1, :], 0))
                eng.memset(vals[:, DF + 1:SW], 0.0)
                eng.memset(vals[:, DF:DF + 1], 1.0)
                step(eng.memset(old[:, :], 0.0))
                assert n[0] == SETUP
                wait(eng, s_c, 2)

                def body(c):
                    n[0] = 0
                    at = SETUP + c * STEPS
                    wait(eng, s_row, 16 * c)
                    eng.tensor_scalar(idx[:, :], idxT[:, bass.ds(c, 1)], 1.0, None, ALU.mult).then_inc(s_idx, 1)
                    wait(eng, s_ld, 64 * (c + 1))
                    step(eng.tensor_scalar(krow[:, :], drow[:, :], float(R), None, ALU.mult), at)
                    step(eng.tensor_scalar(kcol[:, :], dcol[:, :], float(R), None, ALU.mult), at)
                    if first:
                        step(eng.tensor_tensor(krow[:, :], krow[:, :], trow[:, :], ALU.add), at)
                        step(eng.tensor_tensor(kcol[:, :], kcol[:, :], tcol[:, :], ALU.add), at)
                    wait(eng, s_put, 16 * c)
                    eng.tensor_scalar(kidx[:, :], kcol[:, :], float(HALF * R), None, ALU.add).then_inc(s_kidx, 1)
                    step(eng.tensor_scalar(same[:, :], krow[:, :], kcol[:, :], None, ALU.is_equal), at)
                    step(eng.tensor_tensor(dup[:, :], same[:, :], tri[:, :], ALU.mult), at)
                    step(eng.tensor_reduce(ndup[:, :], dup[:, :], AX.X, ALU.add), at)
                    step(eng.tensor_scalar(ndup[:, :], ndup[:, :], 1.0, 4e6, ALU.min, ALU.mult), at)
                    step(eng.scalar_tensor_tensor(wcol[:, :], kcol[:, :], float(HALF * R), ndup[:, :], ALU.add, ALU.add), at)
                    step(eng.tensor_copy(widx[:, :], wcol[:, :]), at)
                    wait(eng, s_row, 16 * (c + 1))
                    step(eng.tensor_tensor(vals[:, 0:DF], grow[:, 0:DF], grow[:, DF:2 * DF], ALU.add), at)
                    step(eng.tensor_tensor(vals[:, 0:DF], vals[:, 0:DF], grow[:, 2 * DF:DF3], ALU.add), at)
                    assert n[0] == STEPS
                    eng.sem_inc(s_vals, 1)
                    wait(eng, s_old, 16 * (c + 1))
                    wait(eng, s_mm, c + 1)
                    eng.tensor_tensor(old[:, :], ps_aux[:, 0:SW], old[:, :], ALU.add).then_inc(s_new, 1)
                chunks(body, eng)

            @block.tensor
            def _(eng):
                def body(c):
                    wait(eng, s_vals, c + 1)
                    eng.matmul(ps_aux[:, 0:SW], same[:, :], vals[:, :], start=True, stop=True).then_inc(s_mm, 1)
                chunks(body, eng)

        with nc.Block() as block:
            @block.sync
            def _(eng):
                def body(t):
                    wait_alone(eng, s_free, t + 1, F["s_mark"][1])
                    eng.dma_start(big[:, :, :].rearrange("p r w -> p (r w)"),
                                  sums[bass.ds(t * (P * R), P * R), :].rearrange("(p r) w -> p (r w)", r=R)).then_inc(s_big, 16)
                    if not first:
                        eng.dma_start(hs[:, :], V["table"][bass.ds(t * P, P), :]).then_inc(s_self, 16)
                    F["tile_io"](eng, t)
                tiles(body, eng)
                wait(eng, s_big, 16 * T)
                if not first:
                    wait(eng, s_self, 16 * T)

            @block.tensor
            def _(eng):
                def body(t):
                    wait(eng, s_new, CH + 1 + t)
                    for i in range(R * NB):
                        r, b = divmod(i, NB)
                        last = eng.transpose(ps_slot[:, i // 4, (i % 4) * P:(i % 4 + 1) * P], big[:, r, b * P:(b + 1) * P], ident[:, :])
                    last.then_inc(s_tp, 1)
                    for part in range(2):
                        F["project"](eng, t, part, act_share=False)
                tiles(body, eng)

            @block.scalar
            def _(eng):
                tiles(lambda t: F["finish_act"](eng, t), eng)

            @block.vector
            def _(eng):
                eng.sem_inc(s_free, 1)

                def body(t):
                    wait(eng, s_big, 16 * (t + 1))
                    if first:
                        eng.tensor_reduce(dinv[:, bass.ds(t, 1)], big[:, :, DF], AX.X, ALU.add).then_inc(E["deg"], 1)
                        eng.sem_inc(s_new, 1)
                    else:
                        wait(eng, s_self, 16 * (t + 1))
                        eng.tensor_tensor(selff[:, :], hs[:, 0:DF], hs[:, DF:2 * DF], ALU.add).then_inc(E["cnt"], 1)
                        wait(eng, E["cnt"], t + 1)
                        eng.tensor_tensor(selff[:, :], selff[:, :], hs[:, 2 * DF:DF3], ALU.add).then_inc(E["stat"], 1)
                        wait(eng, E["stat"], t + 1)
                        eng.tensor_tensor(big[:, 0, 0:DF], big[:, 0, 0:DF], selff[:, :], ALU.add).then_inc(s_new, 1)
                    wait(eng, s_tp, t + 1)
                    tin = tile_in[:, :, :, :].rearrange("p b r w -> p r b w")
                    per = 4 // NB
                    for q in range(-(-R // per)):
                        m = min(per, R - q * per)
                        last = eng.tensor_copy(tin[:, q * per:q * per + m, :, :],
                                               ps_slot[:, q, 0:m * NB * P].rearrange("p (r b w) -> p r b w", r=m, b=NB))
                    last.then_inc(F["s_cpv"], 1)
                    F["finish_dve"](eng, t)
                    eng.sem_inc(s_free, 1)
                tiles(body, eng)


_INS = ['x', 'src', 'dst', 'edge_type_8', 'L0_gnn_weight', 'L0_gnn_bias', 'L1_gnn_W', 'L1_gnn_b']


def kernel(**inputs):
    import numpy as _np
    import concourse.bacc as _bacc
    from concourse import mybir as _mybir
    from concourse.bass_utils import run_bass_kernel_spmd as _run

    nc = _bacc.Bacc("TRN2", target_bir_lowering=False, num_devices=1)
    arrays, args = {}, []
    for name in _INS:
        a = _np.ascontiguousarray(inputs[name])
        arrays[f"in_{name}_dram"] = a
        args.append(nc.dram_tensor(f"in_{name}_dram", a.shape, _mybir.dt.from_np(a.dtype), kind="ExternalInput").ap())
    shape = tuple(inputs['x'].shape)
    args.append(nc.dram_tensor("out_0_dram", shape, _mybir.dt.float32, kind="ExternalOutput").ap())
    program(nc, *args)
    r = _run(nc, [arrays], core_ids=[0])
    return r.results[0]["out_0_dram"]
```
